# Optimizing a Trainium2 kernel written in Bass

```python
import numpy as np
import jax
import jax.numpy as jnp

def _softmax(x, axis=-1):
    return jax.nn.softmax(x, axis=axis)

def _gelu(x):
    return jax.nn.gelu(x, approximate=True)

def _silu(x):
    return jax.nn.silu(x)

def _sigmoid(x):
    return jax.nn.sigmoid(x)

def _layernorm(x, axis=-1, eps=1e-05):
    m = jnp.mean(x, axis=axis, keepdims=True)
    v = jnp.var(x, axis=axis, keepdims=True)
    return (x - m) / jnp.sqrt(v + eps)

def _scatter_add(tgt, idx, src, axis=0):
    return tgt.at[idx].add(src)

def _segment_sum(src, seg, n):
    return jax.ops.segment_sum(src, seg, n)
kernel_name = 'mk_seq_preln_d2_jaxref_r4_b30a8e'

def setup_inputs(seed: int=0):
    np.random.seed(seed)
    _w = jnp.asarray

    def _L0_attn_setup():
        import jax, jax.numpy as jnp
        import numpy as np
        GAMMA = 0.9
        SCALE_BASE = 512.0

        def _xpos(x, downscale=False):
            B, L, D = x.shape
            half = D // 2
            scale_vec = (jnp.arange(0, D, 2, dtype=jnp.float32) + 0.4 * D) / (1.4 * D)
            power = jnp.arange(L, dtype=jnp.float32) / SCALE_BASE
            scale = scale_vec[None, :] ** power[:, None]
            if downscale:
                scale = 1.0 / scale
            inv_freq = 1.0 / 10000.0 ** (jnp.arange(half, dtype=jnp.float32) / half)
            sinusoid = jnp.arange(L, dtype=jnp.float32)[:, None] * inv_freq[None, :]
            sin = jnp.repeat(jnp.sin(sinusoid) * scale, 2, axis=-1)
            cos = jnp.repeat(jnp.cos(sinusoid) * scale, 2, axis=-1)
            x_even = x[..., 0::2]
            x_odd = x[..., 1::2]
            rot = jnp.stack((-x_odd, x_even), axis=-1).reshape(x.shape)
            return x * cos + rot * sin

        def _get_D(seq_len):
            n = jnp.arange(seq_len, dtype=jnp.float32)[:, None]
            m = jnp.arange(seq_len, dtype=jnp.float32)[None, :]
            D = GAMMA ** jnp.abs(n - m)
            return D
        key = jax.random.key(seed)
        k1, k2, k3, k4 = jax.random.split(key, 4)
        B, L, H, Dh = (8, 512, 256, 256)
        X = jax.random.normal(k1, (B, L, H), dtype=jnp.float32)
        W_Q = jax.random.normal(k2, (H, Dh), dtype=jnp.float32) / H
        W_K = jax.random.normal(k3, (H, Dh), dtype=jnp.float32) / H
        W_V = jax.random.normal(k4, (H, Dh), dtype=jnp.float32) / H
        return {'X': X, 'W_Q': W_Q, 'W_K': W_K, 'W_V': W_V}
    _L0_attn_in = _L0_attn_setup()

    def _L0_ffn_setup():
        import jax, jax.numpy as jnp
        import numpy as np
        D_MODEL, D_FF, N_EXP = (256, 1024, 8)
        key = jax.random.key(seed)
        ks = jax.random.split(key, 8)
        s = lambda fan_in: 1.0 / np.sqrt(fan_in)
        x = jax.random.normal(ks[0], (4, 512, D_MODEL), dtype=jnp.float32)
        Wr = jax.random.uniform(ks[1], (N_EXP, D_MODEL), jnp.float32, -s(D_MODEL), s(D_MODEL))
        br = jax.random.uniform(ks[2], (N_EXP,), jnp.float32, -s(D_MODEL), s(D_MODEL))
        W1 = jax.random.uniform(ks[3], (N_EXP, D_FF, D_MODEL), jnp.float32, -s(D_MODEL), s(D_MODEL))
        b1 = jax.random.uniform(ks[4], (N_EXP, D_FF), jnp.float32, -s(D_MODEL), s(D_MODEL))
        W2 = jax.random.uniform(ks[5], (N_EXP, D_MODEL, D_FF), jnp.float32, -s(D_FF), s(D_FF))
        b2 = jax.random.uniform(ks[6], (N_EXP, D_MODEL), jnp.float32, -s(D_FF), s(D_FF))
        return {'x': x, 'Wr': Wr, 'br': br, 'W1': W1, 'b1': b1, 'W2': W2, 'b2': b2}
    _L0_ffn_in = _L0_ffn_setup()

    def _L1_attn_setup():
        import jax, jax.numpy as jnp
        import numpy as np
        import math
        B, T, D, H = (2, 512, 256, 16)
        DH = D // H

        def rotate_half(x):
            x1 = x[..., ::2]
            x2 = x[..., 1::2]
            return jnp.stack((-x2, x1), axis=-1).reshape(x.shape)
        key = jax.random.key(seed)
        k1, k2, k3 = jax.random.split(key, 3)
        x = jax.random.normal(k1, (B, T, D), dtype=jnp.float32)
        Wqkv = jax.random.normal(k2, (3 * D, D), dtype=jnp.float32) * (1.0 / math.sqrt(D))
        Wo = jax.random.normal(k3, (D, D), dtype=jnp.float32) * (1.0 / math.sqrt(D))
        return {'x': x, 'Wqkv': Wqkv, 'Wo': Wo}
    _L1_attn_in = _L1_attn_setup()

    def _L1_ffn_setup():
        import jax, jax.numpy as jnp
        import numpy as np
        DIM = 256
        DEPTH = 2
        HEADS = 8
        DIM_HEAD = 64
        WINDOW = 128
        INNER = HEADS * DIM_HEAD
        HID = int(DIM * 4 * 2 / 3)
        B, N = (2, 2048)
        QK_SCALE = 8.0

        def shift_token(t):
            t1, t2 = jnp.split(t, 2, axis=-1)
            t2 = jnp.pad(t2, ((0, 0), (1, 0), (0, 0)))[:, :-1]
            return jnp.concatenate([t1, t2], axis=-1)

        def l2norm(t):
            return t / jnp.clip(jnp.linalg.norm(t, axis=-1, keepdims=True), 1e-12)

        def rotate_half(x):
            x1, x2 = jnp.split(x, 2, axis=-1)
            return jnp.concatenate([-x2, x1], axis=-1)

        def rotary_xpos(q, k):
            n = q.shape[-2]
            half_idx = jnp.arange(0, DIM_HEAD, 2, dtype=jnp.float32)
            inv_freq = 1.0 / 10000.0 ** (half_idx / DIM_HEAD)
            t = jnp.arange(n, dtype=jnp.float32)
            freqs = t[:, None] * inv_freq[None, :]
            freqs = jnp.concatenate([freqs, freqs], axis=-1)
            base = (half_idx + 0.4 * DIM_HEAD) / (1.4 * DIM_HEAD)
            power = (t - n // 2) / float(WINDOW // 2)
            scale = base[None, :] ** power[:, None]
            scale = jnp.concatenate([scale, scale], axis=-1)
            cos, sin = (jnp.cos(freqs), jnp.sin(freqs))
            q = q * cos * scale + rotate_half(q) * sin * scale
            k = k * cos / scale + rotate_half(k) * sin / scale
            return (q, k)

        def local_attention(q, k, v):
            b, h, n, d = q.shape
            w = n // WINDOW
            bq = q.reshape(b, h, w, WINDOW, d) * QK_SCALE
            bk = k.reshape(b, h, w, WINDOW, d)
            bv = v.reshape(b, h, w, WINDOW, d)

            def look_around(t):
                p = jnp.pad(t, ((0, 0), (0, 0), (1, 0), (0, 0), (0, 0)))
                return jnp.concatenate([p[:, :, :w], p[:, :, 1:]], axis=3)
            bk, bv = (look_around(bk), look_around(bv))
            bt = jnp.arange(n).reshape(w, WINDOW)
            btp = jnp.pad(bt, ((1, 0), (0, 0)), constant_values=-1)
            btk = jnp.concatenate([btp[:w], btp[1:]], axis=1)
            sim = jnp.einsum('bhwid,bhwjd->bhwij', bq, bk)
            i = bt[:, :, None]
            j = btk[:, None, :]
            mask = (i < j) | (i > j + WINDOW) | (j == -1)
            sim = jnp.where(mask, -jnp.finfo(sim.dtype).max, sim)
            attn = jax.nn.softmax(sim, axis=-1)
            out = jnp.einsum('bhwij,bhwjd->bhwid', attn, bv)
            return out.reshape(b, h, n, d)

        def _layer(x, wqkv, qs, ksc, wo, lg, lb, w1, b1, w2, b2):
            b, n, _ = x.shape
            h = shift_token(x)
            qkv = h @ wqkv
            q, k, v = jnp.split(qkv, 3, axis=-1)
            to_heads = lambda t: t.reshape(b, n, HEADS, DIM_HEAD).transpose(0, 2, 1, 3)
            q, k, v = (to_heads(q), to_heads(k), to_heads(v))
            q = l2norm(q) * qs
            k = l2norm(k) * ksc
            q, k = rotary_xpos(q, k)
            o = local_attention(q, k, v)
            o = o.transpose(0, 2, 1, 3).reshape(b, n, INNER)
            x = x + o @ wo
            h = shift_token(x)
            mu = h.mean(-1, keepdims=True)
            var = h.var(-1, keepdims=True)
            h = (h - mu) / jnp.sqrt(var + 1e-05) * lg + lb
            h = h @ w1 + b1
            a, g = jnp.split(h, 2, axis=-1)
            h = a * jax.nn.gelu(g, approximate=False)
            x = x + h @ w2 + b2
            return x
        key = jax.random.key(seed)
        ks = jax.random.split(key, 6)
        return {'x': jax.random.normal(ks[0], (B, N, DIM), jnp.float32), 'wqkv': jax.random.normal(ks[1], (DEPTH, DIM, 3 * INNER), jnp.float32) * 0.02, 'q_scale': jnp.ones((DEPTH, DIM_HEAD), jnp.float32), 'k_scale': jnp.ones((DEPTH, DIM_HEAD), jnp.float32), 'wo': jax.random.normal(ks[2], (DEPTH, INNER, DIM), jnp.float32) * 0.02, 'ln_g': jnp.ones((DEPTH, DIM), jnp.float32), 'ln_b': jnp.zeros((DEPTH, DIM), jnp.float32), 'w1': jax.random.normal(ks[3], (DEPTH, DIM, 2 * HID), jnp.float32) * 0.02, 'b1': jnp.zeros((DEPTH, 2 * HID), jnp.float32), 'w2': jax.random.normal(ks[4], (DEPTH, HID, DIM), jnp.float32) * 0.02, 'b2': jnp.zeros((DEPTH, DIM), jnp.float32)}
    _L1_ffn_in = _L1_ffn_setup()
    _d = {'L0_attn_X': _L0_attn_in['X'], 'L0_attn_W_Q': _L0_attn_in['W_Q'], 'L0_attn_W_K': _L0_attn_in['W_K'], 'L0_attn_W_V': _L0_attn_in['W_V'], 'L0_ffn_Wr': _L0_ffn_in['Wr'], 'L0_ffn_br': _L0_ffn_in['br'], 'L0_ffn_W1': _L0_ffn_in['W1'], 'L0_ffn_b1': _L0_ffn_in['b1'], 'L0_ffn_W2': _L0_ffn_in['W2'], 'L0_ffn_b2': _L0_ffn_in['b2'], 'L1_attn_Wqkv': _L1_attn_in['Wqkv'], 'L1_attn_Wo': _L1_attn_in['Wo'], 'L1_ffn_wqkv': _L1_ffn_in['wqkv'], 'L1_ffn_q_scale': _L1_ffn_in['q_scale'], 'L1_ffn_k_scale': _L1_ffn_in['k_scale'], 'L1_ffn_wo': _L1_ffn_in['wo'], 'L1_ffn_ln_g': _L1_ffn_in['ln_g'], 'L1_ffn_ln_b': _L1_ffn_in['ln_b'], 'L1_ffn_w1': _L1_ffn_in['w1'], 'L1_ffn_b1': _L1_ffn_in['b1'], 'L1_ffn_w2': _L1_ffn_in['w2'], 'L1_ffn_b2': _L1_ffn_in['b2']}
    _x0 = _d['L0_attn_X']
    _d['L0_attn_X'] = jax.random.normal(jax.random.fold_in(jax.random.key(seed), 1), (8, 512, 256), dtype=_x0.dtype)
    del _x0
    return _d

def reference(L0_attn_X, L0_attn_W_Q, L0_attn_W_K, L0_attn_W_V, L0_ffn_Wr, L0_ffn_br, L0_ffn_W1, L0_ffn_b1, L0_ffn_W2, L0_ffn_b2, L1_attn_Wqkv, L1_attn_Wo, L1_ffn_wqkv, L1_ffn_q_scale, L1_ffn_k_scale, L1_ffn_wo, L1_ffn_ln_g, L1_ffn_ln_b, L1_ffn_w1, L1_ffn_b1, L1_ffn_w2, L1_ffn_b2):

    def _L0_attn_ref(X, W_Q, W_K, W_V):
        import jax, jax.numpy as jnp
        import numpy as np
        GAMMA = 0.9
        SCALE_BASE = 512.0

        def _xpos(x, downscale=False):
            B, L, D = x.shape
            half = D // 2
            scale_vec = (jnp.arange(0, D, 2, dtype=jnp.float32) + 0.4 * D) / (1.4 * D)
            power = jnp.arange(L, dtype=jnp.float32) / SCALE_BASE
            scale = scale_vec[None, :] ** power[:, None]
            if downscale:
                scale = 1.0 / scale
            inv_freq = 1.0 / 10000.0 ** (jnp.arange(half, dtype=jnp.float32) / half)
            sinusoid = jnp.arange(L, dtype=jnp.float32)[:, None] * inv_freq[None, :]
            sin = jnp.repeat(jnp.sin(sinusoid) * scale, 2, axis=-1)
            cos = jnp.repeat(jnp.cos(sinusoid) * scale, 2, axis=-1)
            x_even = x[..., 0::2]
            x_odd = x[..., 1::2]
            rot = jnp.stack((-x_odd, x_even), axis=-1).reshape(x.shape)
            return x * cos + rot * sin

        def _get_D(seq_len):
            n = jnp.arange(seq_len, dtype=jnp.float32)[:, None]
            m = jnp.arange(seq_len, dtype=jnp.float32)[None, :]
            D = GAMMA ** jnp.abs(n - m)
            return D
        B, L, H = X.shape
        D = _get_D(L)
        Q = _xpos(X @ W_Q)
        K = _xpos(X @ W_K, downscale=True)
        V = X @ W_V
        scores = jnp.einsum('bqd,bkd->bqk', Q, K)
        p_attn = jax.nn.softmax(scores, axis=-1)
        p_attn = p_attn * D[None, :, :]
        return jnp.einsum('bqk,bkv->bqv', p_attn, V)

    def _L0_ffn_ref(x, Wr, br, W1, b1, W2, b2):
        import jax, jax.numpy as jnp
        import numpy as np
        D_MODEL, D_FF, N_EXP = (256, 1024, 8)
        B, S, D = x.shape
        xf = x.reshape(-1, D)
        logits = xf @ Wr.T + br
        expert_idx = jnp.argmax(logits, axis=-1)
        h = jax.nn.relu(jnp.einsum('td,efd->etf', xf, W1) + b1[:, None, :])
        y = jnp.einsum('etf,edf->etd', h, W2) + b2[:, None, :]
        out = y[expert_idx, jnp.arange(xf.shape[0])]
        return out.reshape(B, S, D)

    def _L1_attn_ref(x, Wqkv, Wo):
        import jax, jax.numpy as jnp
        import numpy as np
        import math
        B, T, D, H = (2, 512, 256, 16)
        DH = D // H

        def rotate_half(x):
            x1 = x[..., ::2]
            x2 = x[..., 1::2]
            return jnp.stack((-x2, x1), axis=-1).reshape(x.shape)
        b, t, d = x.shape
        pos = jnp.arange(t, dtype=jnp.float32)
        freqs = jnp.exp(-math.log(10000.0) * jnp.arange(0, DH, 2, dtype=jnp.float32) / DH)
        angles = pos[:, None] * freqs[None, :]
        angles = jnp.repeat(angles, 2, axis=-1)
        sin = jnp.sin(angles)[None, None, :, :]
        cos = jnp.cos(angles)[None, None, :, :]
        qkv = x @ Wqkv.T
        q, k, v = jnp.split(qkv, 3, axis=-1)
        q = q.reshape(b, t, H, DH).transpose(0, 2, 1, 3)
        k = k.reshape(b, t, H, DH).transpose(0, 2, 1, 3)
        v = v.reshape(b, t, H, DH).transpose(0, 2, 1, 3)
        q = cos * q + rotate_half(q) * sin
        k = cos * k + rotate_half(k) * sin
        scores = jnp.einsum('bhqd,bhkd->bhqk', q, k) / math.sqrt(DH)
        causal = jnp.tril(jnp.ones((t, t), dtype=bool))
        scores = jnp.where(causal, scores, -jnp.inf)
        attn = jax.nn.softmax(scores, axis=-1)
        out = jnp.einsum('bhqk,bhkd->bhqd', attn, v)
        out = out.transpose(0, 2, 1, 3).reshape(b, t, d)
        return out @ Wo.T

    def _L1_ffn_ref(x, wqkv, q_scale, k_scale, wo, ln_g, ln_b, w1, b1, w2, b2):
        import jax, jax.numpy as jnp
        import numpy as np
        DIM = 256
        DEPTH = 2
        HEADS = 8
        DIM_HEAD = 64
        WINDOW = 128
        INNER = HEADS * DIM_HEAD
        HID = int(DIM * 4 * 2 / 3)
        B, N = (2, 2048)
        QK_SCALE = 8.0

        def shift_token(t):
            t1, t2 = jnp.split(t, 2, axis=-1)
            t2 = jnp.pad(t2, ((0, 0), (1, 0), (0, 0)))[:, :-1]
            return jnp.concatenate([t1, t2], axis=-1)

        def l2norm(t):
            return t / jnp.clip(jnp.linalg.norm(t, axis=-1, keepdims=True), 1e-12)

        def rotate_half(x):
            x1, x2 = jnp.split(x, 2, axis=-1)
            return jnp.concatenate([-x2, x1], axis=-1)

        def rotary_xpos(q, k):
            n = q.shape[-2]
            half_idx = jnp.arange(0, DIM_HEAD, 2, dtype=jnp.float32)
            inv_freq = 1.0 / 10000.0 ** (half_idx / DIM_HEAD)
            t = jnp.arange(n, dtype=jnp.float32)
            freqs = t[:, None] * inv_freq[None, :]
            freqs = jnp.concatenate([freqs, freqs], axis=-1)
            base = (half_idx + 0.4 * DIM_HEAD) / (1.4 * DIM_HEAD)
            power = (t - n // 2) / float(WINDOW // 2)
            scale = base[None, :] ** power[:, None]
            scale = jnp.concatenate([scale, scale], axis=-1)
            cos, sin = (jnp.cos(freqs), jnp.sin(freqs))
            q = q * cos * scale + rotate_half(q) * sin * scale
            k = k * cos / scale + rotate_half(k) * sin / scale
            return (q, k)

        def local_attention(q, k, v):
            b, h, n, d = q.shape
            w = n // WINDOW
            bq = q.reshape(b, h, w, WINDOW, d) * QK_SCALE
            bk = k.reshape(b, h, w, WINDOW, d)
            bv = v.reshape(b, h, w, WINDOW, d)

            def look_around(t):
                p = jnp.pad(t, ((0, 0), (0, 0), (1, 0), (0, 0), (0, 0)))
                return jnp.concatenate([p[:, :, :w], p[:, :, 1:]], axis=3)
            bk, bv = (look_around(bk), look_around(bv))
            bt = jnp.arange(n).reshape(w, WINDOW)
            btp = jnp.pad(bt, ((1, 0), (0, 0)), constant_values=-1)
            btk = jnp.concatenate([btp[:w], btp[1:]], axis=1)
            sim = jnp.einsum('bhwid,bhwjd->bhwij', bq, bk)
            i = bt[:, :, None]
            j = btk[:, None, :]
            mask = (i < j) | (i > j + WINDOW) | (j == -1)
            sim = jnp.where(mask, -jnp.finfo(sim.dtype).max, sim)
            attn = jax.nn.softmax(sim, axis=-1)
            out = jnp.einsum('bhwij,bhwjd->bhwid', attn, bv)
            return out.reshape(b, h, n, d)

        def _layer(x, wqkv, qs, ksc, wo, lg, lb, w1, b1, w2, b2):
            b, n, _ = x.shape
            h = shift_token(x)
            qkv = h @ wqkv
            q, k, v = jnp.split(qkv, 3, axis=-1)
            to_heads = lambda t: t.reshape(b, n, HEADS, DIM_HEAD).transpose(0, 2, 1, 3)
            q, k, v = (to_heads(q), to_heads(k), to_heads(v))
            q = l2norm(q) * qs
            k = l2norm(k) * ksc
            q, k = rotary_xpos(q, k)
            o = local_attention(q, k, v)
            o = o.transpose(0, 2, 1, 3).reshape(b, n, INNER)
            x = x + o @ wo
            h = shift_token(x)
            mu = h.mean(-1, keepdims=True)
            var = h.var(-1, keepdims=True)
            h = (h - mu) / jnp.sqrt(var + 1e-05) * lg + lb
            h = h @ w1 + b1
            a, g = jnp.split(h, 2, axis=-1)
            h = a * jax.nn.gelu(g, approximate=False)
            x = x + h @ w2 + b2
            return x
        for l in range(DEPTH):
            x = _layer(x, wqkv[l], q_scale[l], k_scale[l], wo[l], ln_g[l], ln_b[l], w1[l], b1[l], w2[l], b2[l])
        return x
    x = L0_attn_X
    x = x + _L0_attn_ref(_layernorm(x, axis=-1), L0_attn_W_Q, L0_attn_W_K, L0_attn_W_V)
    x = x + _L0_ffn_ref(_layernorm(x, axis=-1), L0_ffn_Wr, L0_ffn_br, L0_ffn_W1, L0_ffn_b1, L0_ffn_W2, L0_ffn_b2)
    x = x + _L1_attn_ref(_layernorm(x, axis=-1), L1_attn_Wqkv, L1_attn_Wo)
    x = x + _L1_ffn_ref(_layernorm(x, axis=-1), L1_ffn_wqkv, L1_ffn_q_scale, L1_ffn_k_scale, L1_ffn_wo, L1_ffn_ln_g, L1_ffn_ln_b, L1_ffn_w1, L1_ffn_b1, L1_ffn_w2, L1_ffn_b2)
    return x

_drawn_inputs = setup_inputs


def setup_inputs(seed=0):
    import zlib

    import numpy as np

    out = dict(_drawn_inputs(seed))
    spreads = {'L1_ffn_q_scale': (1.0, 0.6),
     'L1_ffn_k_scale': (1.0, 0.6),
     'L1_ffn_ln_g': (1.0, 0.6),
     'L1_ffn_ln_b': (0.0, 0.8),
     'L1_ffn_b1': (0.0, 0.8),
     'L1_ffn_b2': (0.0, 0.1)}
    factors = {'L0_attn_W_Q': 8.0,
     'L0_attn_W_K': 8.0,
     'L0_attn_W_V': 7.71,
     'L0_ffn_b1': 3.841,
     'L0_ffn_b2': 2.945}
    for name, (base, spread) in spreads.items():
        noise = np.random.default_rng([zlib.crc32(name.encode()), seed]).standard_normal(out[name].shape)
        drawn = base * np.exp(spread * noise) if base else spread * noise
        out[name] = jnp.asarray(drawn.astype(out[name].dtype))
    for name, factor in factors.items():
        out[name] = (out[name] * factor).astype(out[name].dtype)
    return out
```

```python
from contextlib import ExitStack

import numpy as np
import concourse.bass as bass
from concourse import mybir

F32 = mybir.dt.float32
F32R = mybir.dt.float32r
BF16 = mybir.dt.bfloat16
I32 = mybir.dt.int32
U32 = mybir.dt.uint32
ALU = mybir.AluOpType
ACT = mybir.ActivationFunctionType
AX = mybir.AxisListType.X

P = 128
B, L, D = 8, 512, 256
NT = L // P
DC = D // P
NS = 2
PAIRS = B // NS
TOK = B * L
TILES = TOK // P
EXPERTS, FF = 8, 1024
FC = FF // P
SLOTS = TILES + EXPERTS - 1
MAXSLOT = SLOTS + 1
EPS = 1e-5
LOOP_SEMS = 150


class Chain:

    def __init__(self, eng, sem):
        self.eng, self.sem, self.n = eng, sem, 0

    def mark(self, ins):
        self.n += 1
        ins.then_inc(self.sem, 1)
        return self.n

    def step(self, ins):
        self.eng.wait_ge(self.sem, self.mark(ins))

    def wait(self, n):
        self.eng.wait_ge(self.sem, n)


def layer_norm(dve, chain, var_ready, rstd_ready, k, parts, stats, mv, ve, rstd, out):
    for t in range(NT):
        for i, src in enumerate(parts(t)):
            last = chain.mark(dve.bn_stats(stats[:, t, 6 * i:6 * i + 6], src))
    chain.wait(last)
    n = len(parts(0))
    for t in range(NT):
        last = chain.mark(dve.bn_aggr(mv[:, t, :], stats[:, t, 0:6 * n]))
    chain.wait(last)
    dve.tensor_scalar(ve[:, :], mv[:, :, 1], EPS, None, ALU.add).then_inc(var_ready, 1)
    dve.wait_ge(rstd_ready, k)
    for t in range(NT):
        for src, dst in zip(parts(t), out(t)):
            last = dve.tensor_scalar(dst, src, mv[:, t, 0:1], rstd[:, t:t + 1], ALU.subtract, ALU.mult)
            yield t, last


def phase_attn0(nc, g):
    with ExitStack() as ctx:
        def sb(name, shape, dt=F32):
            return ctx.enter_context(nc.sbuf_tensor(f"a_{name}", shape, dt))

        def stream(name, shape, dt=F32):
            return [sb(f"{name}{s}", shape, dt) for s in range(NS)]

        sems = []

        def sem(name):
            sems.append(ctx.enter_context(nc.semaphore(f"a_{name}", num=LOOP_SEMS + len(sems))))
            return sems[-1]

        def sem2(name):
            return [sem(f"{name}{s}") for s in range(NS)]

        wq = sb("wq", [P, DC, D])
        wk = sb("wk", [P, DC, D])
        wv = sb("wv", [P, DC, D])
        wr = sb("wr", [P, DC, EXPERTS])
        br = sb("br", [P, EXPERTS])
        xpos = sb("xpos", [P, 4, L])
        decay = sb("decay", [P, 7 * P])
        x, xn = stream("x", [P, NT, D]), stream("xn", [P, NT, D])
        xnT = stream("xnT", [P, DC, L])
        qT, kT = stream("qT", [P, DC, L]), stream("kT", [P, DC, L])
        v = stream("v", [P, NT, D])
        prods = stream("prods", [P, 4, L])
        probs = stream("probs", [P, L])
        probsT = stream("probsT", [P, NT, P])
        stats, mv = stream("stats", [P, NT, 6]), stream("mv", [P, NT, 2])
        ve, rstd = stream("ve", [P, NT]), stream("rstd", [P, NT])
        nmax, rsum, rinv = stream("nmax", [P, NT]), stream("rsum", [P, NT]), stream("rinv", [P, NT])
        bank = [[ctx.enter_context(nc.psum_tensor(f"bank{s}{i}", [P, L], F32)) for i in range(4)]
                for s in range(NS)]

        consts_in = g.once("consts_in")
        x_in = sem2("x_in")
        dve_chain, var_ready, rstd_ready = sem("dve_chain"), sem2("var_ready"), sem2("rstd_ready")
        xn_ready, xnT_psum, xnT_ready = sem2("xn_ready"), sem2("xnT_psum"), sem2("xnT_ready")
        qk_psum, qk_mults, qk_ready = sem2("qk_psum"), sem2("qk_mults"), sem2("qk_ready")
        v_psum, v_ready = sem2("v_psum"), sem2("v_ready")
        scores_ready, nmax_ready, probs_ready = sem2("scores_ready"), sem2("nmax_ready"), sem2("probs_ready")
        probsT_psum, probsT_ready = sem2("probsT_psum"), sem2("probsT_ready")
        o_psum, x1_ready = sem2("o_psum"), sem2("x1_ready")
        logits_psum, logits_read, kept, stored = sem2("logits_psum"), sem2("logits_read"), sem2("kept"), sem2("stored")
        sem_range = range(sems[0].num, sems[-1].num + 1)
        assert len(sem_range) == len(sems)

        CONSTS = [(wq, g.W_Q.rearrange("(c p) n -> p c n", p=P)), (wk, g.W_K.rearrange("(c p) n -> p c n", p=P)),
                  (wv, g.W_V.rearrange("(c p) n -> p c n", p=P)), (wr, g.WrT.rearrange("(c p) n -> p c n", p=P)),
                  (br, g.br.partition_broadcast(P)), (xpos, g.xpos0), (decay, g.decay)]

        with nc.Block() as block:
            @block.sync
            def _(sp):
                for dst, src in CONSTS:
                    sp.dma_start(dst[:], src).then_inc(consts_in, 16)
                sp.dma_start(g.ident[:], g.ident_d).then_inc(consts_in, 16)
                sp.wait_ge(consts_in, 16 * (len(CONSTS) + 1))

            @block.gpsimd
            def _(pool):
                pool.memset(g.minus_half[:], -0.5).then_inc(g.pool_consts, 1)
                pool.memset(g.zrow[:], 0.0).then_inc(g.pool_consts, 1)
                pool.wait_ge(g.pool_consts, 2)
                for i in range(MAXSLOT // 8):
                    pool.dma_start(g.xs_d[i * 8 * P:(i + 1) * 8 * P, :].rearrange("(p a) n -> p (a n)", p=P),
                                   g.zrow[:]).then_inc(g.zeros_out, 16)

        with nc.Fori(0, PAIRS) as pair:
            with nc.Block() as block:
                @block.sync
                def _(sp):
                    for s in range(NS):
                        sp.dma_start(x[s][:], g.X[pair * NS + s].rearrange("(t p) n -> p t n", p=P)).then_inc(x_in[s], 16)
                    sp.wait_ge(qk_psum[0], 1)
                    for i in range(NS):
                        sp.dma_start(g.w1[:, bass.ds(pair * NS + i, 1)],
                                     g.W1T[bass.ds(pair * NS + i, 1)].rearrange("e (c p) f -> p e c f", p=P)).then_inc(g.w1_in, 16)
                    for s in range(NS):
                        sp.wait_ge(x1_ready[s], NT)
                        sp.dma_start(g.x1_d[pair * NS + s].rearrange("(t p) n -> p t n", p=P), x[s][:]).then_inc(stored[s], 16)
                    for s in range(NS):
                        sp.wait_ge(stored[s], 16)

                @block.vector
                def _(dve):
                    chain = Chain(dve, dve_chain)

                    def norm(s, k):
                        for t, ins in layer_norm(dve, chain, var_ready[s], rstd_ready[s], k,
                                                 lambda t: [x[s][:, t, :]], stats[s], mv[s], ve[s], rstd[s],
                                                 lambda t: [xn[s][:, t, :]]):
                            ins.then_inc(xn_ready[s], 1)

                    def rotate(s):
                        for i in range(2):
                            dve.wait_ge(qk_psum[s], i + 1)
                            even, odd = bank[s][2 * i], bank[s][2 * i + 1]
                            cos, sin = xpos[:, 2 * i, :], xpos[:, 2 * i + 1, :]
                            if i == 1:
                                dve.wait_ge(qk_ready[s], 2)
                            for j, (a, b) in enumerate([(even, cos), (odd, sin), (odd, cos), (even, sin)]):
                                dve.tensor_tensor(prods[s][:, j, :], a[:], b, ALU.mult).then_inc(qk_mults[s], 1)

                    def row_max(s, qt):
                        dve.wait_ge(scores_ready[s], qt + 1)
                        dve.tensor_reduce(nmax[s][:, qt:qt + 1], bank[s][qt % 2][:], AX, ALU.max, negate=True)\
                           .then_inc(nmax_ready[s], 1)

                    def decayed(s, qt):
                        dve.wait_ge(probsT_psum[s], qt + 1)
                        if qt:
                            dve.wait_ge(o_psum[s], qt)
                        dve.tensor_tensor(probsT[s][:].rearrange("p a b -> p (a b)"), bank[s][2][:],
                                          decay[:, qt * P:qt * P + L], ALU.mult).then_inc(probsT_ready[s], 1)

                    def residual(s, qt):
                        chain.step(dve.reciprocal(rinv[s][:, qt:qt + 1], rsum[s][:, qt:qt + 1]))
                        dve.wait_ge(o_psum[s], qt + 1)
                        dve.scalar_tensor_tensor(x[s][:, qt, :], bank[s][3][:, 0:D], rinv[s][:, qt:qt + 1],
                                                 x[s][:, qt, :], ALU.mult, ALU.add).then_inc(x1_ready[s], 1)

                    for s in range(NS):
                        dve.wait_ge(x_in[s], 16)
                        norm(s, 1)
                    for s in range(NS):
                        rotate(s)
                    for qt in range(NT + 1):
                        for s in range(NS):
                            if qt < NT:
                                row_max(s, qt)
                            if qt:
                                decayed(s, qt - 1)
                        for s in range(NS):
                            if qt:
                                residual(s, qt - 1)
                    for s in range(NS):
                        dve.wait_ge(x1_ready[s], NT)
                        norm(s, 2)
                    for s in range(NS):
                        dve.wait_ge(logits_psum[s], 1)
                        dve.tensor_tensor(g.logits[:, bass.ds(pair * (NS * NT) + s * NT, NT), :],
                                          bank[s][2][:, 0:NT * EXPERTS].rearrange("p (t e) -> p t e", e=EXPERTS),
                                          br[:].unsqueeze(1).to_broadcast([P, NT, EXPERTS]), ALU.add).then_inc(logits_read[s], 1)

                @block.gpsimd
                def _(pool):
                    def power(s, k):
                        pool.wait_ge(var_ready[s], k)
                        pool.tensor_tensor(rstd[s][:], ve[s][:], g.minus_half[:, 0:NT], ALU.pow).then_inc(rstd_ready[s], 1)

                    for s in range(NS):
                        power(s, 1)
                    for s in range(NS):
                        for i, dst in enumerate([qT, kT]):
                            for j, op in enumerate([ALU.subtract, ALU.add]):
                                pool.wait_ge(qk_mults[s], 4 * i + 2 * j + 2)
                                pool.tensor_tensor(dst[s][:, j, :], prods[s][:, 2 * j, :], prods[s][:, 2 * j + 1, :], op)\
                                    .then_inc(qk_ready[s], 1)
                    for s in range(NS):
                        power(s, 2)
                    for s in range(NS):
                        pool.wait_ge(xn_ready[s], 2 * NT)
                        pool.tensor_copy(g.xn2[:, bass.ds(pair * (NS * NT) + s * NT, NT), :], xn[s][:]).then_inc(kept[s], 1)

                @block.scalar
                def _(act):
                    def xnT_out(s, k):
                        for c in range(DC):
                            act.wait_ge(xnT_psum[s], 2 * k + c + 1)
                            act.activation(xnT[s][:, c, :], bank[s][c][:], ACT.Copy).then_inc(xnT_ready[s], 1)

                    for s in range(NS):
                        xnT_out(s, 0)
                    for s in range(NS):
                        for h in range(2):
                            act.wait_ge(v_psum[s], h + 1)
                            act.activation(v[s][:, 2 * h:2 * h + 2, :].rearrange("p a b -> p (a b)"), bank[s][h][:], ACT.Copy)\
                               .then_inc(v_ready[s], 1)
                    for qt in range(NT):
                        for s in range(NS):
                            act.wait_ge(nmax_ready[s], qt + 1)
                            if qt:
                                act.wait_ge(probsT_psum[s], qt)
                            act.activation(probs[s][:], bank[s][qt % 2][:], ACT.Exp, bias=nmax[s][:, qt:qt + 1],
                                           accum_out=rsum[s][:, qt:qt + 1]).then_inc(probs_ready[s], 1)
                    for s in range(NS):
                        xnT_out(s, 1)

                @block.tensor
                def _(pe):
                    def transposes(s, k):
                        for c in range(DC):
                            for t in range(NT):
                                if c == 0:
                                    pe.wait_ge(xn_ready[s], k * NT + t + 1)
                                last = pe.transpose(bank[s][c][:, t * P:(t + 1) * P], xn[s][:, t, c * P:(c + 1) * P], g.ident[:])
                            last.then_inc(xnT_psum[s], 1)

                    def project(s):
                        pe.wait_ge(xnT_ready[s], DC)
                        for i, w in enumerate([wq, wk]):
                            wp = w[:].rearrange("p c (n two) -> p c two n", two=2)
                            for j in range(2):
                                for c in range(DC):
                                    last = pe.matmul(bank[s][2 * i + j][:], wp[:, c, j, :], xnT[s][:, c, :],
                                                     start=c == 0, stop=c == DC - 1)
                            last.then_inc(qk_psum[s], 1)

                    def values(s):
                        pe.wait_ge(qk_mults[s], 4)
                        for t in range(NT):
                            for c in range(DC):
                                last = pe.matmul(bank[s][t // 2][:, (t % 2) * D:(t % 2 + 1) * D], xnT[s][:, c, t * P:(t + 1) * P],
                                                 wv[:, c, :], start=c == 0, stop=c == DC - 1)
                            if t % 2:
                                last.then_inc(v_psum[s], 1)

                    def scores(s, qt):
                        if qt == 0:
                            pe.wait_ge(qk_ready[s], 4)
                            pe.wait_ge(v_ready[s], 2)
                        if qt >= 2:
                            pe.wait_ge(probs_ready[s], qt - 1)
                        for c in range(DC):
                            last = pe.matmul(bank[s][qt % 2][:], qT[s][:, c, qt * P:(qt + 1) * P], kT[s][:, c, :],
                                             start=c == 0, stop=c == DC - 1)
                        last.then_inc(scores_ready[s], 1)

                    def flip(s, qt):
                        pe.wait_ge(probs_ready[s], qt + 1)
                        if qt:
                            pe.wait_ge(probsT_ready[s], qt)
                        for kt in range(NT):
                            last = pe.transpose(bank[s][2][:, (NT - 1 - kt) * P:(NT - kt) * P],
                                                probs[s][:, kt * P:(kt + 1) * P], g.ident[:])
                        last.then_inc(probsT_psum[s], 1)

                    def output(s, qt):
                        pe.wait_ge(probsT_ready[s], qt + 1)
                        if qt:
                            pe.wait_ge(x1_ready[s], qt)
                        for kt in range(NT):
                            last = pe.matmul(bank[s][3][:, 0:D], probsT[s][:, NT - 1 - kt, :], v[s][:, kt, :],
                                             start=kt == 0, stop=kt == NT - 1)
                        last.then_inc(o_psum[s], 1)

                    for s in range(NS):
                        transposes(s, 0)
                    for s in range(NS):
                        project(s)
                    for s in range(NS):
                        values(s)
                    for qt in range(NT + 1):
                        for s in range(NS):
                            if qt < NT:
                                scores(s, qt)
                            if qt:
                                flip(s, qt - 1)
                        for s in range(NS):
                            if qt:
                                output(s, qt - 1)
                    for s in range(NS):
                        transposes(s, 1)
                    for s in range(NS):
                        pe.wait_ge(xnT_ready[s], 2 * DC)
                        for t in range(NT):
                            for c in range(DC):
                                last = pe.matmul(bank[s][2][:, t * EXPERTS:(t + 1) * EXPERTS], xnT[s][:, c, t * P:(t + 1) * P],
                                                 wr[:, c, :], start=c == 0, stop=c == DC - 1)
                        last.then_inc(logits_psum[s], 1)
            nc.all_engine_barrier(sems_to_clear=sem_range)


class Shared:

    def __init__(self, nc, ctx):
        self.nc, self.ctx = nc, ctx

    def take(self, v):
        self.X, self.W_Q, self.W_K, self.W_V, self.WrT, self.br = v["X"], v["W_Q"], v["W_K"], v["W_V"], v["WrT"], v["br"]
        self.W1T, self.W2T, self.b1T, self.b2d = v["W1T"], v["W2T"], v["b1T"], v["b2d"]
        self.Wqkv1T, self.Wo1T = v["Wqkv1T"], v["Wo1T"]
        self.wqkv, self.wo, self.w1d, self.w2d = v["wqkv"], v["wo"], v["w1d"], v["w2d"]
        self.b1l, self.b2l, self.qs, self.ks, self.lng, self.lnb = v["b1l"], v["b2l"], v["qs"], v["ks"], v["lng"], v["lnb"]
        self.xpos0, self.decay, self.ranks, self.iota = v["xpos0"], v["decay"], v["ranks"], v["iota"]
        self.rope1, self.rope2 = v["rope1"], v["rope2"]
        self.ident_d, self.shift_d, self.mask_d = v["ident_d"], v["shift_d"], v["mask_d"]

    def once(self, name):
        return self.ctx.enter_context(self.nc.semaphore(name))

    def keep(self, name, shape, dt=F32):
        return self.ctx.enter_context(self.nc.sbuf_tensor(name, shape, dt))


SLOT_LOOPS = 3
PER_LOOP = SLOTS // SLOT_LOOPS
assert PER_LOOP * SLOT_LOOPS == SLOTS


def phase_route(nc, g):
    TE = TILES * EXPERTS
    with ExitStack() as ctx:
        def sb(name, shape, dt=F32):
            return ctx.enter_context(nc.sbuf_tensor(f"m_{name}", shape, dt))

        ranks, iota = sb("ranks", [P, 2 * P]), sb("iota", [P, P])
        best, score = sb("best", [P, TILES]), sb("score", [P, TILES, EXPERTS])
        onehot = sb("onehot", [P, TILES, EXPERTS])
        order = sb("order", [P, EXPERTS])
        totals, upto = sb("totals", [P, EXPERTS, TILES]), sb("upto", [P, EXPERTS, TILES])
        ones, starts = sb("ones", [P, TILES]), sb("starts", [P, TILES])
        passed = sb("passed", [P, EXPERTS, TILES])
        slots_of, ends, base = sb("slots_of", [P, EXPERTS]), sb("ends", [P, EXPERTS]), sb("base", [P, EXPERTS])
        over, owner = sb("over", [P, MAXSLOT, EXPERTS]), sb("owner", [P, MAXSLOT])
        rows, row = sb("rows", [P, TILES, EXPERTS]), sb("row", [P, TILES])
        rank_psum = ctx.enter_context(nc.psum_tensor("rank_psum", [P, TE], F32))
        total_psum = ctx.enter_context(nc.psum_tensor("total_psum", [P, TE], F32))
        tables_in, dve_chain = g.once("tables_in"), g.once("rt_chain")
        onehot_ready, counted = g.once("onehot_ready"), g.once("counted")
        rows_ready, scattered = g.once("rows_ready"), g.once("scattered")

        with nc.Block() as block:
            @block.sync
            def _(sp):
                sp.dma_start(ranks[:], g.ranks).then_inc(tables_in, 16)
                sp.dma_start(iota[:], g.iota).then_inc(tables_in, 16)
                for e in range(EXPERTS):
                    sp.dma_start(g.w2[:, e], g.W2T[e].rearrange("(c p) n -> p c n", p=P)).then_inc(g.w2_in, 16)
                sp.dma_start(g.b1[:], g.b1T).then_inc(g.w2_in, 16)
                sp.dma_start(g.b2[:], g.b2d.partition_broadcast(P)).then_inc(g.w2_in, 16)

            @block.tensor
            def _(pe):
                pe.wait_ge(tables_in, 32)
                pe.wait_ge(onehot_ready, 1)
                oh = onehot[:].rearrange("p t e -> p (t e)")
                pe.matmul(rank_psum[:], ranks[:, 0:P], oh, start=True, stop=True)
                pe.matmul(total_psum[:], ranks[:, P:2 * P], oh, start=True, stop=True).then_inc(counted, 1)

            @block.vector
            def _(dve):
                chain = Chain(dve, dve_chain)
                step = chain.step

                def over_experts(a):
                    return a.unsqueeze(2).to_broadcast([P, a.shape[1], EXPERTS])

                dve.wait_ge(tables_in, 32)
                step(dve.memset(ones[:], 1.0))
                step(dve.tensor_reduce(best[:], g.logits[:], AX, ALU.max))
                step(dve.tensor_tensor(onehot[:], g.logits[:], over_experts(best[:]), ALU.is_equal))
                step(dve.tensor_scalar(order[:], iota[:, 0:EXPERTS], -1.0, float(EXPERTS), ALU.mult, ALU.add))
                step(dve.tensor_tensor(score[:], onehot[:], order[:].unsqueeze(1).to_broadcast([P, TILES, EXPERTS]), ALU.mult))
                step(dve.tensor_reduce(best[:], score[:], AX, ALU.max))
                dve.tensor_tensor(onehot[:], score[:], over_experts(best[:]), ALU.is_equal).then_inc(onehot_ready, 1)
                dve.wait_ge(counted, 1)
                step(dve.tensor_copy(totals[:], total_psum[:].rearrange("p (t e) -> p e t", e=EXPERTS)))
                for e in range(EXPERTS):
                    last = chain.mark(dve.tensor_tensor_scan(upto[:, e, :], ones[:], totals[:, e, :], 0.0, ALU.mult, ALU.add))
                chain.wait(last)
                step(dve.tensor_scalar(starts[:], iota[:, 0:TILES], float(P), None, ALU.mult))
                step(dve.tensor_tensor(passed[:], upto[:, :, TILES - 1:TILES].to_broadcast([P, EXPERTS, TILES]),
                                       starts[:].unsqueeze(1).to_broadcast([P, EXPERTS, TILES]), ALU.is_gt))
                step(dve.tensor_reduce(slots_of[:], passed[:], AX, ALU.add))
                step(dve.tensor_tensor_scan(ends[:], ones[:, 0:EXPERTS], slots_of[:], 0.0, ALU.mult, ALU.add))
                step(dve.tensor_tensor(base[:], ends[:], slots_of[:], ALU.subtract))
                step(dve.tensor_scalar(base[:], base[:], float(P), None, ALU.mult))
                step(dve.tensor_tensor(over[:], ends[:].unsqueeze(1).to_broadcast([P, MAXSLOT, EXPERTS]),
                                       iota[:, 0:MAXSLOT].unsqueeze(2).to_broadcast([P, MAXSLOT, EXPERTS]), ALU.is_le))
                step(dve.tensor_reduce(owner[:], over[:], AX, ALU.add))
                step(dve.tensor_scalar(g.owner[:], owner[:], float(EXPERTS - 1), None, ALU.min))
                step(dve.tensor_tensor(passed[:], upto[:], totals[:], ALU.subtract))
                step(dve.tensor_tensor(rows[:], rank_psum[:].rearrange("p (t e) -> p t e", e=EXPERTS),
                                       passed[:].rearrange("p e t -> p t e"), ALU.add))
                step(dve.tensor_tensor(rows[:], rows[:], base[:].unsqueeze(1).to_broadcast([P, TILES, EXPERTS]), ALU.add))
                step(dve.tensor_tensor(rows[:], rows[:], onehot[:], ALU.mult))
                step(dve.tensor_reduce(row[:], rows[:], AX, ALU.add))
                dve.tensor_copy(g.row_of[:], row[:]).then_inc(rows_ready, 1)

            @block.gpsimd
            def _(pool):
                pool.wait_ge(rows_ready, 1)
                pool.wait_ge(g.zeros_out, 16 * (MAXSLOT // 8))
                for t in range(TILES):
                    pool.indirect_dma_start(g.xs_d, bass.IndirectOffsetOnAxis(ap=g.row_of[:, t:t + 1], axis=0),
                                            g.xn2[:, t, :], None).then_inc(scattered, 16)
                pool.wait_ge(scattered, 16 * TILES)


def phase_experts(nc, g):
    with ExitStack() as ctx:
        def sb(name, shape, dt=F32):
            return ctx.enter_context(nc.sbuf_tensor(f"m_{name}", shape, dt))

        sems = []

        def sem(name):
            sems.append(ctx.enter_context(nc.semaphore(f"m_{name}", num=LOOP_SEMS + len(sems))))
            return sems[-1]

        XB = 3
        xs = sb("xs", [P, XB, D])
        xsT = sb("xsT", [P, 2, DC, P])
        hT = sb("hT", [P, 2, FC, P])
        y = sb("y", [P, 2, D])
        b1s = sb("b1s", [P, 2, FC])
        W = DC * FF
        staged = g.xn2[:].rearrange("p t n -> p (t n)").rearrange("p (k w n) -> p k w n", k=2, w=2)
        w1s = [staged[:, k, 0].rearrange("p (c f) -> p c f", c=DC) for k in range(2)]
        w2s = [staged[:, k, 1].rearrange("p (c n) -> p c n", c=FC) for k in range(2)]
        xT_bank = [ctx.enter_context(nc.psum_tensor(f"xT_bank{i}", [P, 512], F32)) for i in range(2)]
        h_bank = [ctx.enter_context(nc.psum_tensor(f"h_bank{i}", [P, 4, P], F32)) for i in range(4)]
        y_bank = [ctx.enter_context(nc.psum_tensor(f"y_bank{i}", [P, 512], F32)) for i in range(2)]

        x_in = [sem(f"xs_in{i}") for i in range(XB)]
        xT_psum, xT_ready, w1_staged, w2_staged = sem("xT_psum"), sem("xT_ready"), sem("w1_staged"), sem("w2_staged")
        h_psum, h_ready, y_psum, y_ready = sem("h_psum"), sem("h_ready"), sem("y_psum"), sem("y_ready")
        y_out = [sem(f"y_out{i}") for i in range(2)]
        sem_range = range(sems[0].num, sems[-1].num + 1)
        N = PER_LOOP

        with nc.Fori(0, SLOT_LOOPS) as loop:
            with nc.Block() as block:
                @block.sync
                def _(sp):
                    def store(j):
                        sp.wait_ge(y_ready, j + 1)
                        sp.dma_start(g.ys_d[bass.ds((loop * N + j) * P, P), :], y[:, j % 2, :]).then_inc(y_out[j % 2], 16)

                    for j in range(N):
                        if j >= XB:
                            sp.wait_ge(xT_psum, j - XB + 1)
                        sp.dma_start(xs[:, j % XB, :], g.xs_d[bass.ds((loop * N + j) * P, P), :]).then_inc(x_in[j % XB], 16)
                        if j >= XB:
                            store(j - XB)
                    for j in range(N - XB, N):
                        store(j)
                    for k in range(2):
                        sp.wait_ge(y_out[k], 16 * ((N - k + 1) // 2))

                @block.vector
                def _(dve):
                    owner = [None, None]

                    def stage(j):
                        k = j % 2
                        owner[k] = dve.value_load(g.owner[0:1, bass.ds(loop * N + j, 1)], min_val=0, max_val=EXPERTS - 1)
                        e = bass.ds(owner[k], 1)
                        if j >= 2:
                            dve.wait_ge(h_ready, 2 * (j - 1))
                        dve.tensor_copy(b1s[:, k, :].unsqueeze(1), g.b1[:, e, :]).then_inc(w1_staged, 1)
                        dve.tensor_copy(w1s[k].unsqueeze(1), g.w1[:, e]).then_inc(w1_staged, 1)
                        if j >= 2:
                            dve.wait_ge(y_psum, j - 1)
                        dve.tensor_copy(w2s[k].unsqueeze(1), g.w2[:, e]).then_inc(w2_staged, 1)

                    def finish(j):
                        dve.wait_ge(y_psum, j + 1)
                        if j >= 2:
                            dve.wait_ge(y_out[j % 2], 16 * (j // 2))
                        dve.tensor_tensor(y[:, j % 2, :].unsqueeze(1), y_bank[j % 2][:, 0:D].unsqueeze(1),
                                          g.b2[:, bass.ds(owner[j % 2], 1), :], ALU.add).then_inc(y_ready, 1)

                    dve.wait_ge(g.w1_in, 16 * EXPERTS)
                    dve.wait_ge(g.w2_in, 16 * (EXPERTS + 2))
                    stage(0)
                    for j in range(1, N + 1):
                        if j >= 2:
                            finish(j - 2)
                        if j < N:
                            stage(j)
                    finish(N - 1)

                @block.scalar
                def _(act):
                    def xT_out(j):
                        act.wait_ge(xT_psum, j + 1)
                        if j >= 2:
                            act.wait_ge(h_psum, 2 * (j - 1))
                        act.activation(xsT[:, j % 2].rearrange("p c n -> p (c n)"), xT_bank[j % 2][:, 0:DC * P], ACT.Copy)\
                           .then_inc(xT_ready, 1)

                    xT_out(0)
                    for j in range(N):
                        if j + 1 < N:
                            xT_out(j + 1)
                        act.wait_ge(w1_staged, 2 * (j + 1))
                        if j >= 2:
                            act.wait_ge(y_psum, j - 1)
                        for h in range(2):
                            act.wait_ge(h_psum, 2 * j + h + 1)
                            for f in range(4):
                                last = act.activation(hT[:, j % 2, 4 * h + f, :], h_bank[2 * (j % 2) + h][:, f, :], ACT.Relu,
                                                      bias=b1s[:, j % 2, 4 * h + f:4 * h + f + 1])
                            last.then_inc(h_ready, 1)

                @block.tensor
                def _(pe):
                    def flip(j):
                        pe.wait_ge(x_in[j % XB], 16 * (j // XB + 1))
                        if j >= 2:
                            pe.wait_ge(xT_ready, j - 1)
                        for c in range(DC):
                            last = pe.transpose(xT_bank[j % 2][:, c * P:(c + 1) * P], xs[:, j % XB, c * P:(c + 1) * P], g.ident[:])
                        last.then_inc(xT_psum, 1)

                    def up(j):
                        pe.wait_ge(xT_ready, j + 1)
                        pe.wait_ge(w1_staged, 2 * (j + 1))
                        if j >= 2:
                            pe.wait_ge(h_ready, 2 * (j - 1))
                        for h in range(2):
                            for f in range(4):
                                for c in range(DC):
                                    last = pe.matmul(h_bank[2 * (j % 2) + h][:, f, :], w1s[j % 2][:, c, (4 * h + f) * P:(4 * h + f + 1) * P],
                                                     xsT[:, j % 2, c, :], start=c == 0, stop=c == DC - 1)
                            last.then_inc(h_psum, 1)

                    def down(j):
                        pe.wait_ge(h_ready, 2 * (j + 1))
                        pe.wait_ge(w2_staged, j + 1)
                        if j >= 2:
                            pe.wait_ge(y_ready, j - 1)
                        for f in range(FC):
                            last = pe.matmul(y_bank[j % 2][:, 0:D], hT[:, j % 2, f, :], w2s[j % 2][:, f, :], start=f == 0, stop=f == FC - 1)
                        last.then_inc(y_psum, 1)

                    flip(0)
                    for j in range(N + 1):
                        if j + 1 < N:
                            flip(j + 1)
                        if j < N:
                            up(j)
                        if j:
                            down(j - 1)
            nc.all_engine_barrier(sems_to_clear=sem_range)


H1, DH1 = 16, 16
HG = 4
GROUPS = H1 // HG
HP = H1 // 2


def phase_attn1(nc, g):
    with ExitStack() as ctx:
        def sb(name, shape, dt=F32):
            return ctx.enter_context(nc.sbuf_tensor(f"c_{name}", shape, dt))

        def stream(name, shape, dt=F32):
            return [sb(f"{name}{s}", shape, dt) for s in range(NS)]

        sems = []

        def sem(name):
            sems.append(ctx.enter_context(nc.semaphore(f"c_{name}", num=LOOP_SEMS + len(sems))))
            return sems[-1]

        def sem2(name):
            return [sem(f"{name}{s}") for s in range(NS)]

        QK = 2 * D
        w = sb("wqkv1", [P, DC, 3 * D])
        wo = sb("wo1", [P, GROUPS, D])
        rope = sb("rope1", [P, NT, 2, 2, DH1])
        x, xn = stream("cx", [P, NT, D]), stream("cxn", [P, NT, D])
        yrow = stream("yrow", [P, NT, D])
        rowb = stream("rowb", [P, NT], I32)
        xnT = stream("cxnT", [P, DC, L])
        cosed, sined = stream("cosed", [P, QK]), stream("sined", [P, QK])
        qhl = stream("qhl", [P, H1, 4, DH1], F32R)
        khl = stream("khl", [P, H1, 4, DH1], F32R)
        qT, kT = stream("cqT", [P, HP, L], F32R), stream("ckT", [P, HP, L], F32R)
        v = stream("cv", [P, NT, H1, 2 * DH1])
        probs, probsT = stream("cprobs", [P, 2, L]), stream("cprobsT", [P, 2, NT, P])
        oT = stream("oT", [P, GROUPS, L])
        stats, mv = stream("cstats", [P, NT, 6]), stream("cmv", [P, NT, 2])
        ve, rstd = stream("cve", [P, NT]), stream("crstd", [P, NT])
        UNITS = H1 * NT
        nmax, rsum, rinv = stream("cnmax", [P, UNITS]), stream("crsum", [P, UNITS]), stream("crinv", [P, UNITS])
        identr = sb("identr", [P, P], F32R)
        bank = [[ctx.enter_context(nc.psum_tensor(f"cbank{s}{i}", [P, L], F32)) for i in range(4)]
                for s in range(NS)]

        c_in, c_set = g.once("c_in"), g.once("c_set")
        y_in = [g.once(f"rows_in{s}") for s in range(NS)]
        x_in, row_copied = sem2("cx_in"), sem2("row_copied")
        x2_ready, dve_chain, var_ready, rstd_ready = sem2("x2_ready"), sem("c_chain"), sem2("cvar"), sem2("crstd")
        xn_ready, xnT_psum, xnT_ready = sem2("cxn_ready"), sem2("cxnT_psum"), sem2("cxnT_ready")
        qk_psum, v_psum, v_ready = sem2("cqk_psum"), sem2("cv_psum"), sem2("cv_ready")
        turned, rotated, split = sem2("turned"), sem2("rotated"), sem2("split")
        qkT_psum, qkT_ready = sem2("qkT_psum"), sem2("qkT_ready")
        scores_ready, nmax_ready, probs_ready, normed = sem2("cscores"), sem2("cnmax_r"), sem2("cprobs_r"), sem2("normed")
        pT_psum, pT_ready, pv_done, oT_ready = sem2("pT_psum"), sem2("pT_ready"), sem2("pv_done"), sem2("oT_ready")
        wo_psum, x3_ready, stored = sem2("wo_psum"), sem2("x3_ready"), sem2("cstored")
        sem_range = range(sems[0].num, sems[-1].num + 1)
        assert len(sem_range) == len(sems)

        def kw(qt):
            return max(2, qt + 1) * P

        units = [(h, qt) for h in range(H1) for qt in range(NT)]

        with nc.Block() as block:
            @block.sync
            def _(sp):
                sp.dma_start(w[:], g.Wqkv1T.rearrange("(c p) n -> p c n", p=P)).then_inc(c_in, 16)
                sp.dma_start(rope[:], g.rope1).then_inc(c_in, 16)
                sp.wait_ge(c_set, 4)
                for h in range(H1):
                    j = h % HG
                    sp.dma_start(wo[32 * j:32 * j + DH1, h // HG, :], g.Wo1T[h * DH1:(h + 1) * DH1, :]).then_inc(c_in, 16)
                sp.wait_ge(c_in, 16 * (2 + H1))

            @block.gpsimd
            def _(pool):
                pool.memset(wo[:], 0.0).then_inc(c_set, 1)
                for s in range(NS):
                    pool.memset(v[s][:], 0.0).then_inc(c_set, 1)

            @block.vector
            def _(dve):
                dve.tensor_copy(identr[:], g.ident[:]).then_inc(c_set, 1)
                dve.wait_ge(c_set, 4)

        with nc.Fori(0, PAIRS) as pair:
            with nc.Block() as block:
                @block.sync
                def _(sp):
                    for s in range(NS):
                        sp.dma_start(x[s][:], g.x1_d[pair * NS + s].rearrange("(t p) n -> p t n", p=P)).then_inc(x_in[s], 16)
                    for s in range(NS):
                        sp.wait_ge(x3_ready[s], NT)
                        sp.dma_start(g.x3_d[pair * NS + s].rearrange("(t p) n -> p t n", p=P), x[s][:]).then_inc(stored[s], 16)
                    for s in range(NS):
                        sp.wait_ge(xn_ready[s], 2 * NT)
                        sp.dma_start(g.y_d[0][pair * NS + s].rearrange("(t p) n -> p t n", p=P), xn[s][:]).then_inc(stored[s], 16)
                    for s in range(NS):
                        sp.wait_ge(stored[s], 32)

                @block.gpsimd
                def _(pool):
                    def power(s, k):
                        pool.wait_ge(var_ready[s], k)
                        pool.tensor_tensor(rstd[s][:], ve[s][:], g.minus_half[:, 0:NT], ALU.pow).then_inc(rstd_ready[s], 1)

                    for s in range(NS):
                        pool.tensor_copy(rowb[s][:], g.row_of[:, bass.ds(pair * (NS * NT) + s * NT, NT)]).then_inc(row_copied[s], 1)
                    for s in range(NS):
                        pool.wait_ge(row_copied[s], 1)
                        for t in range(NT):
                            pool.indirect_dma_start(yrow[s][:, t, :], None, g.ys_d,
                                                    bass.IndirectOffsetOnAxis(ap=rowb[s][:, t:t + 1], axis=0)).then_inc(y_in[s], 16)
                    for s in range(NS):
                        power(s, 1)
                    for t in range(NT):
                        for s in range(NS):
                            pool.wait_ge(turned[s], 3 * (t + 1))
                            if t:
                                pool.wait_ge(split[s], 2 * t)
                            pool.tensor_tensor(cosed[s][:], cosed[s][:], sined[s][:], ALU.add).then_inc(rotated[s], 1)
                    for s in range(NS):
                        power(s, 2)

                @block.vector
                def _(dve):
                    chain = Chain(dve, dve_chain)

                    def norm(s, k):
                        for t, ins in layer_norm(dve, chain, var_ready[s], rstd_ready[s], k,
                                                 lambda t: [x[s][:, t, :]], stats[s], mv[s], ve[s], rstd[s],
                                                 lambda t: [xn[s][:, t, :]]):
                            ins.then_inc(xn_ready[s], 1)

                    def turn(s, t):
                        dve.wait_ge(qk_psum[s], t + 1)
                        if t:
                            dve.wait_ge(split[s], 2 * t)
                        def heads(a):
                            return a.rearrange("p (i h d) -> p i h d", i=2, d=DH1)

                        src, out = heads(bank[s][0][:]), heads(sined[s][:])
                        dve.tensor_tensor(heads(cosed[s][:]), src, rope[:, t, :, 0, :].unsqueeze(2).to_broadcast([P, 2, H1, DH1]),
                                          ALU.mult).then_inc(turned[s], 1)
                        for a in range(2):
                            dve.tensor_tensor(out[:, :, :, a::2], src[:, :, :, 1 - a::2],
                                              rope[:, t, :, 1, a::2].unsqueeze(2).to_broadcast([P, 2, H1, DH1 // 2]),
                                              ALU.mult).then_inc(turned[s], 1)

                    def parts(s, t):
                        dve.wait_ge(rotated[s], t + 1)
                        if t:
                            dve.wait_ge(qkT_psum[s], 4 * t)
                        q = cosed[s][:, 0:D].rearrange("p (h d) -> p h d", d=DH1)
                        k = cosed[s][:, D:QK].rearrange("p (h d) -> p h d", d=DH1)
                        twice = [P, H1, 2, DH1]
                        hi = [(qhl[s][:, :, 0::2, :], q), (khl[s][:, :, 0:2, :], k)]
                        lo = [(qhl[s][:, :, 1::2, :], q), (khl[s][:, :, 2:4, :], k)]
                        for dst, src in hi:
                            m = chain.mark(dve.tensor_copy(dst, src.unsqueeze(2).to_broadcast(twice)))
                        chain.wait(m)
                        for (dst, src), (high, _) in zip(lo, hi):
                            dve.tensor_tensor(dst, src.unsqueeze(2).to_broadcast(twice), high.bitcast(F32), ALU.subtract)\
                               .then_inc(split[s], 1)

                    def row_max(s, u):
                        h, qt = units[u]
                        dve.wait_ge(scores_ready[s], u + 1)
                        dve.tensor_reduce(nmax[s][:, u:u + 1], bank[s][u % 2][:, 0:(qt + 1) * P], AX, ALU.max, negate=True)\
                           .then_inc(nmax_ready[s], 1)

                    def norm_probs(s, u):
                        n = (units[u][1] + 1) * P
                        dve.wait_ge(probs_ready[s], u + 1)
                        chain.step(dve.reciprocal(rinv[s][:, u:u + 1], rsum[s][:, u:u + 1]))
                        dve.tensor_scalar(probs[s][:, u % 2, 0:n], probs[s][:, u % 2, 0:n], rinv[s][:, u:u + 1], None, ALU.mult)\
                           .then_inc(normed[s], 1)

                    def pT_out(s, u):
                        n = units[u][1] + 1
                        dve.wait_ge(pT_psum[s], u + 1)
                        if u >= 2:
                            dve.wait_ge(pv_done[s], u - 1)
                        dve.tensor_copy(probsT[s][:, u % 2, 0:n, :], bank[s][2][:, 0:n * P].rearrange("p (a b) -> p a b", b=P)).then_inc(pT_ready[s], 1)

                    for s in range(NS):
                        dve.wait_ge(x_in[s], 16)
                        dve.wait_ge(y_in[s], pair * (16 * NT) + 16 * NT)
                        dve.tensor_tensor(x[s][:], x[s][:], yrow[s][:], ALU.add).then_inc(x2_ready[s], 1)
                    for s in range(NS):
                        dve.wait_ge(x2_ready[s], 1)
                        norm(s, 1)
                    for t in range(NT + 1):
                        for s in range(NS):
                            if t:
                                parts(s, t - 1)
                            if t < NT:
                                turn(s, t)
                    for u in range(UNITS + 1):
                        for s in range(NS):
                            if u:
                                norm_probs(s, u - 1)
                        for s in range(NS):
                            if u < UNITS:
                                row_max(s, u)
                        for s in range(NS):
                            if u % 2:
                                pT_out(s, u - 1)
                    for s in range(NS):
                        for t in range(NT):
                            dve.wait_ge(wo_psum[s], t + 1)
                            dve.tensor_tensor(x[s][:, t, :], bank[s][t % 2][:, 0:D], x[s][:, t, :], ALU.add).then_inc(x3_ready[s], 1)
                    for s in range(NS):
                        dve.wait_ge(x3_ready[s], NT)
                        norm(s, 2)

                @block.scalar
                def _(act):
                    for s in range(NS):
                        for c in range(DC):
                            act.wait_ge(xnT_psum[s], c + 1)
                            act.activation(xnT[s][:, c, :], bank[s][c][:], ACT.Copy).then_inc(xnT_ready[s], 1)

                    def qkT_out(s, t, i):
                        act.wait_ge(qkT_psum[s], 4 * t + i + 1)
                        dst = (qT, kT)[i // 2][s]
                        act.activation(dst[:, 4 * (i % 2):4 * (i % 2) + 4, t * P:(t + 1) * P],
                                       bank[s][2 + i % 2][:].rearrange("p (a b) -> p a b", b=P), ACT.Copy).then_inc(qkT_ready[s], 1)

                    for t in range(NT + 1):
                        for s in range(NS):
                            if t < NT:
                                act.wait_ge(v_psum[s], t + 1)
                                act.activation(v[s][:, t, :, 0:DH1], bank[s][1][:, 0:D].rearrange("p (h d) -> p h d", d=DH1), ACT.Copy)\
                                   .then_inc(v_ready[s], 1)
                            if t:
                                for i in range(4):
                                    qkT_out(s, t - 1, i)
                    def exps(s, u):
                        n = (units[u][1] + 1) * P
                        act.wait_ge(nmax_ready[s], u + 1)
                        if u >= 2:
                            act.wait_ge(pT_psum[s], u - 1)
                        act.activation(probs[s][:, u % 2, 0:n], bank[s][u % 2][:, 0:n], ACT.Exp, bias=nmax[s][:, u:u + 1],
                                       accum_out=rsum[s][:, u:u + 1]).then_inc(probs_ready[s], 1)

                    def pT_out(s, u):
                        n = units[u][1] + 1
                        act.wait_ge(pT_psum[s], u + 1)
                        if u >= 2:
                            act.wait_ge(pv_done[s], u - 1)
                        act.activation(probsT[s][:, u % 2, 0:n, :], bank[s][2][:, 0:n * P].rearrange("p (a b) -> p a b", b=P), ACT.Copy)\
                           .then_inc(pT_ready[s], 1)

                    def oT_out(s, i):
                        act.wait_ge(pv_done[s], HG * NT * (i + 1))
                        act.activation(oT[s][:, i, :], bank[s][3][:], ACT.Copy).then_inc(oT_ready[s], 1)

                    for u in range(UNITS + 2):
                        for s in range(NS):
                            if u < UNITS:
                                exps(s, u)
                        for s in range(NS):
                            if 1 <= u <= UNITS and u % 2 == 0:
                                pT_out(s, u - 1)
                            if u >= 2 and (u - 1) % (HG * NT) == 0:
                                oT_out(s, (u - 1) // (HG * NT) - 1)

                @block.tensor
                def _(pe):
                    def transposes(s):
                        for c in range(DC):
                            for t in range(NT):
                                if c == 0:
                                    pe.wait_ge(xn_ready[s], t + 1)
                                last = pe.transpose(bank[s][c][:, t * P:(t + 1) * P], xn[s][:, t, c * P:(c + 1) * P], g.ident[:])
                            last.then_inc(xnT_psum[s], 1)

                    def project(s, t):
                        if t == 0:
                            pe.wait_ge(xnT_ready[s], DC)
                        else:
                            pe.wait_ge(turned[s], 3 * t)
                        for c in range(DC):
                            last = pe.matmul(bank[s][0][:], xnT[s][:, c, t * P:(t + 1) * P], w[:, c, 0:QK], start=c == 0, stop=c == DC - 1)
                        last.then_inc(qk_psum[s], 1)
                        if t:
                            pe.wait_ge(v_ready[s], t)
                        for c in range(DC):
                            last = pe.matmul(bank[s][1][:, 0:D], xnT[s][:, c, t * P:(t + 1) * P], w[:, c, QK:3 * D], start=c == 0, stop=c == DC - 1)
                        last.then_inc(v_psum[s], 1)

                    def flip_qk(s, t):
                        pe.wait_ge(split[s], 2 * (t + 1))
                        for i in range(4):
                            if 4 * t + i >= 2:
                                pe.wait_ge(qkT_ready[s], 4 * t + i - 1)
                            out = bank[s][2 + i % 2]
                            for a in range(4):
                                p = 4 * (i % 2) + a
                                src = (qhl, khl)[i // 2][s][:, 2 * p:2 * p + 2].rearrange("p h a d -> p (h a d)")
                                last = pe.transpose(out[:, a * P:(a + 1) * P].bitcast(F32R), src, identr[:])
                            last.then_inc(qkT_psum[s], 1)

                    def scores(s, u):
                        h, qt = units[u]
                        if u == 0:
                            pe.wait_ge(qkT_ready[s], 4 * NT)
                            pe.wait_ge(v_ready[s], NT)
                        if u >= 2:
                            pe.wait_ge(probs_ready[s], u - 1)
                        r = slice(64 * (h % 2), 64 * (h % 2) + 64)
                        S = bank[s][u % 2]
                        pe.matmul(S[:, 0:kw(qt)], qT[s][r, h // 2, qt * P:(qt + 1) * P], kT[s][r, h // 2, 0:kw(qt)], start=True, stop=False)
                        pe.matmul(S[:, qt * P:(qt + 1) * P], g.mask[:, 0, :], g.mask[:, 2, :], start=False, stop=True)\
                          .then_inc(scores_ready[s], 1)

                    def flip(s, u):
                        h, qt = units[u]
                        pe.wait_ge(normed[s], u + 1)
                        if u:
                            pe.wait_ge(pT_ready[s], u)
                        for kt in range(qt + 1):
                            last = pe.transpose(bank[s][2][:, kt * P:(kt + 1) * P], probs[s][:, u % 2, kt * P:(kt + 1) * P], g.ident[:])
                        last.then_inc(pT_psum[s], 1)

                    def output(s, u):
                        h, qt = units[u]
                        pe.wait_ge(pT_ready[s], u + 1)
                        if qt == 0 and h and h % HG == 0:
                            pe.wait_ge(oT_ready[s], h // HG)
                        j = h % HG
                        for kt in range(qt + 1):
                            last = pe.matmul(bank[s][3][32 * j:32 * j + 32, qt * P:(qt + 1) * P], v[s][:, kt, h, :], probsT[s][:, u % 2, kt, :],
                                             start=kt == 0, stop=kt == qt, tile_position=(0, 32 * j))
                        last.then_inc(pv_done[s], 1)

                    for s in range(NS):
                        transposes(s)
                    for t in range(NT + 1):
                        for s in range(NS):
                            if t < NT:
                                project(s, t)
                            if t:
                                flip_qk(s, t - 1)
                    for u in range(UNITS + 2):
                        for s in range(NS):
                            if u < UNITS:
                                scores(s, u)
                        for s in range(NS):
                            if u >= 2:
                                output(s, u - 2)
                        for s in range(NS):
                            if 1 <= u <= UNITS:
                                flip(s, u - 1)
                    for s in range(NS):
                        pe.wait_ge(oT_ready[s], GROUPS)
                        for t in range(NT):
                            if t >= 2:
                                pe.wait_ge(x3_ready[s], t - 1)
                            for c in range(GROUPS):
                                last = pe.matmul(bank[s][t % 2][:, 0:D], oT[s][:, c, t * P:(t + 1) * P], wo[:, c, :], start=c == 0, stop=c == GROUPS - 1)
                            last.then_inc(wo_psum[s], 1)
            nc.all_engine_barrier(sems_to_clear=sem_range)


H2, DH2 = 8, 64
INNER = H2 * DH2
HP2 = H2 // 2
HID = 682
UC = (HID + P - 1) // P


def phase_layer(nc, g, layer):
    final = layer == 1
    with ExitStack() as ctx:
        def sb(name, shape, dt=F32):
            return ctx.enter_context(nc.sbuf_tensor(f"l{layer}_{name}", shape, dt))

        def stream(name, shape, dt=F32):
            return [sb(f"{name}{s}", shape, dt) for s in range(NS)]

        sems = []

        def sem(name):
            sems.append(ctx.enter_context(nc.semaphore(f"l{layer}_{name}", num=LOOP_SEMS + len(sems))))
            return sems[-1]

        def sem2(name):
            return [sem(f"{name}{s}") for s in range(NS)]

        wqkv = sb("wqkv", [P, DC, 3 * INNER])
        wo = sb("wo", [P, HP2, D])
        w1 = sb("w1", [P, DC, 2 * HID])
        w2 = sb("w2", [P, UC, D])
        b1 = sb("b1", [P, 2, UC])
        b2 = sb("b2", [P, D])
        lng = sb("lng", [P, 2, DC])
        scales = sb("scales", [P, 2, DH2])
        rope = sb("rope", [P, NT, 4, DH2])
        scaled = sb("scaled", [P, NT, 4, DH2])
        y, hn = stream("y", [P, NT, D]), stream("hn", [P, NT, D])
        yT = stream("yT", [P, DC, L + 1])
        work = stream("work", [P, 3, 2 * INNER])
        squares, rot2 = ([w[:, i, :] for w in work] for i in (0, 2))
        uT = [w[:].rearrange("p a (b n) -> p (a b) n", n=L) for w in work]
        assert uT[0].shape[1] == UC
        ss, inv = stream("ss", [P, 2 * H2]), stream("inv", [P, 2 * H2])
        qT, kT = stream("qT", [P, HP2, L]), stream("kT", [P, 2, HP2, L])
        v = stream("v", [P, NT, INNER])
        probs, probsT = stream("probs", [P, 2, 2, 2 * P]), stream("probsT", [P, 2, 4, P])
        rot = [[work[s][:, 1, :], probs[s][:].rearrange("p a b c -> p (a b c)")] for s in range(NS)]
        oT = stream("oT", [P, HP2, L])
        gate = stream("gate", [P, 2, L])
        stats, mv = stream("stats", [P, NT, 12]), stream("mv", [P, NT, 2])
        ve, rstd = stream("ve", [P, NT]), stream("rstd", [P, NT])
        UNITS = HP2 * NT
        nmax, rsum, rinv = stream("nmax", [P, UNITS, 2]), stream("rsum", [P, UNITS, 2]), stream("rinv", [P, UNITS, 2])
        bank = [[ctx.enter_context(nc.psum_tensor(f"l{layer}_bank{s}{i}", [P, L], F32)) for i in range(4)]
                for s in range(NS)]

        w_in, w_set = g.once(f"w_in{layer}"), g.once(f"w_set{layer}")
        y_in, yT_psum, yT_ready = sem2("y_in"), sem2("yT_psum"), sem2("yT_ready")
        qkv_psum, squared, v_ready, summed = sem2("qkv_psum"), sem2("squared"), sem2("v_ready"), sem2("summed")
        inv_ready, turned, added, rotated = sem2("inv_ready"), sem2("turned"), sem2("added"), sem2("rotated")
        qkT_psum, qkT_ready = sem2("qkT_psum"), sem2("qkT_ready")
        scores_ready, nmax_ready, probs_ready, normed = sem2("scores"), sem2("nmax_r"), sem2("probs_r"), sem2("normed")
        pT_psum, pT_ready, pv_done, oT_ready = sem2("pT_psum"), sem2("pT_ready"), sem2("pv_done"), sem2("oT_ready")
        wo_psum, y1_ready, shifted = sem2("wo_psum"), sem2("y1_ready"), sem2("shifted")
        chain_sem, var_ready, rstd_ready, hn_ready = sem("chain"), sem2("var"), sem2("rstd_r"), sem2("hn_ready")
        biased, hT_psum, hT_ready = sem2("biased"), sem2("hT_psum"), sem2("hT_ready")
        ag_psum, gate_ready, u_ready = sem2("ag_psum"), sem2("gate_ready"), sem2("u_ready")
        w2_psum, y2_ready, x_in, stored, xadded = sem2("w2_psum"), sem2("y2_ready"), sem2("x_in"), sem2("stored"), sem2("xadded")
        sem_range = range(sems[0].num, sems[-1].num + 1)
        assert len(sem_range) == len(sems)
        units = [(cp, w, r) for cp in range(HP2 // 2) for w in range(NT) for r in range(2)]

        turns = [(s, t) for t in range(NT) for s in range(NS)]
        LAG = 3

        def rows(c):
            return min(P, HID - c * P)

        WHOLE = HID // P * P
        LOADS = [(wqkv[:], g.wqkv[layer].rearrange("(c p) n -> p c n", p=P)), (wo[:], g.wo[layer].rearrange("(c p) n -> p c n", p=P)),
                 (w1[:], g.w1d[layer].rearrange("(c p) n -> p c n", p=P)),
                 (w2[:, 0:UC - 1, :], g.w2d[layer][0:WHOLE].rearrange("(c p) n -> p c n", p=P)),
                 (w2[0:rows(UC - 1), UC - 1, :], g.w2d[layer][WHOLE:HID]),
                 (b2[:], g.b2l[layer].partition_broadcast(P)),
                 (lng[:, 0, :], g.lng[layer]), (lng[:, 1, :], g.lnb[layer]),
                 (scales[:, 0, :], g.qs[layer].partition_broadcast(P)), (scales[:, 1, :], g.ks[layer].partition_broadcast(P)),
                 (b1[:], g.b1l[layer]), (rope[:], g.rope2)]

        with nc.Block() as block:
            @block.sync
            def _(sp):
                for dst, src in LOADS:
                    sp.dma_start(dst, src).then_inc(w_in, 16)

            @block.vector
            def _(dve):
                for s in range(NS):
                    dve.memset(yT[s][:, 1, 0:1], 0.0)
                    dve.memset(kT[s][DH2:P, 0], 0.0)
                    dve.memset(kT[s][0:DH2, 1], 0.0).then_inc(w_set, 1)
                dve.wait_ge(w_in, 16 * len(LOADS))
                for i in range(2):
                    dve.tensor_tensor(scaled[:, :, 2 * i, :], rope[:, :, 2 * i, :],
                                      scales[:, i, :].unsqueeze(1).to_broadcast([P, NT, DH2]), ALU.mult).then_inc(w_set, 1)
                    for a in range(2):
                        h = DH2 // 2
                        dve.tensor_tensor(scaled[:, :, 2 * i + 1, a * h:(a + 1) * h], rope[:, :, 2 * i + 1, a * h:(a + 1) * h],
                                          scales[:, i, (1 - a) * h:(2 - a) * h].unsqueeze(1).to_broadcast([P, NT, h]),
                                          ALU.mult).then_inc(w_set, 1)
                dve.wait_ge(w_set, NS + 6)

        with nc.Fori(0, PAIRS) as pair:
            with nc.Block() as block:
                @block.sync
                def _(sp):
                    for s in range(NS):
                        sp.dma_start(y[s][:], g.y_d[layer][pair * NS + s].rearrange("(t p) n -> p t n", p=P)).then_inc(y_in[s], 16)
                    if final:
                        for s in range(NS):
                            sp.wait_ge(hT_psum[s], DC)
                            sp.dma_start(hn[s][:], g.x3_d[pair * NS + s].rearrange("(t p) n -> p t n", p=P)).then_inc(x_in[s], 16)
                    dst = g.out if final else g.y_d[layer + 1]
                    for s in range(NS):
                        sp.wait_ge(y2_ready[s], NT)
                        sp.dma_start(dst[pair * NS + s].rearrange("(t p) n -> p t n", p=P), y[s][:]).then_inc(stored[s], 16)
                    for s in range(NS):
                        sp.wait_ge(stored[s], 16)

                @block.gpsimd
                def _(pool):
                    for s, t in turns:
                        pool.wait_ge(turned[s], 7 * t + 3)
                        pool.tensor_tensor(rot[s][t % 2][:, 0:INNER], rot[s][t % 2][:, 0:INNER], rot2[s][:, 0:INNER], ALU.add).then_inc(added[s], 1)
                        pool.wait_ge(summed[s], t + 1)
                        pool.tensor_tensor(inv[s][:], ss[s][:], g.minus_half[:], ALU.pow).then_inc(inv_ready[s], 1)
                    for s in range(NS):
                        pool.wait_ge(var_ready[s], 1)
                        pool.tensor_tensor(rstd[s][:], ve[s][:], g.minus_half[:, 0:NT], ALU.pow).then_inc(rstd_ready[s], 1)
                    for s in range(NS):
                        pool.wait_ge(hn_ready[s], 2 * NT)
                        pool.wait_ge(shifted[s], 1)
                        pool.tensor_tensor(y[s][:], y[s][:], b2[:].unsqueeze(1).to_broadcast([P, NT, D]), ALU.add).then_inc(biased[s], 1)
                    if final:
                        for s in range(NS):
                            pool.wait_ge(x_in[s], 16)
                            pool.wait_ge(biased[s], 1)
                            pool.tensor_tensor(y[s][:], y[s][:], hn[s][:], ALU.add).then_inc(xadded[s], 1)

                @block.vector
                def _(dve):
                    chain = Chain(dve, chain_sem)

                    def heads(a):
                        return a.rearrange("p (h d) -> p h d", d=DH2)

                    def norms(s, t):
                        if t:
                            dve.wait_ge(inv_ready[s], t)
                        chain.step(dve.tensor_reduce(ss[s][:], heads(squares[s]), AX, ALU.add))
                        dve.tensor_scalar(ss[s][:], ss[s][:], 1e-24, None, ALU.max).then_inc(summed[s], 1)

                    def turn(s, t):
                        if t:
                            dve.wait_ge(added[s], t)
                        if t >= 2:
                            dve.wait_ge(qkT_psum[s], 2 * (t - 1))
                        h, rot_t = DH2 // 2, rot[s][t % 2]
                        for i in range(2):
                            src = heads(bank[s][i][:])
                            dst, dst2 = (heads(a[:, i * INNER:(i + 1) * INNER]) for a in (rot_t, rot2[s]))
                            dve.wait_ge(squared[s], 2 * t + i + 1)
                            dve.tensor_tensor(dst, src, scaled[:, t, 2 * i:2 * i + 1, :].to_broadcast([P, H2, DH2]), ALU.mult).then_inc(turned[s], 1)
                            for a in range(2):
                                dve.tensor_tensor(dst2[:, :, a * h:(a + 1) * h], src[:, :, (1 - a) * h:(2 - a) * h],
                                                  scaled[:, t, 2 * i + 1:2 * i + 2, a * h:(a + 1) * h].to_broadcast([P, H2, h]),
                                                  ALU.mult).then_inc(turned[s], 1)

                        dve.wait_ge(turned[s], 7 * t + 6)
                        dve.tensor_tensor(rot_t[:, INNER:2 * INNER], rot_t[:, INNER:2 * INNER], rot2[s][:, INNER:2 * INNER], ALU.add)\
                           .then_inc(turned[s], 1)

                    def normalise(s, t):
                        dve.wait_ge(turned[s], 7 * (t + 1))
                        dve.wait_ge(added[s], t + 1)
                        dve.wait_ge(inv_ready[s], t + 1)
                        dve.tensor_tensor(heads(rot[s][t % 2]), heads(rot[s][t % 2]), inv[s][:].unsqueeze(2).to_broadcast([P, 2 * H2, DH2]), ALU.mult)\
                           .then_inc(rotated[s], 1)

                    def row_max(s, u):
                        w = units[u][1]
                        dve.wait_ge(scores_ready[s], u + 1)
                        S = bank[s][u % 2][:].rearrange("p (h k) -> p h k", h=2)
                        dve.tensor_reduce(nmax[s][:, u, :], S[:, :, 0:(1 + min(w, 1)) * P], AX, ALU.max, negate=True).then_inc(nmax_ready[s], 1)

                    def norm_probs(s, u):
                        w = units[u][1]
                        n = (1 + min(w, 1)) * P
                        dve.wait_ge(probs_ready[s], 2 * (u + 1))
                        chain.step(dve.reciprocal(rinv[s][:, u, :], rsum[s][:, u, :]))
                        for h in range(2):
                            dve.tensor_scalar(probs[s][:, u % 2, h, 0:n], probs[s][:, u % 2, h, 0:n], rinv[s][:, u, h:h + 1], None, ALU.mult)\
                               .then_inc(normed[s], 1)

                    for i in range(len(turns) + 1):
                        if i < len(turns):
                            turn(*turns[i])
                            norms(*turns[i])
                        if i:
                            normalise(*turns[i - 1])
                    for u in range(UNITS + 1):
                        for s in range(NS):
                            if u:
                                norm_probs(s, u - 1)
                        for s in range(NS):
                            if u < UNITS:
                                row_max(s, u)
                    for s in range(NS):
                        for t in range(NT):
                            dve.wait_ge(wo_psum[s], t + 1)
                            dve.tensor_tensor(y[s][:, t, :], bank[s][t % 2][:, 0:D], y[s][:, t, :], ALU.add).then_inc(y1_ready[s], 1)
                    for s in range(NS):
                        dve.wait_ge(y1_ready[s], NT)
                        dve.wait_ge(shifted[s], 1)
                        late = bank[s][2][:].rearrange("p (t n) -> p t n", t=NT)
                        for t, ins in layer_norm(dve, chain, var_ready[s], rstd_ready[s], 1,
                                                 lambda t: [y[s][:, t, 0:P], late[:, t, :]], stats[s], mv[s], ve[s], rstd[s],
                                                 lambda t: [hn[s][:, t, 0:P], hn[s][:, t, P:D]]):
                            ins.then_inc(hn_ready[s], 1)
                    for s in range(NS):
                        for c in range(DC):
                            dve.wait_ge(hT_psum[s], c + 1)
                            dve.tensor_scalar(yT[s][:, c, 1:L + 1], bank[s][c][:], lng[:, 0, c:c + 1], lng[:, 1, c:c + 1], ALU.mult, ALU.add)\
                               .then_inc(hT_ready[s], 1)
                    for c in range(UC):
                        r = rows(c)
                        for s in range(NS):
                            dve.wait_ge(gate_ready[s], c + 1)
                            dve.scalar_tensor_tensor(uT[s][0:r, c, :], bank[s][2 * (c % 2)][0:r, :], b1[0:r, 0, c:c + 1], gate[s][0:r, c % 2, :],
                                                     ALU.add, ALU.mult).then_inc(u_ready[s], 1)
                    for s in range(NS):
                        dve.wait_ge(xadded[s] if final else biased[s], 1)
                        for t in range(NT):
                            dve.wait_ge(w2_psum[s], t + 1)
                            dve.tensor_tensor(y[s][:, t, :], bank[s][t % 2][:, 0:D], y[s][:, t, :], ALU.add).then_inc(y2_ready[s], 1)

                @block.scalar
                def _(act):
                    for s in range(NS):
                        for c in range(DC):
                            act.wait_ge(yT_psum[s], c + 1)
                            act.activation(yT[s][:, c, c:L + c], bank[s][c][:, 0:L], ACT.Copy).then_inc(yT_ready[s], 1)

                    def qT_out(s, t):
                        act.wait_ge(qkT_psum[s], 2 * t + 1)
                        act.activation(qT[s][:, :, t * P:(t + 1) * P], bank[s][3][:].rearrange("p (a b) -> p a b", b=P), ACT.Copy)\
                           .then_inc(qkT_ready[s], 1)

                    def kT_out(s, t):
                        act.wait_ge(qkT_psum[s], 2 * t + 2)
                        src = bank[s][3][:].rearrange("p (a b) -> p a b", b=P)
                        for half in range(2):
                            r = slice(DH2 * half, DH2 * (half + 1))
                            last = act.activation(kT[s][r, half, :, t * P:(t + 1) * P], src[r], ACT.Copy)
                        last.then_inc(qkT_ready[s], 1)

                    def square(s, t, j):
                        act.wait_ge(qkv_psum[s], 3 * t + j + 1)
                        act.activation(squares[s][:, j * INNER:(j + 1) * INNER], bank[s][j][:], ACT.Square).then_inc(squared[s], 1)

                    for i in range(len(turns) + LAG):
                        now = turns[i] if i < len(turns) else None
                        before = turns[i - LAG] if i >= LAG else None
                        if now:
                            if now[1]:
                                act.wait_ge(summed[now[0]], now[1])
                            square(*now, 0)
                        if before:
                            qT_out(*before)
                        if now:
                            square(*now, 1)
                        if before:
                            kT_out(*before)
                        if now:
                            s, t = now
                            act.wait_ge(qkv_psum[s], 3 * (t + 1))
                            act.activation(v[s][:, t, :], bank[s][2][:], ACT.Copy).then_inc(v_ready[s], 1)

                    def exps(s, u):
                        w = units[u][1]
                        n = (1 + min(w, 1)) * P
                        act.wait_ge(nmax_ready[s], u + 1)
                        if u >= 2:
                            act.wait_ge(pT_psum[s], u - 1)
                        for h in range(2):
                            act.activation(probs[s][:, u % 2, h, 0:n], bank[s][u % 2][:, 2 * P * h:2 * P * h + n], ACT.Exp,
                                           bias=nmax[s][:, u, h:h + 1], accum_out=rsum[s][:, u, h:h + 1]).then_inc(probs_ready[s], 1)

                    def pT_out(s, u):
                        act.wait_ge(pT_psum[s], u + 1)
                        if u >= 2:
                            act.wait_ge(pv_done[s], u - 1)
                        if units[u][1]:
                            act.activation(probsT[s][:, u % 2].rearrange("p a b -> p (a b)"), bank[s][2][:], ACT.Copy).then_inc(pT_ready[s], 1)
                        else:
                            act.activation(probsT[s][:, u % 2, 0:4:2, :], bank[s][2][:].rearrange("p (a b) -> p a b", b=P)[:, 0:4:2, :], ACT.Copy)\
                               .then_inc(pT_ready[s], 1)

                    def oT_out(s, i):
                        cp, w = i // NT, i % NT
                        act.wait_ge(pv_done[s], 2 * (i + 1))
                        act.activation(oT[s][:, 2 * cp:2 * cp + 2, w * P:(w + 1) * P], bank[s][3][:, 0:2 * P].rearrange("p (a b) -> p a b", b=P),
                                       ACT.Copy).then_inc(oT_ready[s], 1)

                    for u in range(UNITS + 2):
                        for s in range(NS):
                            if u < UNITS:
                                exps(s, u)
                        for s in range(NS):
                            if 1 <= u <= UNITS:
                                pT_out(s, u - 1)
                            if u >= 2 and u % 2:
                                oT_out(s, (u - 2) // 2)
                    for c in range(UC):
                        r = rows(c)
                        for s in range(NS):
                            act.wait_ge(ag_psum[s], c + 1)
                            if c >= 2:
                                act.wait_ge(u_ready[s], c - 1)
                            act.activation(gate[s][0:r, c % 2, :], bank[s][2 * (c % 2) + 1][0:r, :], ACT.Gelu, bias=b1[0:r, 1, c:c + 1])\
                               .then_inc(gate_ready[s], 1)

                @block.tensor
                def _(pe):
                    for s in range(NS):
                        pe.wait_ge(y_in[s], 16)
                        for c in range(DC):
                            for t in range(NT):
                                last = pe.transpose(bank[s][c][:, t * P:(t + 1) * P], y[s][:, t, c * P:(c + 1) * P], g.ident[:])
                            last.then_inc(yT_psum[s], 1)

                    def project(s, t, i):
                        if i == 0 and t == 0:
                            pe.wait_ge(yT_ready[s], DC)
                        elif i == 0:
                            pe.wait_ge(turned[s], 7 * t)
                        elif i == 2 and t:
                            pe.wait_ge(v_ready[s], t)
                        for c in range(DC):
                            last = pe.matmul(bank[s][i][:], yT[s][:, c, t * P:(t + 1) * P], wqkv[:, c, i * INNER:(i + 1) * INNER],
                                             start=c == 0, stop=c == DC - 1)
                        last.then_inc(qkv_psum[s], 1)

                    def flip_qk(s, t, i):
                        pe.wait_ge(rotated[s], t + 1)
                        if 2 * t + i >= 1:
                            pe.wait_ge(qkT_ready[s], 2 * t + i)
                        for a in range(HP2):
                            last = pe.transpose(bank[s][3][:, a * P:(a + 1) * P], rot[s][t % 2][:, i * INNER + a * P:i * INNER + (a + 1) * P], g.ident[:])
                        last.then_inc(qkT_psum[s], 1)

                    def scores(s, u):
                        cp, w, half = units[u]
                        if u == 0:
                            pe.wait_ge(qkT_ready[s], 2 * NT)
                            pe.wait_ge(v_ready[s], NT)
                        if u >= 2:
                            pe.wait_ge(probs_ready[s], 2 * (u - 1))
                        k0, n = (w - 1, 2) if w else (0, 1)
                        for h in range(2):
                            p = 2 * cp + h
                            out = bank[s][u % 2][:, 2 * P * h:2 * P * h + n * P]
                            pe.matmul(out, qT[s][:, p, w * P:(w + 1) * P], kT[s][:, half, p, k0 * P:(k0 + n) * P], start=True, stop=False)
                            last = pe.matmul(out, g.mask[:, 0, :], g.mask[:, 3 - n:3, :].rearrange("p a b -> p (a b)"), start=False, stop=True)
                        last.then_inc(scores_ready[s], 1)

                    def flip(s, u):
                        w = units[u][1]
                        pe.wait_ge(normed[s], 2 * (u + 1))
                        if u:
                            pe.wait_ge(pT_ready[s], u)
                        for h in range(2):
                            for k in range(1 + min(w, 1)):
                                last = pe.transpose(bank[s][2][:, (2 * h + k) * P:(2 * h + k + 1) * P], probs[s][:, u % 2, h, k * P:(k + 1) * P], g.ident[:])
                        last.then_inc(pT_psum[s], 1)

                    def output(s, u):
                        cp, w, half = units[u]
                        pe.wait_ge(pT_ready[s], u + 1)
                        if half == 0 and u:
                            pe.wait_ge(oT_ready[s], u // 2)
                        k0, n = (w - 1, 2) if w else (0, 1)
                        for h in range(2):
                            for k in range(n):
                                head = (2 * (2 * cp + h) + half) * DH2
                                last = pe.matmul(bank[s][3][DH2 * half:DH2 * (half + 1), h * P:(h + 1) * P], v[s][:, k0 + k, head:head + DH2],
                                                 probsT[s][:, u % 2, 2 * h + k, :], start=k == 0, stop=k == n - 1, tile_position=(0, DH2 * half))
                        last.then_inc(pv_done[s], 1)

                    def hidden(s, c):
                        if c >= 2:
                            pe.wait_ge(u_ready[s], c - 1)
                        r = rows(c)
                        for i in range(2):
                            for k in range(DC):
                                last = pe.matmul(bank[s][2 * (c % 2) + i][0:r, :], w1[:, k, i * HID + c * P:i * HID + c * P + r],
                                                 yT[s][:, k, 1:L + 1], start=k == 0, stop=k == DC - 1)
                        last.then_inc(ag_psum[s], 1)

                    for i in range(len(turns) + LAG):
                        for j in range(3):
                            if i < len(turns):
                                project(*turns[i], j)
                            if i >= LAG and j < 2:
                                flip_qk(*turns[i - LAG], j)
                    for u in range(UNITS + 2):
                        for s in range(NS):
                            if u < UNITS:
                                scores(s, u)
                        for s in range(NS):
                            if u >= 2:
                                output(s, u - 2)
                        for s in range(NS):
                            if 1 <= u <= UNITS:
                                flip(s, u - 1)
                    for s in range(NS):
                        pe.wait_ge(oT_ready[s], UNITS // 2)
                        for t in range(NT):
                            if t >= 2:
                                pe.wait_ge(y1_ready[s], t - 1)
                            for c in range(HP2):
                                last = pe.matmul(bank[s][t % 2][:, 0:D], oT[s][:, c, t * P:(t + 1) * P], wo[:, c, :], start=c == 0, stop=c == HP2 - 1)
                            last.then_inc(wo_psum[s], 1)
                    for s in range(NS):
                        pe.wait_ge(y1_ready[s], NT)
                        late = bank[s][2][:].rearrange("p (t n) -> p t n", t=NT)
                        pe.matmul(late, g.shift[:, 0, :], y[s][:, :, P:D], start=True, stop=False)
                        pe.matmul(late[:, 1:NT, :], g.shift[:, 1, :], y[s][:, 0:NT - 1, P:D], start=False, stop=True).then_inc(shifted[s], 1)
                    for s in range(NS):
                        for c in range(DC):
                            for t in range(NT):
                                pe.wait_ge(hn_ready[s], 2 * (t + 1))
                                last = pe.transpose(bank[s][c][:, t * P:(t + 1) * P], hn[s][:, t, c * P:(c + 1) * P], g.ident[:])
                            last.then_inc(hT_psum[s], 1)
                    for c in range(UC):
                        for s in range(NS):
                            if c == 0:
                                pe.wait_ge(hT_ready[s], DC)
                            hidden(s, c)
                    for s in range(NS):
                        pe.wait_ge(u_ready[s], UC)
                        for t in range(NT):
                            if t >= 2:
                                pe.wait_ge(y2_ready[s], t - 1)
                            for c in range(UC):
                                r = rows(c)
                                last = pe.matmul(bank[s][t % 2][:, 0:D], uT[s][0:r, c, t * P:(t + 1) * P], w2[0:r, c, :], start=c == 0, stop=c == UC - 1)
                            last.then_inc(w2_psum[s], 1)
            nc.all_engine_barrier(sems_to_clear=sem_range)


def shape_tables():
    f = np.float32
    t = {}
    scale_vec = ((np.arange(0, D, 2, dtype=f) + f(0.4 * D)) / f(1.4 * D)).astype(f)
    scale = (scale_vec[None, :] ** (np.arange(L, dtype=f) / f(512.0))[:, None]).astype(f)
    inv_freq = (f(1.0) / f(10000.0) ** (np.arange(D // 2, dtype=f) / f(D // 2))).astype(f)
    angle = (np.arange(L, dtype=f)[:, None] * inv_freq[None, :]).astype(f)
    sin, cos = np.sin(angle), np.cos(angle)
    inv = (f(1.0) / scale).astype(f)
    t["xpos0"] = np.stack([(cos * scale).T, (sin * scale).T, (cos * inv).T, (sin * inv).T], axis=1)
    t["decay"] = f(0.9) ** np.abs(np.arange(7 * P)[None, :] - (NT - 1) * P - np.arange(P)[:, None]).astype(f)
    t["ident"] = np.eye(P, dtype=f)
    t["ranks"] = np.concatenate([np.triu(np.ones((P, P), f), 1), np.ones((P, P), f)], axis=1)
    t["iota"] = np.tile(np.arange(P, dtype=f)[None, :], (P, 1))
    dh = 16
    freqs = np.exp(f(-np.log(10000.0)) * np.arange(0, dh, 2, dtype=f) / f(dh)).astype(f)
    ang = np.repeat(np.arange(L, dtype=f)[:, None] * freqs[None, :], 2, axis=1).astype(f)
    sign = np.where(np.arange(dh) % 2 == 0, f(-1), f(1)).astype(f)
    rope = np.stack([np.cos(ang), np.sin(ang) * sign], axis=1)
    rope = rope.astype(f)
    rope = np.stack([rope * f(0.25), rope], axis=1)
    t["rope1"] = rope.reshape(NT, P, 2, 2, dh).transpose(1, 0, 2, 3, 4)
    dh, window = 64, 128
    half = np.arange(0, dh, 2, dtype=f)
    invf = (f(1.0) / f(10000.0) ** (half / f(dh))).astype(f)
    fr = (np.arange(L, dtype=f)[:, None] * invf[None, :]).astype(f)
    fr = np.concatenate([fr, fr], axis=-1)
    base = ((half + f(0.4 * dh)) / f(1.4 * dh)).astype(f)
    power = ((np.arange(L, dtype=f) - f(L // 2)) / f(window // 2)).astype(f)
    sc = (base[None, :] ** power[:, None]).astype(f)
    sc = np.concatenate([sc, sc], axis=-1)
    sign = np.where(np.arange(dh) < dh // 2, f(-1), f(1)).astype(f)
    c, s_ = np.cos(fr), np.sin(fr) * sign
    w = np.stack([c * sc * f(8), s_ * sc * f(8), c / sc, s_ / sc], axis=1).astype(f)
    t["rope2"] = w.reshape(NT, P, 4, dh).transpose(1, 0, 2, 3)
    shift = np.zeros((P, 2, P), f)
    shift[np.arange(P - 1), 0, np.arange(1, P)] = 1
    shift[P - 1, 1, 0] = 1
    t["shift"] = shift
    a, cc = np.arange(P)[:, None], np.arange(P)[None, :]
    ban = np.stack([a > cc, cc > a], axis=1) * -1e30
    t["mask"] = np.concatenate([np.eye(P)[:, None, :], ban], axis=1).astype(f)
    return {k: np.ascontiguousarray(v) for k, v in t.items()}


def build(nc, g):
    with g.ctx:
        g.ident, g.shift = g.keep("ident", [P, P]), g.keep("shift", [P, 2, P])
        g.mask, g.minus_half = g.keep("mask", [P, 3, P], BF16), g.keep("minus_half", [P, 2 * H2])
        g.row_of, g.owner = g.keep("row_of", [P, TILES], I32), g.keep("owner", [P, MAXSLOT], I32)
        g.x1_d = nc.dram_tensor("x1_d", (B, L, D), F32).ap()
        g.x3_d = nc.dram_tensor("x3_d", (B, L, D), F32).ap()
        g.y_d = [nc.dram_tensor(f"y{i}_d", (B, L, D), F32).ap() for i in range(2)]
        g.xs_d = nc.dram_tensor("xs_d", (MAXSLOT * P, D), F32).ap()
        g.ys_d = nc.dram_tensor("ys_d", (SLOTS * P, D), F32).ap()
        tables_in = g.once("kept_in")
        g.w1_in, g.w2_in, g.pool_consts, g.zeros_out = (g.once(n) for n in ("w1_in", "w2_in", "pool_consts", "zeros_out"))
        with nc.sbuf_tensor("mask_f32", [P, 3, P], F32) as mask_f32, nc.Block() as block:
            @block.sync
            def _(sp):
                for dst, src in [(g.ident, g.ident_d), (g.shift, g.shift_d), (mask_f32, g.mask_d)]:
                    sp.dma_start(dst[:], src).then_inc(tables_in, 16)

            @block.vector
            def _(dve):
                dve.wait_ge(tables_in, 48)
                dve.tensor_copy(g.mask[:], mask_f32[:]).then_inc(tables_in, 1)
                dve.wait_ge(tables_in, 49)

        with ExitStack() as experts:
            def sb(name, shape, dt=F32):
                return experts.enter_context(nc.sbuf_tensor(name, shape, dt))

            g.w1, g.xn2 = sb("w1", [P, EXPERTS, DC, FF]), sb("xn2", [P, TILES, D])
            g.logits = sb("logits", [P, TILES, EXPERTS])
            with nc.sbuf_tensor("zrow", [P, EXPERTS * D], F32) as zrow:
                g.zrow = zrow
                phase_attn0(nc, g)
            g.w2, g.b1, g.b2 = sb("w2", [P, EXPERTS, FC, D]), sb("b1", [P, EXPERTS, FC]), sb("b2", [P, EXPERTS, D])
            phase_route(nc, g)
            phase_experts(nc, g)
        phase_attn1(nc, g)
        for layer in range(2):
            phase_layer(nc, g, layer)


def kernel(**inputs):
    import concourse.bacc as bacc
    from concourse.bass_utils import run_bass_kernel_spmd

    a = {k: np.asarray(v) for k, v in inputs.items()}
    tables = shape_tables()
    HIDDEN = a["L1_ffn_b1"].shape[1] // 2
    b1 = np.zeros((2, UC * P, 2), np.float32)
    b1[:, 0:HIDDEN] = a["L1_ffn_b1"].reshape(2, 2, HIDDEN).transpose(0, 2, 1)
    laid_out = {
        "X": a["L0_attn_X"], "W_Q": a["L0_attn_W_Q"], "W_K": a["L0_attn_W_K"], "W_V": a["L0_attn_W_V"],
        "WrT": a["L0_ffn_Wr"].T, "br": a["L0_ffn_br"],
        "W1T": a["L0_ffn_W1"].transpose(0, 2, 1), "W2T": a["L0_ffn_W2"].transpose(0, 2, 1),
        "b1T": a["L0_ffn_b1"].reshape(EXPERTS, FC, P).transpose(2, 0, 1), "b2d": a["L0_ffn_b2"],
        "Wqkv1T": a["L1_attn_Wqkv"].T, "Wo1T": a["L1_attn_Wo"].T,
        "wqkv": a["L1_ffn_wqkv"], "wo": a["L1_ffn_wo"], "w1d": a["L1_ffn_w1"], "w2d": a["L1_ffn_w2"],
        "b1l": b1.reshape(2, UC, P, 2).transpose(0, 2, 3, 1), "b2l": a["L1_ffn_b2"],
        "qs": a["L1_ffn_q_scale"], "ks": a["L1_ffn_k_scale"],
        "lng": a["L1_ffn_ln_g"].reshape(2, DC, P).transpose(0, 2, 1), "lnb": a["L1_ffn_ln_b"].reshape(2, DC, P).transpose(0, 2, 1),
        "xpos0": tables["xpos0"], "decay": tables["decay"], "ranks": tables["ranks"], "iota": tables["iota"],
        "rope1": tables["rope1"], "rope2": tables["rope2"],
        "ident_d": tables["ident"], "shift_d": tables["shift"], "mask_d": tables["mask"],
    }
    nc = bacc.Bacc("TRN2", target_bir_lowering=False, num_devices=1)
    g = Shared(nc, ExitStack())
    arrays = {}
    views = {}
    for name, value in laid_out.items():
        value = np.ascontiguousarray(value)
        arrays[f"in_{name}"] = value
        views[name] = nc.dram_tensor(f"in_{name}", value.shape, mybir.dt.from_np(value.dtype), kind="ExternalInput").ap()
    g.take(views)
    g.out = nc.dram_tensor("out", (B, L, D), F32, kind="ExternalOutput").ap()
    build(nc, g)
    result = run_bass_kernel_spmd(nc, [arrays], core_ids=[0])
    return result.results[0]["out"]
```

```python
from contextlib import ExitStack

import numpy as np
import concourse.bass as bass
from concourse import mybir

F32 = mybir.dt.float32
F32R = mybir.dt.float32r
BF16 = mybir.dt.bfloat16
I32 = mybir.dt.int32
U32 = mybir.dt.uint32
ALU = mybir.AluOpType
ACT = mybir.ActivationFunctionType
AX = mybir.AxisListType.X

P = 128
B, L, D = 8, 512, 256
NT = L // P
DC = D // P
NS = 2
PAIRS = B // NS
TOK = B * L
TILES = TOK // P
EXPERTS, FF = 8, 1024
FC = FF // P
SLOTS = TILES + EXPERTS - 1
MAXSLOT = SLOTS + 1
ZEROED = 5
EPS = 1e-5
LOOP_SEMS = 150


class Chain:

    def __init__(self, eng, sem):
        self.eng, self.sem, self.n = eng, sem, 0

    def mark(self, ins):
        self.n += 1
        ins.then_inc(self.sem, 1)
        return self.n

    def step(self, ins):
        self.eng.wait_ge(self.sem, self.mark(ins))

    def wait(self, n):
        self.eng.wait_ge(self.sem, n)


def row_stats(dve, chain, var_ready, parts, stats, mv, ve):
    for t in range(NT):
        for i, src in enumerate(parts(t)):
            last = chain.mark(dve.bn_stats(stats[:, t, 6 * i:6 * i + 6], src))
    chain.wait(last)
    n = len(parts(0))
    for t in range(NT):
        last = chain.mark(dve.bn_aggr(mv[:, t, :], stats[:, t, 0:6 * n]))
    chain.wait(last)
    dve.tensor_scalar(ve[:, :], mv[:, :, 1], EPS, None, ALU.add).then_inc(var_ready, 1)


def normalised_rows(dve, rstd_ready, k, parts, mv, rstd, out):
    dve.wait_ge(rstd_ready, k)
    for t in range(NT):
        for src, dst in zip(parts(t), out(t)):
            yield dve.tensor_scalar(dst, src, mv[:, t, 0:1], rstd[:, t:t + 1], ALU.subtract, ALU.mult)


def phase_attn0(nc, g):
    with ExitStack() as ctx:
        def sb(name, shape, dt=F32):
            return ctx.enter_context(nc.sbuf_tensor(f"a_{name}", shape, dt))

        def stream(name, shape, dt=F32):
            return [sb(f"{name}{s}", shape, dt) for s in range(NS)]

        sems = []

        def sem(name):
            sems.append(ctx.enter_context(nc.semaphore(f"a_{name}", num=LOOP_SEMS + len(sems))))
            return sems[-1]

        def sem2(name):
            return [sem(f"{name}{s}") for s in range(NS)]

        wq = sb("wq", [P, DC, D])
        wk = sb("wk", [P, DC, D])
        wv = sb("wv", [P, DC, D])
        wr = sb("wr", [P, DC, EXPERTS])
        br = sb("br", [P, EXPERTS])
        xpos = sb("xpos", [P, 4, L])
        decay = sb("decay", [P, 7 * P])
        x, xn = stream("x", [P, NT, D]), stream("xn", [P, NT, D])
        xnT = stream("xnT", [P, DC, L])
        qT, kT = stream("qT", [P, DC, L]), stream("kT", [P, DC, L])
        v = stream("v", [P, NT, D])
        prods = stream("prods", [P, 4, L])
        probs = stream("probs", [P, L])
        probsT = stream("probsT", [P, NT, P])
        stats, mv = stream("stats", [P, NT, 6]), stream("mv", [P, NT, 2])
        ve, rstd = stream("ve", [P, NT]), stream("rstd", [P, NT])
        nmax, rsum, rinv = stream("nmax", [P, NT]), stream("rsum", [P, NT]), stream("rinv", [P, NT])
        bank = [[ctx.enter_context(nc.psum_tensor(f"bank{s}{i}", [P, L], F32)) for i in range(4)]
                for s in range(NS)]

        consts_in = g.once("consts_in")
        x_in = sem2("x_in")
        dve_chain, var_ready, rstd_ready = sem("dve_chain"), sem2("var_ready"), sem2("rstd_ready")
        xn_ready, xnT_psum, xnT_ready = sem2("xn_ready"), sem2("xnT_psum"), sem2("xnT_ready")
        qk_psum, qk_mults, qk_ready = sem2("qk_psum"), sem2("qk_mults"), sem2("qk_ready")
        v_psum, v_ready = sem2("v_psum"), sem2("v_ready")
        scores_ready, nmax_ready, probs_ready = sem2("scores_ready"), sem2("nmax_ready"), sem2("probs_ready")
        probsT_psum, probsT_ready = sem2("probsT_psum"), sem2("probsT_ready")
        o_psum, x1_ready = sem2("o_psum"), sem2("x1_ready")
        logits_psum, logits_read, kept, stored = sem2("logits_psum"), sem2("logits_read"), sem2("kept"), sem2("stored")
        sem_range = range(sems[0].num, sems[-1].num + 1)
        assert len(sem_range) == len(sems)

        CONSTS = [(wq, g.W_Q.rearrange("(c p) n -> p c n", p=P)), (wk, g.W_K.rearrange("(c p) n -> p c n", p=P)),
                  (wv, g.W_V.rearrange("(c p) n -> p c n", p=P)), (wr, g.WrT.rearrange("(c p) n -> p c n", p=P)),
                  (br, g.br.partition_broadcast(P)), (xpos, g.xpos0), (decay, g.decay)]

        with nc.Block() as block:
            @block.scalar
            def _(act):
                for dst, src in CONSTS:
                    act.dma_start(dst[:], src).then_inc(consts_in, 16)

            @block.gpsimd
            def _(pool):
                pool.memset(g.minus_half[:], -0.5).then_inc(g.pool_consts, 1)
                pool.memset(g.zrow[:], 0.0).then_inc(g.pool_consts, 1)
                pool.wait_ge(g.pool_consts, 2)

        with nc.Fori(0, PAIRS) as pair:
            with nc.Block() as block:
                @block.sync
                def _(sp):
                    for s in range(NS):
                        sp.dma_start(x[s][:], g.X[pair * NS + s].rearrange("(t p) n -> p t n", p=P)).then_inc(x_in[s], 16)
                    sp.wait_ge(qk_psum[0], 1)
                    for i in range(NS):
                        sp.dma_start(g.w1[:, bass.ds(pair * NS + i, 1)],
                                     g.W1T[bass.ds(pair * NS + i, 1)].rearrange("e (c p) f -> p e c f", p=P)).then_inc(g.w1_in, 16)
                    for i in range(MAXSLOT // PAIRS // ZEROED):
                        first = pair * (MAXSLOT // PAIRS * P) + i * ZEROED * P
                        sp.dma_start(g.xs_d[bass.ds(first, ZEROED * P), :].rearrange("(p a) n -> p (a n)", p=P), g.zrow[:]).then_inc(g.zeros_out, 16)
                    for s in range(NS):
                        sp.wait_ge(x1_ready[s], NT)
                        sp.dma_start(g.x1_d[pair * NS + s].rearrange("(t p) n -> p t n", p=P), x[s][:]).then_inc(stored[s], 16)
                    for s in range(NS):
                        sp.wait_ge(stored[s], 16)

                @block.vector
                def _(dve):
                    chain = Chain(dve, dve_chain)

                    def measure(s):
                        row_stats(dve, chain, var_ready[s], lambda t: [x[s][:, t, :]], stats[s], mv[s], ve[s])

                    def norm(s, k):
                        for ins in normalised_rows(dve, rstd_ready[s], k, lambda t: [x[s][:, t, :]], mv[s], rstd[s],
                                                   lambda t: [xn[s][:, t, :]]):
                            ins.then_inc(xn_ready[s], 1)

                    def rotate(s):
                        for i in range(2):
                            dve.wait_ge(qk_psum[s], i + 1)
                            even, odd = bank[s][2 * i], bank[s][2 * i + 1]
                            cos, sin = xpos[:, 2 * i, :], xpos[:, 2 * i + 1, :]
                            if i == 1:
                                dve.wait_ge(qk_ready[s], 2)
                            for j, (a, b) in enumerate([(even, cos), (odd, sin), (odd, cos), (even, sin)]):
                                dve.tensor_tensor(prods[s][:, j, :], a[:], b, ALU.mult).then_inc(qk_mults[s], 1)

                    def row_max(s, qt):
                        dve.wait_ge(scores_ready[s], qt + 1)
                        dve.tensor_reduce(nmax[s][:, qt:qt + 1], bank[s][qt % 2][:], AX, ALU.max, negate=True)\
                           .then_inc(nmax_ready[s], 1)

                    def decayed(s, qt):
                        dve.wait_ge(probsT_psum[s], qt + 1)
                        if qt:
                            dve.wait_ge(o_psum[s], qt)
                        dve.tensor_tensor(probsT[s][:].rearrange("p a b -> p (a b)"), bank[s][2][:],
                                          decay[:, qt * P:qt * P + L], ALU.mult).then_inc(probsT_ready[s], 1)

                    def residual(s, qt):
                        chain.step(dve.reciprocal(rinv[s][:, qt:qt + 1], rsum[s][:, qt:qt + 1]))
                        dve.wait_ge(o_psum[s], qt + 1)
                        dve.scalar_tensor_tensor(x[s][:, qt, :], bank[s][3][:, 0:D], rinv[s][:, qt:qt + 1],
                                                 x[s][:, qt, :], ALU.mult, ALU.add).then_inc(x1_ready[s], 1)

                    for s in range(NS):
                        dve.wait_ge(x_in[s], 16)
                        measure(s)
                    for s in range(NS):
                        norm(s, 1)
                    dve.wait_ge(consts_in, 16 * len(CONSTS))
                    for s in range(NS):
                        rotate(s)
                    for qt in range(NT + 1):
                        for s in range(NS):
                            if qt < NT:
                                row_max(s, qt)
                            if qt:
                                decayed(s, qt - 1)
                        for s in range(NS):
                            if qt:
                                residual(s, qt - 1)
                    for s in range(NS):
                        dve.wait_ge(x1_ready[s], NT)
                        measure(s)
                    for s in range(NS):
                        norm(s, 2)
                    for s in range(NS):
                        dve.wait_ge(xn_ready[s], 2 * NT)
                        dve.tensor_copy(g.xn2[:, bass.ds(pair * (NS * NT) + s * NT, NT), :], xn[s][:]).then_inc(kept[s], 1)
                    for s in range(NS):
                        dve.wait_ge(logits_psum[s], 1)
                        dve.tensor_tensor(g.logits[:, bass.ds(pair * (NS * NT) + s * NT, NT), :],
                                          bank[s][2][:, 0:NT * EXPERTS].rearrange("p (t e) -> p t e", e=EXPERTS),
                                          br[:].unsqueeze(1).to_broadcast([P, NT, EXPERTS]), ALU.add).then_inc(logits_read[s], 1)

                @block.gpsimd
                def _(pool):
                    def power(s, k):
                        pool.wait_ge(var_ready[s], k)
                        pool.tensor_tensor(rstd[s][:], ve[s][:], g.minus_half[:, 0:NT], ALU.pow).then_inc(rstd_ready[s], 1)

                    for s in range(NS):
                        power(s, 1)
                    for s in range(NS):
                        for i, dst in enumerate([qT, kT]):
                            for j, op in enumerate([ALU.subtract, ALU.add]):
                                pool.wait_ge(qk_mults[s], 4 * i + 2 * j + 2)
                                pool.tensor_tensor(dst[s][:, j, :], prods[s][:, 2 * j, :], prods[s][:, 2 * j + 1, :], op)\
                                    .then_inc(qk_ready[s], 1)
                    for s in range(NS):
                        power(s, 2)

                @block.scalar
                def _(act):
                    def xnT_out(s, k):
                        for c in range(DC):
                            act.wait_ge(xnT_psum[s], 2 * k + c + 1)
                            act.activation(xnT[s][:, c, :], bank[s][c][:], ACT.Copy).then_inc(xnT_ready[s], 1)

                    for s in range(NS):
                        xnT_out(s, 0)
                    for s in range(NS):
                        for h in range(2):
                            act.wait_ge(v_psum[s], h + 1)
                            act.activation(v[s][:, 2 * h:2 * h + 2, :].rearrange("p a b -> p (a b)"), bank[s][h][:], ACT.Copy)\
                               .then_inc(v_ready[s], 1)
                    for qt in range(NT):
                        for s in range(NS):
                            act.wait_ge(nmax_ready[s], qt + 1)
                            if qt:
                                act.wait_ge(probsT_psum[s], qt)
                            act.activation(probs[s][:], bank[s][qt % 2][:], ACT.Exp, bias=nmax[s][:, qt:qt + 1],
                                           accum_out=rsum[s][:, qt:qt + 1]).then_inc(probs_ready[s], 1)
                    for s in range(NS):
                        xnT_out(s, 1)

                @block.tensor
                def _(pe):
                    def transposes(s, k):
                        for c in range(DC):
                            for t in range(NT):
                                if c == 0:
                                    pe.wait_ge(xn_ready[s], k * NT + t + 1)
                                last = pe.transpose(bank[s][c][:, t * P:(t + 1) * P], xn[s][:, t, c * P:(c + 1) * P], g.ident[:])
                            last.then_inc(xnT_psum[s], 1)

                    def project(s):
                        pe.wait_ge(xnT_ready[s], DC)
                        for i, w in enumerate([wq, wk]):
                            wp = w[:].rearrange("p c (n two) -> p c two n", two=2)
                            for j in range(2):
                                for c in range(DC):
                                    last = pe.matmul(bank[s][2 * i + j][:], wp[:, c, j, :], xnT[s][:, c, :],
                                                     start=c == 0, stop=c == DC - 1)
                            last.then_inc(qk_psum[s], 1)

                    def values(s):
                        pe.wait_ge(qk_mults[s], 4)
                        for t in range(NT):
                            for c in range(DC):
                                last = pe.matmul(bank[s][t // 2][:, (t % 2) * D:(t % 2 + 1) * D], xnT[s][:, c, t * P:(t + 1) * P],
                                                 wv[:, c, :], start=c == 0, stop=c == DC - 1)
                            if t % 2:
                                last.then_inc(v_psum[s], 1)

                    def scores(s, qt):
                        if qt == 0:
                            pe.wait_ge(qk_ready[s], 4)
                            pe.wait_ge(v_ready[s], 2)
                        if qt >= 2:
                            pe.wait_ge(probs_ready[s], qt - 1)
                        for c in range(DC):
                            last = pe.matmul(bank[s][qt % 2][:], qT[s][:, c, qt * P:(qt + 1) * P], kT[s][:, c, :],
                                             start=c == 0, stop=c == DC - 1)
                        last.then_inc(scores_ready[s], 1)

                    def flip(s, qt):
                        pe.wait_ge(probs_ready[s], qt + 1)
                        if qt:
                            pe.wait_ge(probsT_ready[s], qt)
                        for kt in range(NT):
                            last = pe.transpose(bank[s][2][:, (NT - 1 - kt) * P:(NT - kt) * P],
                                                probs[s][:, kt * P:(kt + 1) * P], g.ident[:])
                        last.then_inc(probsT_psum[s], 1)

                    def output(s, qt):
                        pe.wait_ge(probsT_ready[s], qt + 1)
                        if qt:
                            pe.wait_ge(x1_ready[s], qt)
                        for kt in range(NT):
                            last = pe.matmul(bank[s][3][:, 0:D], probsT[s][:, NT - 1 - kt, :], v[s][:, kt, :],
                                             start=kt == 0, stop=kt == NT - 1)
                        last.then_inc(o_psum[s], 1)

                    for s in range(NS):
                        transposes(s, 0)
                    pe.wait_ge(consts_in, 16 * len(CONSTS))
                    for s in range(NS):
                        project(s)
                    for s in range(NS):
                        values(s)
                    for qt in range(NT + 1):
                        for s in range(NS):
                            if qt < NT:
                                scores(s, qt)
                            if qt:
                                flip(s, qt - 1)
                        for s in range(NS):
                            if qt:
                                output(s, qt - 1)
                    for s in range(NS):
                        transposes(s, 1)
                    for s in range(NS):
                        pe.wait_ge(xnT_ready[s], 2 * DC)
                        for t in range(NT):
                            for c in range(DC):
                                last = pe.matmul(bank[s][2][:, t * EXPERTS:(t + 1) * EXPERTS], xnT[s][:, c, t * P:(t + 1) * P],
                                                 wr[:, c, :], start=c == 0, stop=c == DC - 1)
                        last.then_inc(logits_psum[s], 1)
            nc.all_engine_barrier(sems_to_clear=sem_range)


class Shared:

    def __init__(self, nc, ctx):
        self.nc, self.ctx = nc, ctx

    def take(self, v):
        self.X, self.W_Q, self.W_K, self.W_V, self.WrT, self.br = v["X"], v["W_Q"], v["W_K"], v["W_V"], v["WrT"], v["br"]
        self.W1T, self.W2T, self.b1T, self.b2d = v["W1T"], v["W2T"], v["b1T"], v["b2d"]
        self.Wqkv1T, self.Wo1T = v["Wqkv1T"], v["Wo1T"]
        self.wqkv, self.wo, self.w1d, self.w2d = v["wqkv"], v["wo"], v["w1d"], v["w2d"]
        self.b1l, self.b2l, self.qs, self.ks, self.lng, self.lnb = v["b1l"], v["b2l"], v["qs"], v["ks"], v["lng"], v["lnb"]
        self.xpos0, self.decay, self.ranks, self.iota = v["xpos0"], v["decay"], v["ranks"], v["iota"]
        self.rope1, self.rope2 = v["rope1"], v["rope2"]
        self.ident_d, self.shift_d, self.mask_d = v["ident_d"], v["shift_d"], v["mask_d"]

    def once(self, name):
        return self.ctx.enter_context(self.nc.semaphore(name))

    def keep(self, name, shape, dt=F32):
        return self.ctx.enter_context(self.nc.sbuf_tensor(name, shape, dt))


SLOT_LOOPS = 3
PER_LOOP = SLOTS // SLOT_LOOPS
assert PER_LOOP * SLOT_LOOPS == SLOTS


def phase_route(nc, g):
    TE = TILES * EXPERTS
    with ExitStack() as ctx:
        def sb(name, shape, dt=F32):
            return ctx.enter_context(nc.sbuf_tensor(f"m_{name}", shape, dt))

        ranks, iota = sb("ranks", [P, 2 * P]), sb("iota", [P, P])
        best, score = sb("best", [P, TILES]), sb("score", [P, TILES, EXPERTS])
        onehot = sb("onehot", [P, TILES, EXPERTS])
        order = sb("order", [P, EXPERTS])
        totals, upto = sb("totals", [P, EXPERTS, TILES]), sb("upto", [P, EXPERTS, TILES])
        ones, starts = sb("ones", [P, TILES]), sb("starts", [P, TILES])
        passed = sb("passed", [P, EXPERTS, TILES])
        slots_of, ends, base = sb("slots_of", [P, EXPERTS]), sb("ends", [P, EXPERTS]), sb("base", [P, EXPERTS])
        over, owner = sb("over", [P, MAXSLOT, EXPERTS]), sb("owner", [P, MAXSLOT])
        rows, row = sb("rows", [P, TILES, EXPERTS]), sb("row", [P, TILES])
        rank_psum = ctx.enter_context(nc.psum_tensor("rank_psum", [P, TE], F32))
        total_psum = ctx.enter_context(nc.psum_tensor("total_psum", [P, TE], F32))
        tables_in, dve_chain = g.once("tables_in"), g.once("rt_chain")
        onehot_ready, counted = g.once("onehot_ready"), g.once("counted")
        rows_ready, scattered = g.once("rows_ready"), g.once("scattered")

        with nc.Block() as block:
            @block.sync
            def _(sp):
                sp.dma_start(ranks[:], g.ranks).then_inc(tables_in, 16)
                sp.dma_start(iota[:], g.iota).then_inc(tables_in, 16)
                sp.dma_start(g.b1[:], g.b1T).then_inc(g.w1_in, 16)
                for e in range(EXPERTS):
                    sp.dma_start(g.w2[:, e], g.W2T[e].rearrange("(c p) n -> p c n", p=P)).then_inc(g.w2_in, 16)
                sp.dma_start(g.b2[:], g.b2d.partition_broadcast(P)).then_inc(g.w2_in, 16)

            @block.tensor
            def _(pe):
                pe.wait_ge(tables_in, 32)
                pe.wait_ge(onehot_ready, 1)
                oh = onehot[:].rearrange("p t e -> p (t e)")
                pe.matmul(rank_psum[:], ranks[:, 0:P], oh, start=True, stop=True)
                pe.matmul(total_psum[:], ranks[:, P:2 * P], oh, start=True, stop=True).then_inc(counted, 1)

            @block.vector
            def _(dve):
                chain = Chain(dve, dve_chain)
                step = chain.step

                def over_experts(a):
                    return a.unsqueeze(2).to_broadcast([P, a.shape[1], EXPERTS])

                dve.wait_ge(tables_in, 32)
                step(dve.memset(ones[:], 1.0))
                step(dve.tensor_reduce(best[:], g.logits[:], AX, ALU.max))
                step(dve.tensor_tensor(onehot[:], g.logits[:], over_experts(best[:]), ALU.is_equal))
                step(dve.tensor_scalar(order[:], iota[:, 0:EXPERTS], -1.0, float(EXPERTS), ALU.mult, ALU.add))
                step(dve.tensor_tensor(score[:], onehot[:], order[:].unsqueeze(1).to_broadcast([P, TILES, EXPERTS]), ALU.mult))
                step(dve.tensor_reduce(best[:], score[:], AX, ALU.max))
                dve.tensor_tensor(onehot[:], score[:], over_experts(best[:]), ALU.is_equal).then_inc(onehot_ready, 1)
                dve.wait_ge(counted, 1)
                step(dve.tensor_copy(totals[:], total_psum[:].rearrange("p (t e) -> p e t", e=EXPERTS)))
                for e in range(EXPERTS):
                    last = chain.mark(dve.tensor_tensor_scan(upto[:, e, :], ones[:], totals[:, e, :], 0.0, ALU.mult, ALU.add))
                chain.wait(last)
                step(dve.tensor_scalar(starts[:], iota[:, 0:TILES], float(P), None, ALU.mult))
                step(dve.tensor_tensor(passed[:], upto[:, :, TILES - 1:TILES].to_broadcast([P, EXPERTS, TILES]),
                                       starts[:].unsqueeze(1).to_broadcast([P, EXPERTS, TILES]), ALU.is_gt))
                step(dve.tensor_reduce(slots_of[:], passed[:], AX, ALU.add))
                step(dve.tensor_tensor_scan(ends[:], ones[:, 0:EXPERTS], slots_of[:], 0.0, ALU.mult, ALU.add))
                step(dve.tensor_tensor(base[:], ends[:], slots_of[:], ALU.subtract))
                step(dve.tensor_scalar(base[:], base[:], float(P), None, ALU.mult))
                step(dve.tensor_tensor(over[:], ends[:].unsqueeze(1).to_broadcast([P, MAXSLOT, EXPERTS]),
                                       iota[:, 0:MAXSLOT].unsqueeze(2).to_broadcast([P, MAXSLOT, EXPERTS]), ALU.is_le))
                step(dve.tensor_reduce(owner[:], over[:], AX, ALU.add))
                step(dve.tensor_scalar(g.owner[:], owner[:], float(EXPERTS - 1), None, ALU.min))
                step(dve.tensor_tensor(passed[:], upto[:], totals[:], ALU.subtract))
                step(dve.tensor_tensor(rows[:], rank_psum[:].rearrange("p (t e) -> p t e", e=EXPERTS),
                                       passed[:].rearrange("p e t -> p t e"), ALU.add))
                step(dve.tensor_tensor(rows[:], rows[:], base[:].unsqueeze(1).to_broadcast([P, TILES, EXPERTS]), ALU.add))
                step(dve.tensor_tensor(rows[:], rows[:], onehot[:], ALU.mult))
                step(dve.tensor_reduce(row[:], rows[:], AX, ALU.add))
                dve.tensor_copy(g.row_of[:], row[:]).then_inc(rows_ready, 1)

            @block.gpsimd
            def _(pool):
                pool.wait_ge(rows_ready, 1)
                pool.wait_ge(g.zeros_out, 16 * (MAXSLOT // ZEROED))
                for t in range(TILES):
                    pool.indirect_dma_start(g.xs_d, bass.IndirectOffsetOnAxis(ap=g.row_of[:, t:t + 1], axis=0),
                                            g.xn2[:, t, :], None).then_inc(scattered, 16)
                pool.wait_ge(scattered, 16 * TILES)


def phase_experts(nc, g):
    with ExitStack() as ctx:
        def sb(name, shape, dt=F32):
            return ctx.enter_context(nc.sbuf_tensor(f"m_{name}", shape, dt))

        sems = []

        def sem(name):
            sems.append(ctx.enter_context(nc.semaphore(f"m_{name}", num=LOOP_SEMS + len(sems))))
            return sems[-1]

        XB = 3
        xs = sb("xs", [P, XB, D])
        xsT = sb("xsT", [P, 2, DC, P])
        hT = sb("hT", [P, 2, FC, P])
        y = sb("y", [P, 2, D])
        b1s = sb("b1s", [P, 2, FC])
        W = DC * FF
        staged = g.xn2[:].rearrange("p t n -> p (t n)").rearrange("p (k w n) -> p k w n", k=2, w=2)
        w1s = [staged[:, k, 0].rearrange("p (c f) -> p c f", c=DC) for k in range(2)]
        w2s = [staged[:, k, 1].rearrange("p (c n) -> p c n", c=FC) for k in range(2)]
        xT_bank = [ctx.enter_context(nc.psum_tensor(f"xT_bank{i}", [P, 512], F32)) for i in range(2)]
        h_bank = [ctx.enter_context(nc.psum_tensor(f"h_bank{i}", [P, 4, P], F32)) for i in range(4)]
        y_bank = [ctx.enter_context(nc.psum_tensor(f"y_bank{i}", [P, 512], F32)) for i in range(2)]

        x_in = [sem(f"xs_in{i}") for i in range(XB)]
        xT_psum, xT_ready, w1_staged, w2_staged = sem("xT_psum"), sem("xT_ready"), sem("w1_staged"), sem("w2_staged")
        h_psum, h_ready, y_psum, y_ready = sem("h_psum"), sem("h_ready"), sem("y_psum"), sem("y_ready")
        y_out = [sem(f"y_out{i}") for i in range(2)]
        sem_range = range(sems[0].num, sems[-1].num + 1)
        N = PER_LOOP

        with nc.Fori(0, SLOT_LOOPS) as loop:
            with nc.Block() as block:
                @block.sync
                def _(sp):
                    def store(j):
                        sp.wait_ge(y_ready, j + 1)
                        sp.dma_start(g.ys_d[bass.ds((loop * N + j) * P, P), :], y[:, j % 2, :]).then_inc(y_out[j % 2], 16)

                    for j in range(N):
                        if j >= XB:
                            sp.wait_ge(xT_psum, j - XB + 1)
                        sp.dma_start(xs[:, j % XB, :], g.xs_d[bass.ds((loop * N + j) * P, P), :]).then_inc(x_in[j % XB], 16)
                        if j >= XB:
                            store(j - XB)
                    for j in range(N - XB, N):
                        store(j)
                    for k in range(2):
                        sp.wait_ge(y_out[k], 16 * ((N - k + 1) // 2))

                @block.vector
                def _(dve):
                    owner = [None] * 3

                    def stage_w1(j):
                        k = j % 2
                        owner[j % 3] = dve.value_load(g.owner[0:1, bass.ds(loop * N + j, 1)], min_val=0, max_val=EXPERTS - 1)
                        e = bass.ds(owner[j % 3], 1)
                        if j >= 2:
                            dve.wait_ge(h_ready, 2 * (j - 1))
                        dve.tensor_copy(b1s[:, k, :].unsqueeze(1), g.b1[:, e, :]).then_inc(w1_staged, 1)
                        dve.tensor_copy(w1s[k].unsqueeze(1), g.w1[:, e]).then_inc(w1_staged, 1)

                    def stage_w2(j):
                        if j >= 2:
                            dve.wait_ge(y_psum, j - 1)
                        dve.tensor_copy(w2s[j % 2].unsqueeze(1), g.w2[:, bass.ds(owner[j % 3], 1)]).then_inc(w2_staged, 1)

                    def finish(j):
                        dve.wait_ge(y_psum, j + 1)
                        if j >= 2:
                            dve.wait_ge(y_out[j % 2], 16 * (j // 2))
                        dve.tensor_tensor(y[:, j % 2, :].unsqueeze(1), y_bank[j % 2][:, 0:D].unsqueeze(1),
                                          g.b2[:, bass.ds(owner[j % 3], 1), :], ALU.add).then_inc(y_ready, 1)

                    dve.wait_ge(g.w1_in, 16 * (EXPERTS + 1))
                    stage_w1(0)
                    dve.wait_ge(g.w2_in, 16 * (EXPERTS + 1))
                    stage_w2(0)
                    stage_w1(1)
                    stage_w2(1)
                    for j in range(2, N):
                        stage_w1(j)
                        finish(j - 2)
                        stage_w2(j)
                    finish(N - 2)
                    finish(N - 1)

                @block.scalar
                def _(act):
                    def xT_out(j):
                        act.wait_ge(xT_psum, j + 1)
                        if j >= 2:
                            act.wait_ge(h_psum, 2 * (j - 1))
                        act.activation(xsT[:, j % 2].rearrange("p c n -> p (c n)"), xT_bank[j % 2][:, 0:DC * P], ACT.Copy)\
                           .then_inc(xT_ready, 1)

                    xT_out(0)
                    for j in range(N):
                        if j + 1 < N:
                            xT_out(j + 1)
                        act.wait_ge(w1_staged, 2 * (j + 1))
                        if j >= 2:
                            act.wait_ge(y_psum, j - 1)
                        for h in range(2):
                            act.wait_ge(h_psum, 2 * j + h + 1)
                            for f in range(4):
                                last = act.activation(hT[:, j % 2, 4 * h + f, :], h_bank[2 * (j % 2) + h][:, f, :], ACT.Relu,
                                                      bias=b1s[:, j % 2, 4 * h + f:4 * h + f + 1])
                            last.then_inc(h_ready, 1)

                @block.tensor
                def _(pe):
                    def flip(j):
                        pe.wait_ge(x_in[j % XB], 16 * (j // XB + 1))
                        if j >= 2:
                            pe.wait_ge(xT_ready, j - 1)
                        for c in range(DC):
                            last = pe.transpose(xT_bank[j % 2][:, c * P:(c + 1) * P], xs[:, j % XB, c * P:(c + 1) * P], g.ident[:])
                        last.then_inc(xT_psum, 1)

                    def up(j):
                        pe.wait_ge(xT_ready, j + 1)
                        pe.wait_ge(w1_staged, 2 * (j + 1))
                        if j >= 2:
                            pe.wait_ge(h_ready, 2 * (j - 1))
                        for h in range(2):
                            for f in range(4):
                                for c in range(DC):
                                    last = pe.matmul(h_bank[2 * (j % 2) + h][:, f, :], w1s[j % 2][:, c, (4 * h + f) * P:(4 * h + f + 1) * P],
                                                     xsT[:, j % 2, c, :], start=c == 0, stop=c == DC - 1)
                            last.then_inc(h_psum, 1)

                    def down(j):
                        pe.wait_ge(h_ready, 2 * (j + 1))
                        pe.wait_ge(w2_staged, j + 1)
                        if j >= 2:
                            pe.wait_ge(y_ready, j - 1)
                        for f in range(FC):
                            last = pe.matmul(y_bank[j % 2][:, 0:D], hT[:, j % 2, f, :], w2s[j % 2][:, f, :], start=f == 0, stop=f == FC - 1)
                        last.then_inc(y_psum, 1)

                    flip(0)
                    for j in range(N + 1):
                        if j + 1 < N:
                            flip(j + 1)
                        if j < N:
                            up(j)
                        if j:
                            down(j - 1)
            nc.all_engine_barrier(sems_to_clear=sem_range)


H1, DH1 = 16, 16
HG = 4
GROUPS = H1 // HG
HP = H1 // 2


def phase_attn1(nc, g):
    with ExitStack() as ctx:
        def sb(name, shape, dt=F32):
            return ctx.enter_context(nc.sbuf_tensor(f"c_{name}", shape, dt))

        def stream(name, shape, dt=F32):
            return [sb(f"{name}{s}", shape, dt) for s in range(NS)]

        sems = []

        def sem(name):
            sems.append(ctx.enter_context(nc.semaphore(f"c_{name}", num=LOOP_SEMS + len(sems))))
            return sems[-1]

        def sem2(name):
            return [sem(f"{name}{s}") for s in range(NS)]

        QK = 2 * D
        w = sb("wqkv1", [P, DC, 3 * D])
        wo = sb("wo1", [P, DC, D])
        rope = sb("rope1", [P, NT, 2, 2, DH1])
        x, xn = stream("cx", [P, NT, D]), stream("cxn", [P, NT, D])
        yrow = stream("yrow", [P, NT, D])
        rowb = stream("rowb", [P, NT], I32)
        xnT = stream("cxnT", [P, DC, L])
        cosed, sined = stream("cosed", [P, QK]), stream("sined", [P, QK])
        qhl = stream("qhl", [P, H1, 4, DH1], F32R)
        khl = stream("khl", [P, H1, 4, DH1], F32R)
        qT, kT = stream("cqT", [P, HP, L], F32R), stream("ckT", [P, HP, L], F32R)
        v = stream("cv", [P, NT, H1, 2 * DH1])
        probs, probsT = stream("cprobs", [P, 2, L]), stream("cprobsT", [P, 2, NT, P])
        raw = stream("raw", [P, NT, GROUPS, P])
        o, oT = yrow, xnT
        stats, mv = stream("cstats", [P, NT, 6]), stream("cmv", [P, NT, 2])
        ve, rstd = stream("cve", [P, NT]), stream("crstd", [P, NT])
        nmax, rsum, rinv = (stream(n, [P, NT, H1]) for n in ("cnmax", "crsum", "crinv"))
        identr = sb("identr", [P, P], F32R)
        bank = [[ctx.enter_context(nc.psum_tensor(f"cbank{s}{i}", [P, L], F32)) for i in range(4)]
                for s in range(NS)]

        c_in, c_set = g.once("c_in"), g.once("c_set")
        y_in = [g.once(f"rows_in{s}") for s in range(NS)]
        x_in, row_copied = sem2("cx_in"), sem2("row_copied")
        x2_ready, dve_chain, var_ready, rstd_ready = sem2("x2_ready"), sem("c_chain"), sem2("cvar"), sem2("crstd")
        xn_ready, xnT_psum, xnT_ready = sem2("cxn_ready"), sem2("cxnT_psum"), sem2("cxnT_ready")
        qk_psum, v_psum, v_ready = sem2("cqk_psum"), sem2("cv_psum"), sem2("cv_ready")
        turned, rotated, split = sem2("turned"), sem2("rotated"), sem2("split")
        qkT_psum, qkT_ready = sem2("qkT_psum"), sem2("qkT_ready")
        scores_ready, nmax_ready, probs_ready = sem2("cscores"), sem2("cnmax_r"), sem2("cprobs_r")
        pT_psum, pT_ready, pv_done, o_ready = sem2("pT_psum"), sem2("pT_ready"), sem2("pv_done"), sem2("o_ready")
        oT_psum, oT_ready, raw_ready, raw_psum = sem2("oT_psum"), sem2("oT_ready"), sem2("raw_ready"), sem2("raw_psum")
        wo_psum, x3_ready, stored = sem2("wo_psum"), sem2("x3_ready"), sem2("cstored")
        sem_range = range(sems[0].num, sems[-1].num + 1)
        assert len(sem_range) == len(sems)

        def kw(qt):
            return max(2, qt + 1) * P

        units = [(qt, 4 * i + a, 2) for qt in range(2) for i in range(H1 // 4) for a in range(2)] +\
                [(qt, h, 1) for qt in range(2, NT) for h in range(H1)]
        UNITS = len(units)
        ends = [max(u for u in range(UNITS) if units[u][0] == qt) + 1 for qt in range(NT)]

        def taken_by_dve(s, u):
            return s == 0

        with nc.Block() as block:
            @block.sync
            def _(sp):
                sp.dma_start(w[:], g.Wqkv1T.rearrange("(c p) n -> p c n", p=P)).then_inc(c_in, 16)
                sp.dma_start(rope[:], g.rope1).then_inc(c_in, 16)
                sp.dma_start(wo[:], g.Wo1T.rearrange("(c p) n -> p c n", p=P)).then_inc(c_in, 16)
                sp.wait_ge(c_in, 48)

            @block.gpsimd
            def _(pool):
                for s in range(NS):
                    pool.memset(v[s][:], 0.0).then_inc(c_set, 1)

            @block.vector
            def _(dve):
                dve.tensor_copy(identr[:], g.ident[:]).then_inc(c_set, 1)
                dve.wait_ge(c_set, 1 + NS)

        with nc.Fori(0, PAIRS) as pair:
            with nc.Block() as block:
                @block.sync
                def _(sp):
                    for s in range(NS):
                        sp.dma_start(x[s][:], g.x1_d[pair * NS + s].rearrange("(t p) n -> p t n", p=P)).then_inc(x_in[s], 16)
                    for s in range(NS):
                        sp.wait_ge(x3_ready[s], NT)
                        sp.dma_start(g.x3_d[pair * NS + s].rearrange("(t p) n -> p t n", p=P), x[s][:]).then_inc(stored[s], 16)
                    for s in range(NS):
                        sp.wait_ge(xn_ready[s], 2 * NT)
                        sp.dma_start(g.y_d[0][pair * NS + s].rearrange("(t p) n -> p t n", p=P), xn[s][:]).then_inc(stored[s], 16)
                    for s in range(NS):
                        sp.wait_ge(stored[s], 32)

                @block.gpsimd
                def _(pool):
                    def power(s, k):
                        pool.wait_ge(var_ready[s], k)
                        pool.tensor_tensor(rstd[s][:], ve[s][:], g.minus_half[:, 0:NT], ALU.pow).then_inc(rstd_ready[s], 1)

                    for s in range(NS):
                        pool.tensor_copy(rowb[s][:], g.row_of[:, bass.ds(pair * (NS * NT) + s * NT, NT)]).then_inc(row_copied[s], 1)
                    for s in range(NS):
                        pool.wait_ge(row_copied[s], 1)
                        for t in range(NT):
                            pool.indirect_dma_start(yrow[s][:, t, :], None, g.ys_d,
                                                    bass.IndirectOffsetOnAxis(ap=rowb[s][:, t:t + 1], axis=0)).then_inc(y_in[s], 16)
                    for s in range(NS):
                        power(s, 1)
                    for t in range(NT):
                        for s in range(NS):
                            pool.wait_ge(turned[s], 3 * (t + 1))
                            if t:
                                pool.wait_ge(split[s], 2 * t)
                            pool.tensor_tensor(cosed[s][:], cosed[s][:], sined[s][:], ALU.add).then_inc(rotated[s], 1)
                    for s in range(NS):
                        power(s, 2)

                @block.vector
                def _(dve):
                    chain = Chain(dve, dve_chain)

                    def measure(s):
                        row_stats(dve, chain, var_ready[s], lambda t: [x[s][:, t, :]], stats[s], mv[s], ve[s])

                    def norm(s, k):
                        for ins in normalised_rows(dve, rstd_ready[s], k, lambda t: [x[s][:, t, :]], mv[s], rstd[s],
                                                   lambda t: [xn[s][:, t, :]]):
                            ins.then_inc(xn_ready[s], 1)

                    def turn(s, t):
                        dve.wait_ge(qk_psum[s], t + 1)
                        if t:
                            dve.wait_ge(split[s], 2 * t)
                        def heads(a):
                            return a.rearrange("p (i h d) -> p i h d", i=2, d=DH1)

                        src, out = heads(bank[s][0][:]), heads(sined[s][:])
                        dve.tensor_tensor(heads(cosed[s][:]), src, rope[:, t, :, 0, :].unsqueeze(2).to_broadcast([P, 2, H1, DH1]),
                                          ALU.mult).then_inc(turned[s], 1)
                        for a in range(2):
                            dve.tensor_tensor(out[:, :, :, a::2], src[:, :, :, 1 - a::2],
                                              rope[:, t, :, 1, a::2].unsqueeze(2).to_broadcast([P, 2, H1, DH1 // 2]),
                                              ALU.mult).then_inc(turned[s], 1)

                    def parts(s, t):
                        dve.wait_ge(rotated[s], t + 1)
                        if t:
                            dve.wait_ge(qkT_psum[s], 4 * t)
                        q = cosed[s][:, 0:D].rearrange("p (h d) -> p h d", d=DH1)
                        k = cosed[s][:, D:QK].rearrange("p (h d) -> p h d", d=DH1)
                        twice = [P, H1, 2, DH1]
                        hi = [(qhl[s][:, :, 0::2, :], q), (khl[s][:, :, 0:2, :], k)]
                        lo = [(qhl[s][:, :, 1::2, :], q), (khl[s][:, :, 2:4, :], k)]
                        for dst, src in hi:
                            m = chain.mark(dve.tensor_copy(dst, src.unsqueeze(2).to_broadcast(twice)))
                        chain.wait(m)
                        for (dst, src), (high, _) in zip(lo, hi):
                            dve.tensor_tensor(dst, src.unsqueeze(2).to_broadcast(twice), high.bitcast(F32), ALU.subtract)\
                               .then_inc(split[s], 1)

                    def row_max(s, u):
                        qt, h, n = units[u]
                        dve.wait_ge(scores_ready[s], u + 1)
                        S = bank[s][u % 2][:] if n == 1 else bank[s][u % 2][:].rearrange("p (h k) -> p h k", h=n)
                        S = S[:, 0:(qt + 1) * P].unsqueeze(1) if n == 1 else S[:, :, 0:(qt + 1) * P]
                        dve.tensor_reduce(nmax[s][:, qt, h:h + 2 * n - 1:2], S, AX, ALU.max, negate=True).then_inc(nmax_ready[s], 1)

                    def pT_out(s, u):
                        qt, h, n = units[u]
                        dve.wait_ge(pT_psum[s], u + 1)
                        if u >= 2:
                            dve.wait_ge(pv_done[s], u - 1)
                        w = n * (qt + 1)
                        dve.tensor_copy(probsT[s][:, u % 2, 0:w, :], bank[s][2][:, 0:w * P].rearrange("p (a b) -> p a b", b=P)).then_inc(pT_ready[s], 1)

                    def outputs(s, qt):
                        if qt == 0:
                            dve.wait_ge(probs_ready[s], UNITS)
                            chain.step(dve.reciprocal(rinv[s][:], rsum[s][:]))
                        dve.wait_ge(raw_psum[s], qt + 1)
                        dve.tensor_tensor(o[s][:, qt, :].rearrange("p (h d) -> p h d", d=DH1),
                                          bank[s][qt % 2][:].rearrange("p (h d) -> p h d", d=2 * DH1)[:, :, 0:DH1],
                                          rinv[s][:, qt, :].unsqueeze(2).to_broadcast([P, H1, DH1]), ALU.mult).then_inc(o_ready[s], 1)

                    for s in range(NS):
                        dve.wait_ge(x_in[s], 16)
                        dve.wait_ge(y_in[s], pair * (16 * NT) + 16 * NT)
                        dve.tensor_tensor(x[s][:], x[s][:], yrow[s][:], ALU.add).then_inc(x2_ready[s], 1)
                        dve.wait_ge(x2_ready[s], 1)
                        measure(s)
                    for s in range(NS):
                        norm(s, 1)
                    for t in range(NT + 1):
                        for s in range(NS):
                            if t:
                                parts(s, t - 1)
                            if t < NT:
                                turn(s, t)
                    for u in range(UNITS + 1):
                        for s in range(NS):
                            if u < UNITS:
                                row_max(s, u)
                        for s in range(NS):
                            if 1 <= u <= UNITS and taken_by_dve(s, u - 1):
                                pT_out(s, u - 1)
                    for s in range(NS):
                        for qt in range(NT):
                            outputs(s, qt)
                    for s in range(NS):
                        for t in range(NT):
                            dve.wait_ge(wo_psum[s], t + 1)
                            dve.tensor_tensor(x[s][:, t, :], bank[s][t % 2][:, 0:D], x[s][:, t, :], ALU.add).then_inc(x3_ready[s], 1)
                    for s in range(NS):
                        dve.wait_ge(x3_ready[s], NT)
                        measure(s)
                    for s in range(NS):
                        norm(s, 2)

                @block.scalar
                def _(act):
                    for s in range(NS):
                        for c in range(DC):
                            act.wait_ge(xnT_psum[s], c + 1)
                            act.activation(xnT[s][:, c, :], bank[s][c][:], ACT.Copy).then_inc(xnT_ready[s], 1)

                    def qkT_out(s, t, i):
                        act.wait_ge(qkT_psum[s], 4 * t + i + 1)
                        dst = (qT, kT)[i // 2][s]
                        act.activation(dst[:, 4 * (i % 2):4 * (i % 2) + 4, t * P:(t + 1) * P],
                                       bank[s][2 + i % 2][:].rearrange("p (a b) -> p a b", b=P), ACT.Copy).then_inc(qkT_ready[s], 1)

                    for t in range(NT + 1):
                        for s in range(NS):
                            if t < NT:
                                act.wait_ge(v_psum[s], t + 1)
                                act.activation(v[s][:, t, :, 0:DH1], bank[s][1][:, 0:D].rearrange("p (h d) -> p h d", d=DH1), ACT.Copy)\
                                   .then_inc(v_ready[s], 1)
                            if t:
                                for i in range(4):
                                    qkT_out(s, t - 1, i)
                    def exps(s, u):
                        qt, h, n = units[u]
                        w = (qt + 1) * P
                        act.wait_ge(nmax_ready[s], u + 1)
                        if u >= 2:
                            act.wait_ge(pT_psum[s], u - 1)
                        for j in range(n):
                            last = act.activation(probs[s][:, u % 2, j * w:(j + 1) * w], bank[s][u % 2][:, j * 2 * P:j * 2 * P + w], ACT.Exp,
                                                  bias=nmax[s][:, qt, h + 2 * j:h + 2 * j + 1], accum_out=rsum[s][:, qt, h + 2 * j:h + 2 * j + 1])
                        last.then_inc(probs_ready[s], 1)

                    def pT_out(s, u):
                        qt, h, n = units[u]
                        act.wait_ge(pT_psum[s], u + 1)
                        if u >= 2:
                            act.wait_ge(pv_done[s], u - 1)
                        w = n * (qt + 1)
                        act.activation(probsT[s][:, u % 2, 0:w, :], bank[s][2][:, 0:w * P].rearrange("p (a b) -> p a b", b=P), ACT.Copy)\
                           .then_inc(pT_ready[s], 1)

                    for u in range(UNITS + 2):
                        for s in range(NS):
                            if u < UNITS:
                                exps(s, u)
                        for s in range(NS):
                            if 1 <= u <= UNITS and not taken_by_dve(s, u - 1):
                                pT_out(s, u - 1)
                        for s in range(NS):
                            if u - 1 in ends:
                                act.wait_ge(pv_done[s], u - 1)
                                act.activation(raw[s][:, ends.index(u - 1)].rearrange("p a b -> p (a b)"), bank[s][3][:], ACT.Copy).then_inc(raw_ready[s], 1)
                    for s in range(NS):
                        for c in range(DC):
                            act.wait_ge(oT_psum[s], c + 1)
                            act.activation(oT[s][:, c, :], bank[s][2 + c][:], ACT.Copy).then_inc(oT_ready[s], 1)

                @block.tensor
                def _(pe):
                    def transposes(s):
                        for c in range(DC):
                            for t in range(NT):
                                if c == 0:
                                    pe.wait_ge(xn_ready[s], t + 1)
                                last = pe.transpose(bank[s][c][:, t * P:(t + 1) * P], xn[s][:, t, c * P:(c + 1) * P], g.ident[:])
                            last.then_inc(xnT_psum[s], 1)

                    def project(s, t):
                        if t == 0:
                            pe.wait_ge(xnT_ready[s], DC)
                        else:
                            pe.wait_ge(turned[s], 3 * t)
                        for c in range(DC):
                            last = pe.matmul(bank[s][0][:], xnT[s][:, c, t * P:(t + 1) * P], w[:, c, 0:QK], start=c == 0, stop=c == DC - 1)
                        last.then_inc(qk_psum[s], 1)
                        if t:
                            pe.wait_ge(v_ready[s], t)
                        for c in range(DC):
                            last = pe.matmul(bank[s][1][:, 0:D], xnT[s][:, c, t * P:(t + 1) * P], w[:, c, QK:3 * D], start=c == 0, stop=c == DC - 1)
                        last.then_inc(v_psum[s], 1)

                    def flip_qk(s, t):
                        pe.wait_ge(split[s], 2 * (t + 1))
                        for i in range(4):
                            if 4 * t + i >= 2:
                                pe.wait_ge(qkT_ready[s], 4 * t + i - 1)
                            out = bank[s][2 + i % 2]
                            for a in range(4):
                                p = 4 * (i % 2) + a
                                src = (qhl, khl)[i // 2][s][:, 2 * p:2 * p + 2].rearrange("p h a d -> p (h a d)")
                                last = pe.transpose(out[:, a * P:(a + 1) * P].bitcast(F32R), src, identr[:])
                            last.then_inc(qkT_psum[s], 1)

                    def scores(s, u):
                        qt, h, n = units[u]
                        if u == 0:
                            pe.wait_ge(qkT_ready[s], 4 * NT)
                            pe.wait_ge(v_ready[s], NT)
                        if u >= 2:
                            pe.wait_ge(probs_ready[s], u - 1)
                        for j in range(n):
                            r, p = slice(64 * (h % 2), 64 * (h % 2) + 64), h // 2 + j
                            S = bank[s][u % 2][:, j * 2 * P:]
                            pe.matmul(S[:, 0:kw(qt)], qT[s][r, p, qt * P:(qt + 1) * P], kT[s][r, p, 0:kw(qt)], start=True, stop=False)
                            last = pe.matmul(S[:, qt * P:(qt + 1) * P], g.mask[:, 0, :], g.mask[:, 2, :], start=False, stop=True)
                        last.then_inc(scores_ready[s], 1)

                    def flip(s, u):
                        qt, h, n = units[u]
                        pe.wait_ge(probs_ready[s], u + 1)
                        if u:
                            pe.wait_ge(pT_ready[s], u)
                        for k in range(n * (qt + 1)):
                            last = pe.transpose(bank[s][2][:, k * P:(k + 1) * P], probs[s][:, u % 2, k * P:(k + 1) * P], g.ident[:])
                        last.then_inc(pT_psum[s], 1)

                    def output(s, u):
                        qt, h, n = units[u]
                        pe.wait_ge(pT_ready[s], u + 1)
                        if u in ends:
                            pe.wait_ge(raw_ready[s], qt)
                        for j in range(n):
                            i, r = (h + 2 * j) // HG, 32 * ((h + 2 * j) % HG)
                            for kt in range(qt + 1):
                                last = pe.matmul(bank[s][3][r:r + 32, i * P:(i + 1) * P], v[s][:, kt, h + 2 * j, :], probsT[s][:, u % 2, j * (qt + 1) + kt, :],
                                                 start=kt == 0, stop=kt == qt, tile_position=(0, r))
                        last.then_inc(pv_done[s], 1)

                    for s in range(NS):
                        transposes(s)
                    for t in range(NT + 1):
                        for s in range(NS):
                            if t < NT:
                                project(s, t)
                            if t:
                                flip_qk(s, t - 1)
                    for u in range(UNITS + 2):
                        for s in range(NS):
                            if u < UNITS:
                                scores(s, u)
                        for s in range(NS):
                            if u >= 2:
                                output(s, u - 2)
                        for s in range(NS):
                            if 1 <= u <= UNITS:
                                flip(s, u - 1)
                    for s in range(NS):
                        for qt in range(NT):
                            pe.wait_ge(raw_ready[s], qt + 1)
                            if qt >= 2:
                                pe.wait_ge(o_ready[s], qt - 1)
                            for i in range(GROUPS):
                                last = pe.transpose(bank[s][qt % 2][:, i * P:(i + 1) * P], raw[s][:, qt, i, :], g.ident[:])
                            last.then_inc(raw_psum[s], 1)
                    for s in range(NS):
                        pe.wait_ge(o_ready[s], NT)
                        for c in range(DC):
                            for t in range(NT):
                                last = pe.transpose(bank[s][2 + c][:, t * P:(t + 1) * P], o[s][:, t, c * P:(c + 1) * P], g.ident[:])
                            last.then_inc(oT_psum[s], 1)
                    for s in range(NS):
                        pe.wait_ge(oT_ready[s], DC)
                        for t in range(NT):
                            if t >= 2:
                                pe.wait_ge(x3_ready[s], t - 1)
                            for c in range(DC):
                                last = pe.matmul(bank[s][t % 2][:, 0:D], oT[s][:, c, t * P:(t + 1) * P], wo[:, c, :], start=c == 0, stop=c == DC - 1)
                            last.then_inc(wo_psum[s], 1)
            nc.all_engine_barrier(sems_to_clear=sem_range)


H2, DH2 = 8, 64
INNER = H2 * DH2
HP2 = H2 // 2
HID = 682
UC = (HID + P - 1) // P


def phase_layer(nc, g, layer):
    final = layer == 1
    with ExitStack() as ctx:
        def sb(name, shape, dt=F32):
            return ctx.enter_context(nc.sbuf_tensor(f"l{layer}_{name}", shape, dt))

        def stream(name, shape, dt=F32):
            return [sb(f"{name}{s}", shape, dt) for s in range(NS)]

        def paired(name, shape, other, other_shape):
            offset = -(-nc.sbuf_base // 32) * 32
            first = sb(name, shape)
            assert int(np.prod(shape)) >= int(np.prod(other_shape))
            return first, nc.alloc_sbuf_tensor_at(f"l{layer}_{other}", other_shape, F32R, offset=offset)

        def paired_streams(name, shape, other, other_shape):
            return zip(*[paired(f"{name}{s}", shape, f"{other}{s}", other_shape) for s in range(NS)])

        sems = []

        def sem(name):
            sems.append(ctx.enter_context(nc.semaphore(f"l{layer}_{name}", num=LOOP_SEMS + len(sems))))
            return sems[-1]

        def sem2(name):
            return [sem(f"{name}{s}") for s in range(NS)]

        def weight(name, shape):
            raw, low = paired(f"{name}_raw", shape, f"{name}_low", shape)
            return raw, [low, sb(f"{name}_high", shape, F32R)]

        wqkv_raw, wqkv = weight("wqkv", [P, DC, 3 * INNER])
        w1_raw, w1 = weight("w1", [P, DC, 2 * HID])
        w2_raw, w2 = weight("w2", [P, UC, D])
        wo = sb("wo", [P, HP2, D])
        b1 = sb("b1", [P, 2, UC])
        b2 = sb("b2", [P, D])
        lng = sb("lng", [P, 2, DC])
        scales = sb("scales", [P, 2, DH2])
        scaled = sb("scaled", [P, NT, 4, DH2])
        y = stream("y", [P, NT, D])
        hT, yT = paired_streams("hT", [P, DC, L + 1], "yT", [P, DC, L + 1])
        work, u_low = paired_streams("work", [P, 3, 2 * INNER], "u_low", [P, UC, L])
        squares, rot2 = ([w[:, i, :] for w in work] for i in (0, 2))
        uT = [w[:].rearrange("p a (b n) -> p (a b) n", n=L) for w in work]
        assert uT[0].shape[1] == UC
        rope = work[0][:, 0, :].rearrange("p (t i d) -> p t i d", t=NT, i=4)
        ss, root, inv = stream("ss", [P, 2 * H2]), stream("root", [P, 2 * H2]), stream("inv", [P, 2 * H2])
        flipped, u_high_part = paired_streams("flipped", [P, UC, L], "u_high", [P, UC, L])
        qT = [f[:, 0:HP2, :] for f in flipped]
        probsT = [f[:, HP2:UC, :].rearrange("p a (b n) -> p a b n", n=P) for f in flipped]
        kT = stream("kT", [P, 2, HP2, L])
        v = stream("v", [P, NT, INNER])
        gate = [a[:, 0:2, :] for a in v]
        hn = [a[:, 2:NT, :].rearrange("p a (b n) -> p (a b) n", n=D) for a in v]
        probs = stream("probs", [P, 2, 2, 2 * P])
        rot = [[work[s][:, 1, :], probs[s][:].rearrange("p a b c -> p (a b c)")] for s in range(NS)]
        oT, part = paired_streams("oT", [P, HP2, L], "part", [P, DC, L + 1])
        stats, mv = stream("stats", [P, NT, 12]), stream("mv", [P, NT, 2])
        ve, rstd = stream("ve", [P, NT]), stream("rstd", [P, NT])
        UNITS = HP2 * NT
        nmax, rsum, rinv = stream("nmax", [P, UNITS, 2]), stream("rsum", [P, UNITS, 2]), stream("rinv", [P, UNITS, 2])
        bank = [[ctx.enter_context(nc.psum_tensor(f"l{layer}_bank{s}{i}", [P, L], F32)) for i in range(4)]
                for s in range(NS)]

        w_in, w_set, w_high = g.once(f"w_in{layer}"), g.once(f"w_set{layer}"), g.once(f"w_high{layer}")
        halves_in = [g.once(f"half_in{layer}{i}") for i in range(4)]
        y_in, yT_psum, yT_ready, yT_split = sem2("y_in"), sem2("yT_psum"), sem2("yT_ready"), sem2("yT_split")
        affine, hT_high, u_done, u_high = sem2("affine"), sem2("hT_high"), sem2("u_done"), sem2("u_high")
        qkv_psum, squared, v_ready, summed = sem2("qkv_psum"), sem2("squared"), sem2("v_ready"), sem2("summed")
        rooted, inv_ready, turned, added = sem2("rooted"), sem2("inv_ready"), sem2("turned"), sem2("added")
        q_rotated, k_rotated = sem2("q_rotated"), sem2("k_rotated")
        qkT_psum, qkT_ready = sem2("qkT_psum"), sem2("qkT_ready")
        scores_ready, nmax_ready, probs_ready, normed = sem2("scores"), sem2("nmax_r"), sem2("probs_r"), sem2("normed")
        pT_psum, pT_ready, pv_done, oT_ready = sem2("pT_psum"), sem2("pT_ready"), sem2("pv_done"), sem2("oT_ready")
        wo_psum, y1_ready, shifted = sem2("wo_psum"), sem2("y1_ready"), sem2("shifted")
        chain_sem, var_ready, rstd_ready, hn_ready = sem("chain"), sem2("var"), sem2("rstd_r"), sem2("hn_ready")
        biased, hT_psum, hT_ready = sem2("biased"), sem2("hT_psum"), sem2("hT_ready")
        ag_psum, gate_ready, u_ready = sem2("ag_psum"), sem2("gate_ready"), sem2("u_ready")
        w2_psum, y2_ready, x_in, stored, xadded = sem2("w2_psum"), sem2("y2_ready"), sem2("x_in"), sem2("stored"), sem2("xadded")
        sem_range = range(sems[0].num, sems[-1].num + 1)
        assert len(sem_range) == len(sems)
        units = [(cp, w, r) for cp in range(HP2 // 2) for w in range(NT) for r in range(2)]

        turns = [(s, t) for t in range(NT) for s in range(NS)]
        LAG = 3

        LEAD = 3
        chunks = [(0, c) for c in range(LEAD)] + [turn for c in range(UC - LEAD) for turn in ((1, c), (0, c + LEAD))] +\
                 [(1, c) for c in range(UC - LEAD, UC)]

        def kT_bank(t):
            return 2 if t == NT - 1 else 3

        def rows(c):
            return min(P, HID - c * P)

        WHOLE = HID // P * P
        tail = rows(UC - 1)
        halves = [[w[:] for w in (wqkv_raw, *wqkv)], [w[:] for w in (w1_raw, *w1)], [w[:, 0:UC - 1, :] for w in (w2_raw, *w2)],
                  [w[0:tail, UC - 1, :] for w in (w2_raw, *w2)]]
        SPLIT_SRC = [g.wqkv[layer].rearrange("(c p) n -> p c n", p=P), g.w1d[layer].rearrange("(c p) n -> p c n", p=P),
                     g.w2d[layer][0:WHOLE].rearrange("(c p) n -> p c n", p=P), g.w2d[layer][WHOLE:HID]]
        LOADS = [(rope, g.rope2),
                 (scales[:, 0, :], g.qs[layer].partition_broadcast(P)), (scales[:, 1, :], g.ks[layer].partition_broadcast(P)),
                 (lng[:, 0, :], g.lng[layer]), (lng[:, 1, :], g.lnb[layer]), (b1[:], g.b1l[layer]),
                 (b2[:], g.b2l[layer].partition_broadcast(P)), (wo[:], g.wo[layer].rearrange("(c p) n -> p c n", p=P))]

        with nc.Block() as block:
            @block.sync
            def _(sp):
                for (raw, _, _), src, arrived in zip(halves, SPLIT_SRC, halves_in):
                    sp.dma_start(raw, src).then_inc(arrived, 16)
                for dst, src in LOADS:
                    sp.dma_start(dst, src).then_inc(w_in, 16)

            @block.vector
            def _(dve):
                for s in range(NS):
                    dve.memset(yT[s][:, 1, 0:1].bitcast(F32), 0.0)
                    dve.memset(kT[s][DH2:P, 0], 0.0)
                    dve.memset(kT[s][0:DH2, 1], 0.0).then_inc(w_set, 1)
                for i, (raw, low, high) in enumerate(halves):
                    dve.wait_ge(w_high, i + 1)
                    dve.tensor_tensor(low, raw, high.bitcast(F32), ALU.subtract).then_inc(w_set, 1)
                dve.wait_ge(w_in, 16 * len(LOADS))
                for i in range(2):
                    dve.tensor_tensor(scaled[:, :, 2 * i, :], rope[:, :, 2 * i, :],
                                      scales[:, i, :].unsqueeze(1).to_broadcast([P, NT, DH2]), ALU.mult).then_inc(w_set, 1)
                    for a in range(2):
                        h = DH2 // 2
                        dve.tensor_tensor(scaled[:, :, 2 * i + 1, a * h:(a + 1) * h], rope[:, :, 2 * i + 1, a * h:(a + 1) * h],
                                          scales[:, i, (1 - a) * h:(2 - a) * h].unsqueeze(1).to_broadcast([P, NT, h]),
                                          ALU.mult).then_inc(w_set, 1)
                dve.wait_ge(w_set, NS + 6 + len(halves))

            @block.scalar
            def _(act):
                for i, (raw, low, high) in enumerate(halves):
                    act.wait_ge(halves_in[i], 16)
                    act.activation(high, raw, ACT.Copy).then_inc(w_high, 1)

        with nc.Fori(0, PAIRS) as pair:
            with nc.Block() as block:
                @block.sync
                def _(sp):
                    for s in range(NS):
                        sp.dma_start(y[s][:], g.y_d[layer][pair * NS + s].rearrange("(t p) n -> p t n", p=P)).then_inc(y_in[s], 16)
                    if final:
                        for s in range(NS):
                            sp.wait_ge(hT_psum[s], DC)
                            sp.dma_start(hn[s][:], g.x3_d[pair * NS + s].rearrange("(t p) n -> p t n", p=P)).then_inc(x_in[s], 16)
                    dst = g.out if final else g.y_d[layer + 1]
                    for s in range(NS):
                        sp.wait_ge(y2_ready[s], NT)
                        sp.dma_start(dst[pair * NS + s].rearrange("(t p) n -> p t n", p=P), y[s][:]).then_inc(stored[s], 16)
                    for s in range(NS):
                        sp.wait_ge(stored[s], 16)

                def heads(a):
                    return a.rearrange("p (h d) -> p h d", d=DH2)

                def normalise(eng, s, t, i):
                    space = heads(rot[s][t % 2][:, i * INNER:(i + 1) * INNER])
                    return eng.tensor_tensor(space, space, inv[s][:, i * H2:(i + 1) * H2].unsqueeze(2).to_broadcast([P, H2, DH2]), ALU.mult)

                @block.gpsimd
                def _(pool):
                    def add(s, t, j):
                        cols = slice(j * INNER, (j + 1) * INNER)
                        pool.wait_ge(turned[s], 6 * t + 3 * (j + 1))
                        pool.tensor_tensor(rot[s][t % 2][:, cols], rot[s][t % 2][:, cols], rot2[s][:, cols], ALU.add).then_inc(added[s], 1)

                    for i in range(len(turns) + 1):
                        if i < len(turns):
                            add(*turns[i], 0)
                        if i:
                            s, t = turns[i - 1]
                            pool.wait_ge(added[s], 2 * (t + 1))
                            pool.wait_ge(inv_ready[s], t + 1)
                            normalise(pool, s, t, 1).then_inc(k_rotated[s], 1)
                        if i < len(turns):
                            add(*turns[i], 1)
                    assert NS == 2 and NT == 4
                    for s in range(NS):
                        pool.wait_ge(var_ready[s], 1)
                        pool.tensor_tensor(rstd[s][:], ve[s][:], g.minus_half[:, 0:NT], ALU.pow).then_inc(rstd_ready[s], 1)
                    for s in range(NS):
                        pool.wait_ge(hn_ready[s], 2 * NT)
                        pool.wait_ge(shifted[s], 1)
                        pool.tensor_tensor(y[s][:], y[s][:], b2[:].unsqueeze(1).to_broadcast([P, NT, D]), ALU.add).then_inc(biased[s], 1)
                    if final:
                        for s in range(NS):
                            pool.wait_ge(x_in[s], 16)
                            pool.wait_ge(biased[s], 1)
                            pool.tensor_tensor(y[s][:], y[s][:], hn[s][:], ALU.add).then_inc(xadded[s], 1)

                @block.vector
                def _(dve):
                    chain = Chain(dve, chain_sem)

                    def norms(s, t):
                        if t:
                            dve.wait_ge(rooted[s], t)
                        chain.step(dve.tensor_reduce(ss[s][:], heads(squares[s]), AX, ALU.add))
                        dve.tensor_scalar(ss[s][:], ss[s][:], 1e-24, None, ALU.max).then_inc(summed[s], 1)

                    def turn(s, t):
                        if t:
                            dve.wait_ge(added[s], 2 * t)
                        if t >= 2:
                            dve.wait_ge(qkT_psum[s], 2 * (t - 1))
                        h, rot_t = DH2 // 2, rot[s][t % 2]
                        for i in range(2):
                            src = heads(bank[s][i][:])
                            dst, dst2 = (heads(a[:, i * INNER:(i + 1) * INNER]) for a in (rot_t, rot2[s]))
                            dve.wait_ge(squared[s], 2 * t + i + 1)
                            dve.tensor_tensor(dst, src, scaled[:, t, 2 * i:2 * i + 1, :].to_broadcast([P, H2, DH2]), ALU.mult).then_inc(turned[s], 1)
                            for a in range(2):
                                dve.tensor_tensor(dst2[:, :, a * h:(a + 1) * h], src[:, :, (1 - a) * h:(2 - a) * h],
                                                  scaled[:, t, 2 * i + 1:2 * i + 2, a * h:(a + 1) * h].to_broadcast([P, H2, h]),
                                                  ALU.mult).then_inc(turned[s], 1)

                    def invert(s, t):
                        dve.wait_ge(rooted[s], t + 1)
                        if t:
                            dve.wait_ge(k_rotated[s], t)
                        dve.reciprocal(inv[s][:], root[s][:]).then_inc(inv_ready[s], 1)

                    def row_max(s, u):
                        w = units[u][1]
                        dve.wait_ge(scores_ready[s], u + 1)
                        S = bank[s][u % 2][:].rearrange("p (h k) -> p h k", h=2)
                        dve.tensor_reduce(nmax[s][:, u, :], S[:, :, 0:(1 + min(w, 1)) * P], AX, ALU.max, negate=True).then_inc(nmax_ready[s], 1)

                    def norm_probs(s, u):
                        w = units[u][1]
                        n = (1 + min(w, 1)) * P
                        dve.wait_ge(probs_ready[s], 2 * (u + 1))
                        chain.step(dve.reciprocal(rinv[s][:, u, :], rsum[s][:, u, :]))
                        for h in range(2):
                            dve.tensor_scalar(probs[s][:, u % 2, h, 0:n], probs[s][:, u % 2, h, 0:n], rinv[s][:, u, h:h + 1], None, ALU.mult)\
                               .then_inc(normed[s], 1)

                    for s in range(NS):
                        dve.memset(part[s][:, 1, 0:1].bitcast(F32), 0.0).then_inc(yT_split[s], 1)
                        for c in range(DC):
                            dve.wait_ge(yT_ready[s], c + 1)
                            dve.tensor_tensor(part[s][:, c, c:L + c], bank[s][c][:, 0:L], yT[s][:, c, c:L + c].bitcast(F32), ALU.subtract)\
                               .then_inc(yT_split[s], 1)
                    for i in range(len(turns) + 1):
                        if i < len(turns):
                            turn(*turns[i])
                        if i:
                            s, t = turns[i - 1]
                            invert(s, t)
                            dve.wait_ge(added[s], 2 * t + 1)
                            dve.wait_ge(inv_ready[s], t + 1)
                            normalise(dve, s, t, 0).then_inc(q_rotated[s], 1)
                        if i < len(turns):
                            norms(*turns[i])
                    for u in range(UNITS + 1):
                        for s in range(NS):
                            if u:
                                norm_probs(s, u - 1)
                        for s in range(NS):
                            if u < UNITS:
                                row_max(s, u)
                    def residual(s, t):
                        dve.wait_ge(wo_psum[s], t + 1)
                        dve.tensor_tensor(y[s][:, t, :], bank[s][t % 2][:, 0:D], y[s][:, t, :], ALU.add).then_inc(y1_ready[s], 1)

                    def parts(s):
                        late = bank[s][2][:].rearrange("p (t n) -> p t n", t=NT)
                        return lambda t: [y[s][:, t, 0:P], late[:, t, :]]

                    def measure(s):
                        dve.wait_ge(y1_ready[s], NT)
                        dve.wait_ge(shifted[s], 1)
                        row_stats(dve, chain, var_ready[s], parts(s), stats[s], mv[s], ve[s])

                    def norm(s):
                        for ins in normalised_rows(dve, rstd_ready[s], 1, parts(s), mv[s], rstd[s],
                                                   lambda t: [hn[s][:, t, 0:P], hn[s][:, t, P:D]]):
                            ins.then_inc(hn_ready[s], 1)

                    def scale_rows(s):
                        for c in range(DC):
                            dve.wait_ge(hT_psum[s], c + 1)
                            dve.tensor_scalar(hT[s][:, c, 1:L + 1], bank[s][c][:], lng[:, 0, c:c + 1], lng[:, 1, c:c + 1], ALU.mult, ALU.add)\
                               .then_inc(affine[s], 1)

                    def low_rows(s):
                        for c in range(DC):
                            dve.wait_ge(hT_high[s], c + 1)
                            dve.tensor_tensor(yT[s][:, c, 1:L + 1], hT[s][:, c, 1:L + 1], part[s][:, c, 1:L + 1].bitcast(F32), ALU.subtract)\
                               .then_inc(hT_ready[s], 1)

                    def gated(s, c):
                        r = rows(c)
                        dve.wait_ge(gate_ready[s], c + 1)
                        dve.scalar_tensor_tensor(uT[s][0:r, c, :], bank[s][2 * (c % 2)][0:r, :], b1[0:r, 0, c:c + 1], gate[s][0:r, c % 2, :],
                                                 ALU.add, ALU.mult).then_inc(u_done[s], 1)

                    def low_units(s, c):
                        r = rows(c)
                        dve.wait_ge(u_high[s], c + 1)
                        dve.tensor_tensor(u_low[s][0:r, c, :], uT[s][0:r, c, :], u_high_part[s][0:r, c, :].bitcast(F32), ALU.subtract)\
                           .then_inc(u_ready[s], 1)

                    for t in range(NT):
                        residual(0, t)
                    residual(1, 0)
                    measure(0)
                    residual(1, 1)
                    residual(1, 2)
                    norm(0)
                    residual(1, 3)
                    scale_rows(0)
                    low_rows(0)
                    measure(1)
                    norm(1)
                    for i in range(len(chunks) + 1):
                        if i < len(chunks):
                            gated(*chunks[i])
                        if i == 0:
                            scale_rows(1)
                        if i:
                            low_units(*chunks[i - 1])
                        if i == 1:
                            low_rows(1)
                    for s in range(NS):
                        dve.wait_ge(xadded[s] if final else biased[s], 1)
                        for t in range(NT):
                            dve.wait_ge(w2_psum[s], t + 1)
                            dve.tensor_tensor(y[s][:, t, :], bank[s][t % 2][:, 0:D], y[s][:, t, :], ALU.add).then_inc(y2_ready[s], 1)

                @block.scalar
                def _(act):
                    for s in range(NS):
                        for c in range(DC):
                            act.wait_ge(yT_psum[s], c + 1)
                            act.activation(yT[s][:, c, c:L + c], bank[s][c][:, 0:L], ACT.Copy).then_inc(yT_ready[s], 1)

                    def qT_out(s, t):
                        act.wait_ge(qkT_psum[s], 2 * t + 1)
                        act.activation(qT[s][:, :, t * P:(t + 1) * P], bank[s][3][:].rearrange("p (a b) -> p a b", b=P), ACT.Copy)\
                           .then_inc(qkT_ready[s], 1)

                    def kT_out(s, t):
                        act.wait_ge(qkT_psum[s], 2 * t + 2)
                        src = bank[s][kT_bank(t)][:].rearrange("p (a b) -> p a b", b=P)
                        for half in range(2):
                            r = slice(DH2 * half, DH2 * (half + 1))
                            last = act.activation(kT[s][r, half, :, t * P:(t + 1) * P], src[r], ACT.Copy)
                        last.then_inc(qkT_ready[s], 1)

                    def square(s, t, j):
                        act.wait_ge(qkv_psum[s], 3 * t + j + 1)
                        act.activation(squares[s][:, j * INNER:(j + 1) * INNER], bank[s][j][:], ACT.Square).then_inc(squared[s], 1)

                    def square_root(s, t):
                        act.wait_ge(summed[s], t + 1)
                        if t:
                            act.wait_ge(inv_ready[s], t)
                        act.activation(root[s][:], ss[s][:], ACT.Sqrt).then_inc(rooted[s], 1)

                    for i in range(len(turns) + LAG):
                        now = turns[i] if i < len(turns) else None
                        before = turns[i - LAG] if i >= LAG else None
                        if now:
                            if now[1]:
                                act.wait_ge(summed[now[0]], now[1])
                            square(*now, 0)
                        if before:
                            qT_out(*before)
                        if now:
                            square(*now, 1)
                        if 1 <= i <= len(turns):
                            square_root(*turns[i - 1])
                        if before:
                            kT_out(*before)
                        if now:
                            s, t = now
                            act.wait_ge(qkv_psum[s], 3 * (t + 1))
                            act.activation(v[s][:, t, :], bank[s][2][:], ACT.Copy).then_inc(v_ready[s], 1)

                    def exps(s, u):
                        w = units[u][1]
                        n = (1 + min(w, 1)) * P
                        act.wait_ge(nmax_ready[s], u + 1)
                        if u >= 2:
                            act.wait_ge(pT_psum[s], u - 1)
                        for h in range(2):
                            act.activation(probs[s][:, u % 2, h, 0:n], bank[s][u % 2][:, 2 * P * h:2 * P * h + n], ACT.Exp,
                                           bias=nmax[s][:, u, h:h + 1], accum_out=rsum[s][:, u, h:h + 1]).then_inc(probs_ready[s], 1)

                    def pT_out(s, u):
                        act.wait_ge(pT_psum[s], u + 1)
                        if u >= 2:
                            act.wait_ge(pv_done[s], u - 1)
                        if units[u][1]:
                            act.activation(probsT[s][:, u % 2].rearrange("p a b -> p (a b)"), bank[s][2][:], ACT.Copy).then_inc(pT_ready[s], 1)
                        else:
                            act.activation(probsT[s][:, u % 2, 0:4:2, :], bank[s][2][:].rearrange("p (a b) -> p a b", b=P)[:, 0:4:2, :], ACT.Copy)\
                               .then_inc(pT_ready[s], 1)

                    def oT_out(s, i):
                        cp, w = i // NT, i % NT
                        act.wait_ge(pv_done[s], 2 * (i + 1))
                        act.activation(oT[s][:, 2 * cp:2 * cp + 2, w * P:(w + 1) * P], bank[s][3][:, 0:2 * P].rearrange("p (a b) -> p a b", b=P),
                                       ACT.Copy).then_inc(oT_ready[s], 1)

                    for u in range(UNITS + 2):
                        for s in range(NS):
                            if u < UNITS:
                                exps(s, u)
                        for s in range(NS):
                            if 1 <= u <= UNITS:
                                pT_out(s, u - 1)
                            if u >= 2 and u % 2:
                                oT_out(s, (u - 2) // 2)
                    def high_rows(s):
                        for c in range(DC):
                            act.wait_ge(affine[s], c + 1)
                            act.activation(part[s][:, c, 1:L + 1], hT[s][:, c, 1:L + 1], ACT.Copy).then_inc(hT_high[s], 1)

                    def high(s, c):
                        r = rows(c)
                        act.wait_ge(u_done[s], c + 1)
                        act.activation(u_high_part[s][0:r, c, :], uT[s][0:r, c, :], ACT.Copy).then_inc(u_high[s], 1)

                    high_rows(0)
                    for i in range(len(chunks) + 1):
                        if i < len(chunks):
                            s, c = chunks[i]
                            r = rows(c)
                            act.wait_ge(ag_psum[s], c + 1)
                            if c >= 2:
                                act.wait_ge(u_done[s], c - 1)
                            act.activation(gate[s][0:r, c % 2, :], bank[s][2 * (c % 2) + 1][0:r, :], ACT.Gelu, bias=b1[0:r, 1, c:c + 1])\
                               .then_inc(gate_ready[s], 1)
                        if i:
                            high(*chunks[i - 1])
                        if i == 1:
                            high_rows(1)

                @block.tensor
                def _(pe):
                    for s in range(NS):
                        pe.wait_ge(y_in[s], 16)
                        for c in range(DC):
                            for t in range(NT):
                                last = pe.transpose(bank[s][c][:, t * P:(t + 1) * P], y[s][:, t, c * P:(c + 1) * P], g.ident[:])
                            last.then_inc(yT_psum[s], 1)

                    def product(out, a, b, start, stop):
                        pe.matmul(out, a[0], b[0], start=start, stop=False)
                        pe.matmul(out, a[0], b[1], start=False, stop=False)
                        return pe.matmul(out, a[1], b[0], start=False, stop=stop)

                    def project(s, t, i):
                        if i == 0 and t == 0:
                            pe.wait_ge(yT_split[s], DC + 1)
                        elif i == 0:
                            pe.wait_ge(turned[s], 6 * t)
                        elif i == 2 and t:
                            pe.wait_ge(v_ready[s], t)
                        for c in range(DC):
                            last = product(bank[s][i][:], [a[:, c, t * P:(t + 1) * P] for a in (yT[s], part[s])],
                                           [wqkv[k][:, c, i * INNER:(i + 1) * INNER] for k in (1, 0)], c == 0, c == DC - 1)
                        last.then_inc(qkv_psum[s], 1)

                    def flip_qk(s, t, i):
                        pe.wait_ge((q_rotated, k_rotated)[i][s], t + 1)
                        if t == NT - 1 and i:
                            pe.wait_ge(v_ready[s], NT)
                        elif 2 * t + i >= 1:
                            pe.wait_ge(qkT_ready[s], 2 * t + i)
                        for a in range(HP2):
                            last = pe.transpose(bank[s][kT_bank(t) if i else 3][:, a * P:(a + 1) * P], rot[s][t % 2][:, i * INNER + a * P:i * INNER + (a + 1) * P], g.ident[:])
                        last.then_inc(qkT_psum[s], 1)

                    def scores(s, u):
                        cp, w, half = units[u]
                        if u == 0:
                            pe.wait_ge(qkT_ready[s], 2)
                            pe.wait_ge(turned[s], 6 * NT)
                        if u == 2:
                            pe.wait_ge(qkT_ready[s], 2 * NT)
                        if u >= 2:
                            pe.wait_ge(probs_ready[s], 2 * (u - 1))
                        k0, n = (w - 1, 2) if w else (0, 1)
                        for h in range(2):
                            p = 2 * cp + h
                            out = bank[s][u % 2][:, 2 * P * h:2 * P * h + n * P]
                            pe.matmul(out, qT[s][:, p, w * P:(w + 1) * P], kT[s][:, half, p, k0 * P:(k0 + n) * P], start=True, stop=False)
                            last = pe.matmul(out, g.mask[:, 0, :], g.mask[:, 3 - n:3, :].rearrange("p a b -> p (a b)"), start=False, stop=True)
                        last.then_inc(scores_ready[s], 1)

                    def flip(s, u):
                        w = units[u][1]
                        if u == 0:
                            pe.wait_ge(qkT_ready[s], 2 * NT)
                        pe.wait_ge(normed[s], 2 * (u + 1))
                        if u:
                            pe.wait_ge(pT_ready[s], u)
                        for h in range(2):
                            for k in range(1 + min(w, 1)):
                                last = pe.transpose(bank[s][2][:, (2 * h + k) * P:(2 * h + k + 1) * P], probs[s][:, u % 2, h, k * P:(k + 1) * P], g.ident[:])
                        last.then_inc(pT_psum[s], 1)

                    def output(s, u):
                        cp, w, half = units[u]
                        pe.wait_ge(pT_ready[s], u + 1)
                        if half == 0 and u:
                            pe.wait_ge(oT_ready[s], u // 2)
                        k0, n = (w - 1, 2) if w else (0, 1)
                        for h in range(2):
                            for k in range(n):
                                head = (2 * (2 * cp + h) + half) * DH2
                                last = pe.matmul(bank[s][3][DH2 * half:DH2 * (half + 1), h * P:(h + 1) * P], v[s][:, k0 + k, head:head + DH2],
                                                 probsT[s][:, u % 2, 2 * h + k, :], start=k == 0, stop=k == n - 1, tile_position=(0, DH2 * half))
                        last.then_inc(pv_done[s], 1)

                    def hidden(s, c):
                        if c >= 2:
                            pe.wait_ge(u_done[s], c - 1)
                        r = rows(c)
                        for i in range(2):
                            for k in range(DC):
                                last = product(bank[s][2 * (c % 2) + i][0:r, :], [w1[a][:, k, i * HID + c * P:i * HID + c * P + r] for a in (1, 0)],
                                               [a[:, k, 1:L + 1] for a in (part[s], yT[s])], k == 0, k == DC - 1)
                        last.then_inc(ag_psum[s], 1)

                    for i in range(len(turns) + LAG):
                        if i >= len(turns) + LAG - NS:
                            for u in range(2):
                                scores(i - (len(turns) + LAG - NS), u)
                        for j in range(3):
                            if i < len(turns):
                                project(*turns[i], j)
                            if i >= LAG and j < 2:
                                flip_qk(*turns[i - LAG], j)
                    for u in range(UNITS + 2):
                        for s in range(NS):
                            if 2 <= u < UNITS:
                                scores(s, u)
                        for s in range(NS):
                            if u >= 2:
                                output(s, u - 2)
                        for s in range(NS):
                            if 1 <= u <= UNITS:
                                flip(s, u - 1)
                    def attended(s, t):
                        if t == 0:
                            pe.wait_ge(oT_ready[s], UNITS // 2)
                        if t >= 2:
                            pe.wait_ge(y1_ready[s], t - 1)
                        for c in range(HP2):
                            last = pe.matmul(bank[s][t % 2][:, 0:D], oT[s][:, c, t * P:(t + 1) * P], wo[:, c, :], start=c == 0, stop=c == HP2 - 1)
                        last.then_inc(wo_psum[s], 1)

                    def shift(s):
                        pe.wait_ge(y1_ready[s], NT)
                        late = bank[s][2][:].rearrange("p (t n) -> p t n", t=NT)
                        pe.matmul(late, g.shift[:, 0, :], y[s][:, :, P:D], start=True, stop=False)
                        pe.matmul(late[:, 1:NT, :], g.shift[:, 1, :], y[s][:, 0:NT - 1, P:D], start=False, stop=True).then_inc(shifted[s], 1)

                    def flip_hn(s):
                        for c in range(DC):
                            for t in range(NT):
                                pe.wait_ge(hn_ready[s], 2 * (t + 1))
                                last = pe.transpose(bank[s][c][:, t * P:(t + 1) * P], hn[s][:, t, c * P:(c + 1) * P], g.ident[:])
                            last.then_inc(hT_psum[s], 1)

                    for t in range(NT):
                        attended(0, t)
                    attended(1, 0)
                    shift(0)
                    for t in range(1, NT):
                        attended(1, t)
                    flip_hn(0)
                    shift(1)
                    for i, (s, c) in enumerate(chunks):
                        if c == 0:
                            pe.wait_ge(hT_ready[s], DC)
                        hidden(s, c)
                        if i == 1:
                            flip_hn(1)
                    for s in range(NS):
                        pe.wait_ge(u_ready[s], UC)
                        for t in range(NT):
                            if t >= 2:
                                pe.wait_ge(y2_ready[s], t - 1)
                            for c in range(UC):
                                r = rows(c)
                                last = product(bank[s][t % 2][:, 0:D], [a[0:r, c, t * P:(t + 1) * P] for a in (u_high_part[s], u_low[s])],
                                               [w2[a][0:r, c, :] for a in (1, 0)], c == 0, c == UC - 1)
                            last.then_inc(w2_psum[s], 1)
            nc.all_engine_barrier(sems_to_clear=sem_range)


def shape_tables():
    f = np.float32
    t = {}
    scale_vec = ((np.arange(0, D, 2, dtype=f) + f(0.4 * D)) / f(1.4 * D)).astype(f)
    scale = (scale_vec[None, :] ** (np.arange(L, dtype=f) / f(512.0))[:, None]).astype(f)
    inv_freq = (f(1.0) / f(10000.0) ** (np.arange(D // 2, dtype=f) / f(D // 2))).astype(f)
    angle = (np.arange(L, dtype=f)[:, None] * inv_freq[None, :]).astype(f)
    sin, cos = np.sin(angle), np.cos(angle)
    inv = (f(1.0) / scale).astype(f)
    t["xpos0"] = np.stack([(cos * scale).T, (sin * scale).T, (cos * inv).T, (sin * inv).T], axis=1)
    t["decay"] = f(0.9) ** np.abs(np.arange(7 * P)[None, :] - (NT - 1) * P - np.arange(P)[:, None]).astype(f)
    t["ident"] = np.eye(P, dtype=f)
    t["ranks"] = np.concatenate([np.triu(np.ones((P, P), f), 1), np.ones((P, P), f)], axis=1)
    t["iota"] = np.tile(np.arange(P, dtype=f)[None, :], (P, 1))
    dh = 16
    freqs = np.exp(f(-np.log(10000.0)) * np.arange(0, dh, 2, dtype=f) / f(dh)).astype(f)
    ang = np.repeat(np.arange(L, dtype=f)[:, None] * freqs[None, :], 2, axis=1).astype(f)
    sign = np.where(np.arange(dh) % 2 == 0, f(-1), f(1)).astype(f)
    rope = np.stack([np.cos(ang), np.sin(ang) * sign], axis=1)
    rope = rope.astype(f)
    rope = np.stack([rope * f(0.25), rope], axis=1)
    t["rope1"] = rope.reshape(NT, P, 2, 2, dh).transpose(1, 0, 2, 3, 4)
    dh, window = 64, 128
    half = np.arange(0, dh, 2, dtype=f)
    invf = (f(1.0) / f(10000.0) ** (half / f(dh))).astype(f)
    fr = (np.arange(L, dtype=f)[:, None] * invf[None, :]).astype(f)
    fr = np.concatenate([fr, fr], axis=-1)
    base = ((half + f(0.4 * dh)) / f(1.4 * dh)).astype(f)
    power = ((np.arange(L, dtype=f) - f(L // 2)) / f(window // 2)).astype(f)
    sc = (base[None, :] ** power[:, None]).astype(f)
    sc = np.concatenate([sc, sc], axis=-1)
    sign = np.where(np.arange(dh) < dh // 2, f(-1), f(1)).astype(f)
    c, s_ = np.cos(fr), np.sin(fr) * sign
    w = np.stack([c * sc * f(8), s_ * sc * f(8), c / sc, s_ / sc], axis=1).astype(f)
    t["rope2"] = w.reshape(NT, P, 4, dh).transpose(1, 0, 2, 3)
    shift = np.zeros((P, 2, P), f)
    shift[np.arange(P - 1), 0, np.arange(1, P)] = 1
    shift[P - 1, 1, 0] = 1
    t["shift"] = shift
    a, cc = np.arange(P)[:, None], np.arange(P)[None, :]
    ban = np.stack([a > cc, cc > a], axis=1) * -1e30
    t["mask"] = np.concatenate([np.eye(P)[:, None, :], ban], axis=1).astype(f)
    return {k: np.ascontiguousarray(v) for k, v in t.items()}


def build(nc, g):
    with g.ctx:
        g.ident, g.shift = g.keep("ident", [P, P]), g.keep("shift", [P, 2, P])
        g.mask, g.minus_half = g.keep("mask", [P, 3, P], BF16), g.keep("minus_half", [P, 2 * H2])
        g.row_of, g.owner = g.keep("row_of", [P, TILES], I32), g.keep("owner", [P, MAXSLOT], I32)
        g.x1_d = nc.dram_tensor("x1_d", (B, L, D), F32).ap()
        g.x3_d = nc.dram_tensor("x3_d", (B, L, D), F32).ap()
        g.y_d = [nc.dram_tensor(f"y{i}_d", (B, L, D), F32).ap() for i in range(2)]
        g.xs_d = nc.dram_tensor("xs_d", (MAXSLOT * P, D), F32).ap()
        g.ys_d = nc.dram_tensor("ys_d", (SLOTS * P, D), F32).ap()
        tables_in = g.once("kept_in")
        g.w1_in, g.w2_in, g.pool_consts, g.zeros_out = (g.once(n) for n in ("w1_in", "w2_in", "pool_consts", "zeros_out"))
        with nc.sbuf_tensor("mask_f32", [P, 3, P], F32) as mask_f32, nc.Block() as block:
            @block.sync
            def _(sp):
                for dst, src in [(g.ident, g.ident_d), (g.shift, g.shift_d), (mask_f32, g.mask_d)]:
                    sp.dma_start(dst[:], src).then_inc(tables_in, 16)

            @block.vector
            def _(dve):
                dve.wait_ge(tables_in, 48)
                dve.tensor_copy(g.mask[:], mask_f32[:]).then_inc(tables_in, 1)
                dve.wait_ge(tables_in, 49)

        with ExitStack() as experts:
            def sb(name, shape, dt=F32):
                return experts.enter_context(nc.sbuf_tensor(name, shape, dt))

            g.w1, g.xn2 = sb("w1", [P, EXPERTS, DC, FF]), sb("xn2", [P, TILES, D])
            g.logits = sb("logits", [P, TILES, EXPERTS])
            with nc.sbuf_tensor("zrow", [P, ZEROED * D], F32) as zrow:
                g.zrow = zrow
                phase_attn0(nc, g)
            g.w2, g.b1, g.b2 = sb("w2", [P, EXPERTS, FC, D]), sb("b1", [P, EXPERTS, FC]), sb("b2", [P, EXPERTS, D])
            phase_route(nc, g)
            phase_experts(nc, g)
        phase_attn1(nc, g)
        for layer in range(2):
            phase_layer(nc, g, layer)


def kernel(**inputs):
    import concourse.bacc as bacc
    from concourse.bass_utils import run_bass_kernel_spmd

    a = {k: np.asarray(v) for k, v in inputs.items()}
    tables = shape_tables()
    HIDDEN = a["L1_ffn_b1"].shape[1] // 2
    b1 = np.zeros((2, UC * P, 2), np.float32)
    b1[:, 0:HIDDEN] = a["L1_ffn_b1"].reshape(2, 2, HIDDEN).transpose(0, 2, 1)
    laid_out = {
        "X": a["L0_attn_X"], "W_Q": a["L0_attn_W_Q"], "W_K": a["L0_attn_W_K"], "W_V": a["L0_attn_W_V"],
        "WrT": a["L0_ffn_Wr"].T, "br": a["L0_ffn_br"],
        "W1T": a["L0_ffn_W1"].transpose(0, 2, 1), "W2T": a["L0_ffn_W2"].transpose(0, 2, 1),
        "b1T": a["L0_ffn_b1"].reshape(EXPERTS, FC, P).transpose(2, 0, 1), "b2d": a["L0_ffn_b2"],
        "Wqkv1T": a["L1_attn_Wqkv"].T, "Wo1T": a["L1_attn_Wo"].T,
        "wqkv": a["L1_ffn_wqkv"], "wo": a["L1_ffn_wo"], "w1d": a["L1_ffn_w1"], "w2d": a["L1_ffn_w2"],
        "b1l": b1.reshape(2, UC, P, 2).transpose(0, 2, 3, 1), "b2l": a["L1_ffn_b2"],
        "qs": a["L1_ffn_q_scale"], "ks": a["L1_ffn_k_scale"],
        "lng": a["L1_ffn_ln_g"].reshape(2, DC, P).transpose(0, 2, 1), "lnb": a["L1_ffn_ln_b"].reshape(2, DC, P).transpose(0, 2, 1),
        "xpos0": tables["xpos0"], "decay": tables["decay"], "ranks": tables["ranks"], "iota": tables["iota"],
        "rope1": tables["rope1"], "rope2": tables["rope2"],
        "ident_d": tables["ident"], "shift_d": tables["shift"], "mask_d": tables["mask"],
    }
    nc = bacc.Bacc("TRN2", target_bir_lowering=False, num_devices=1)
    g = Shared(nc, ExitStack())
    arrays = {}
    views = {}
    for name, value in laid_out.items():
        value = np.ascontiguousarray(value)
        arrays[f"in_{name}"] = value
        views[name] = nc.dram_tensor(f"in_{name}", value.shape, mybir.dt.from_np(value.dtype), kind="ExternalInput").ap()
    g.take(views)
    g.out = nc.dram_tensor("out", (B, L, D), F32, kind="ExternalOutput").ap()
    build(nc, g)
    result = run_bass_kernel_spmd(nc, [arrays], core_ids=[0])
    return result.results[0]["out"]
```

```python
from contextlib import ExitStack

import numpy as np
import concourse.bass as bass
from concourse import mybir

F32 = mybir.dt.float32
F32R = mybir.dt.float32r
BF16 = mybir.dt.bfloat16
I32 = mybir.dt.int32
U32 = mybir.dt.uint32
ALU = mybir.AluOpType
ACT = mybir.ActivationFunctionType
AX = mybir.AxisListType.X

P = 128
B, L, D = 8, 512, 256
NT = L // P
DC = D // P
NS = 2
PAIRS = B // NS
TOK = B * L
TILES = TOK // P
EXPERTS, FF = 8, 1024
FC = FF // P
SLOTS = TILES + EXPERTS - 1
MAXSLOT = SLOTS + 1
ZEROED = 5
EPS = 1e-5
LOOP_SEMS = 150


class Chain:

    def __init__(self, eng, sem):
        self.eng, self.sem, self.n = eng, sem, 0

    def mark(self, ins):
        self.n += 1
        ins.then_inc(self.sem, 1)
        return self.n

    def step(self, ins):
        self.eng.wait_ge(self.sem, self.mark(ins))

    def wait(self, n):
        self.eng.wait_ge(self.sem, n)


def tile_stats(dve, chain, parts, stats, t):
    for i, src in enumerate(parts(t)):
        last = chain.mark(dve.bn_stats(stats[:, t, 6 * i:6 * i + 6], src))
    return last


def row_stats(dve, chain, var_ready, parts, stats, mv, ve, done=0):
    for t in range(done, NT):
        last = tile_stats(dve, chain, parts, stats, t)
    chain.wait(last)
    n = len(parts(0))
    for t in range(NT):
        last = chain.mark(dve.bn_aggr(mv[:, t, :], stats[:, t, 0:6 * n]))
    chain.wait(last)
    dve.tensor_scalar(ve[:, :], mv[:, :, 1], EPS, None, ALU.add).then_inc(var_ready, 1)


def normalised_rows(dve, rstd_ready, k, parts, mv, rstd, out):
    dve.wait_ge(rstd_ready, k)
    for t in range(NT):
        for src, dst in zip(parts(t), out(t)):
            yield dve.tensor_scalar(dst, src, mv[:, t, 0:1], rstd[:, t:t + 1], ALU.subtract, ALU.mult)


def phase_attn0(nc, g):
    with ExitStack() as ctx:
        def sb(name, shape, dt=F32):
            return ctx.enter_context(nc.sbuf_tensor(f"a_{name}", shape, dt))

        def stream(name, shape, dt=F32):
            return [sb(f"{name}{s}", shape, dt) for s in range(NS)]

        sems = []

        def sem(name):
            sems.append(ctx.enter_context(nc.semaphore(f"a_{name}", num=LOOP_SEMS + len(sems))))
            return sems[-1]

        def sem2(name):
            return [sem(f"{name}{s}") for s in range(NS)]

        wq = sb("wq", [P, DC, D])
        wk = sb("wk", [P, DC, D])
        wv = sb("wv", [P, DC, D])
        wr = sb("wr", [P, DC, EXPERTS])
        br = sb("br", [P, EXPERTS])
        xpos = sb("xpos", [P, 4, L])
        decay = sb("decay", [P, 7 * P])
        came = stream("came", [P, NT, D])
        x, xn = stream("x", [P, NT, D]), stream("xn", [P, NT, D])
        xnT = stream("xnT", [P, DC, L])
        qT, kT = stream("qT", [P, DC, L]), stream("kT", [P, DC, L])
        v = stream("v", [P, NT, D])
        prods = stream("prods", [P, 4, L])
        probs = stream("probs", [P, L])
        probsT = stream("probsT", [P, NT, P])
        stats, mv = stream("stats", [P, NT, 6]), stream("mv", [P, NT, 2])
        ve, rstd = stream("ve", [P, NT]), stream("rstd", [P, NT])
        nmax, rsum, rinv = stream("nmax", [P, NT]), stream("rsum", [P, NT]), stream("rinv", [P, NT])
        bank = [[ctx.enter_context(nc.psum_tensor(f"bank{s}{i}", [P, L], F32)) for i in range(4)]
                for s in range(NS)]

        consts_in = g.once("consts_in")
        x_moved = [g.once(f"x_moved{s}") for s in range(NS)]
        x_in = sem2("x_in")
        dve_chain, var_ready, rstd_ready = sem("dve_chain"), sem2("var_ready"), sem2("rstd_ready")
        xn_ready, xnT_psum, xnT_ready = sem2("xn_ready"), sem2("xnT_psum"), sem2("xnT_ready")
        qk_psum, qk_mults, qk_ready = sem2("qk_psum"), sem2("qk_mults"), sem2("qk_ready")
        v_psum, v_ready = sem2("v_psum"), sem2("v_ready")
        scores_ready, nmax_ready, probs_ready = sem2("scores_ready"), sem2("nmax_ready"), sem2("probs_ready")
        probsT_psum, probsT_ready = sem2("probsT_psum"), sem2("probsT_ready")
        o_psum, x1_ready = sem2("o_psum"), sem2("x1_ready")
        logits_psum, logits_read, kept = sem2("logits_psum"), sem2("logits_read"), sem2("kept")
        sem_range = range(sems[0].num, sems[-1].num + 1)
        assert len(sem_range) == len(sems)

        CONSTS = [(wq, g.W_Q.rearrange("(c p) n -> p c n", p=P)), (wk, g.W_K.rearrange("(c p) n -> p c n", p=P)),
                  (wv, g.W_V.rearrange("(c p) n -> p c n", p=P)), (wr, g.WrT.rearrange("(c p) n -> p c n", p=P)),
                  (br, g.br.partition_broadcast(P)), (xpos, g.xpos0), (decay, g.decay)]

        with nc.Block() as block:
            @block.sync
            def _(sp):
                for s in range(NS):
                    sp.dma_start(came[s][:], g.X[s].rearrange("(t p) n -> p t n", p=P)).then_inc(x_moved[s], 16)
                for s in range(NS):
                    sp.wait_ge(x_moved[s], 16)

            @block.scalar
            def _(act):
                for dst, src in CONSTS:
                    act.dma_start(dst[:], src).then_inc(consts_in, 16)

            @block.gpsimd
            def _(pool):
                pool.memset(g.minus_half[:], -0.5).then_inc(g.pool_consts, 1)
                pool.memset(g.zrow[:], 0.0).then_inc(g.pool_consts, 1)
                pool.wait_ge(g.pool_consts, 2)

        with nc.Fori(0, PAIRS) as pair:
            with nc.Block() as block:
                @block.sync
                def _(sp):
                    sp.wait_ge(qk_psum[0], 1)
                    for i in range(NS):
                        sp.dma_start(g.w1[:, bass.ds(pair * NS + i, 1)],
                                     g.W1T[bass.ds(pair * NS + i, 1)].rearrange("e (c p) f -> p e c f", p=P)).then_inc(g.w1_in, 16)
                    for i in range(MAXSLOT // PAIRS // ZEROED):
                        first = pair * (MAXSLOT // PAIRS * P) + i * ZEROED * P
                        sp.dma_start(g.xs_d[bass.ds(first, ZEROED * P), :].rearrange("(p a) n -> p (a n)", p=P), g.zrow[:]).then_inc(g.zeros_out, 16)
                    for s in range(NS):
                        sp.wait_ge(x1_ready[s], NT)
                        sp.dma_start(g.x1_d[pair * NS + s].rearrange("(t p) n -> p t n", p=P), x[s][:]).then_inc(x_moved[s], 16)
                        sp.dma_start(came[s][:], g.X[pair * NS + (NS + s)].rearrange("(t p) n -> p t n", p=P)).then_inc(x_in[s], 16)
                    for s in range(NS):
                        sp.wait_ge(x_in[s], 16)

                @block.vector
                def _(dve):
                    chain = Chain(dve, dve_chain)

                    def measure(s, rows):
                        row_stats(dve, chain, var_ready[s], lambda t: [rows[s][:, t, :]], stats[s], mv[s], ve[s])

                    def norm(s, rows, k):
                        for ins in normalised_rows(dve, rstd_ready[s], k, lambda t: [rows[s][:, t, :]], mv[s], rstd[s],
                                                   lambda t: [xn[s][:, t, :]]):
                            ins.then_inc(xn_ready[s], 1)

                    def rotate(s):
                        for i in range(2):
                            dve.wait_ge(qk_psum[s], i + 1)
                            even, odd = bank[s][2 * i], bank[s][2 * i + 1]
                            cos, sin = xpos[:, 2 * i, :], xpos[:, 2 * i + 1, :]
                            if i == 1:
                                dve.wait_ge(qk_ready[s], 2)
                            for j, (a, b) in enumerate([(even, cos), (odd, sin), (odd, cos), (even, sin)]):
                                dve.tensor_tensor(prods[s][:, j, :], a[:], b, ALU.mult).then_inc(qk_mults[s], 1)

                    def row_max(s, qt):
                        dve.wait_ge(scores_ready[s], qt + 1)
                        dve.tensor_reduce(nmax[s][:, qt:qt + 1], bank[s][qt % 2][:], AX, ALU.max, negate=True)\
                           .then_inc(nmax_ready[s], 1)

                    def decayed(s, qt):
                        dve.wait_ge(probsT_psum[s], qt + 1)
                        if qt:
                            dve.wait_ge(o_psum[s], qt)
                        dve.tensor_tensor(probsT[s][:].rearrange("p a b -> p (a b)"), bank[s][2][:],
                                          decay[:, qt * P:qt * P + L], ALU.mult).then_inc(probsT_ready[s], 1)

                    def residual(s, qt):
                        chain.step(dve.reciprocal(rinv[s][:, qt:qt + 1], rsum[s][:, qt:qt + 1]))
                        dve.wait_ge(o_psum[s], qt + 1)
                        dve.scalar_tensor_tensor(x[s][:, qt, :], bank[s][3][:, 0:D], rinv[s][:, qt:qt + 1],
                                                 came[s][:, qt, :], ALU.mult, ALU.add).then_inc(x1_ready[s], 1)

                    for s in range(NS):
                        measure(s, came)
                    for s in range(NS):
                        norm(s, came, 1)
                    dve.wait_ge(consts_in, 16 * len(CONSTS))
                    for s in range(NS):
                        dve.wait_ge(x_moved[s], pair * 16 + 16)
                    for s in range(NS):
                        rotate(s)
                    for qt in range(NT + 1):
                        for s in range(NS):
                            if qt < NT:
                                row_max(s, qt)
                            if qt:
                                decayed(s, qt - 1)
                        for s in range(NS):
                            if qt:
                                residual(s, qt - 1)
                    for s in range(NS):
                        dve.wait_ge(x1_ready[s], NT)
                        measure(s, x)
                    for s in range(NS):
                        norm(s, x, 2)
                    for s in range(NS):
                        dve.wait_ge(xn_ready[s], 2 * NT)
                        dve.tensor_copy(g.xn2[:, bass.ds(pair * (NS * NT) + s * NT, NT), :], xn[s][:]).then_inc(kept[s], 1)
                    for s in range(NS):
                        dve.wait_ge(logits_psum[s], 1)
                        dve.tensor_tensor(g.logits[:, bass.ds(pair * (NS * NT) + s * NT, NT), :],
                                          bank[s][2][:, 0:NT * EXPERTS].rearrange("p (t e) -> p t e", e=EXPERTS),
                                          br[:].unsqueeze(1).to_broadcast([P, NT, EXPERTS]), ALU.add).then_inc(logits_read[s], 1)

                @block.gpsimd
                def _(pool):
                    def power(s, k):
                        pool.wait_ge(var_ready[s], k)
                        pool.tensor_tensor(rstd[s][:], ve[s][:], g.minus_half[:, 0:NT], ALU.pow).then_inc(rstd_ready[s], 1)

                    for s in range(NS):
                        power(s, 1)
                    for s in range(NS):
                        for i, dst in enumerate([qT, kT]):
                            for j, op in enumerate([ALU.subtract, ALU.add]):
                                pool.wait_ge(qk_mults[s], 4 * i + 2 * j + 2)
                                pool.tensor_tensor(dst[s][:, j, :], prods[s][:, 2 * j, :], prods[s][:, 2 * j + 1, :], op)\
                                    .then_inc(qk_ready[s], 1)
                    for s in range(NS):
                        power(s, 2)

                @block.scalar
                def _(act):
                    def xnT_out(s, k):
                        for c in range(DC):
                            act.wait_ge(xnT_psum[s], 2 * k + c + 1)
                            act.activation(xnT[s][:, c, :], bank[s][c][:], ACT.Copy).then_inc(xnT_ready[s], 1)

                    for s in range(NS):
                        xnT_out(s, 0)
                    for s in range(NS):
                        for h in range(2):
                            act.wait_ge(v_psum[s], h + 1)
                            act.activation(v[s][:, 2 * h:2 * h + 2, :].rearrange("p a b -> p (a b)"), bank[s][h][:], ACT.Copy)\
                               .then_inc(v_ready[s], 1)
                    for qt in range(NT):
                        for s in range(NS):
                            act.wait_ge(nmax_ready[s], qt + 1)
                            if qt:
                                act.wait_ge(probsT_psum[s], qt)
                            act.activation(probs[s][:], bank[s][qt % 2][:], ACT.Exp, bias=nmax[s][:, qt:qt + 1],
                                           accum_out=rsum[s][:, qt:qt + 1]).then_inc(probs_ready[s], 1)
                    for s in range(NS):
                        xnT_out(s, 1)

                @block.tensor
                def _(pe):
                    def transposes(s, k):
                        for c in range(DC):
                            for t in range(NT):
                                if c == 0:
                                    pe.wait_ge(xn_ready[s], k * NT + t + 1)
                                last = pe.transpose(bank[s][c][:, t * P:(t + 1) * P], xn[s][:, t, c * P:(c + 1) * P], g.ident[:])
                            last.then_inc(xnT_psum[s], 1)

                    def project(s):
                        pe.wait_ge(xnT_ready[s], DC)
                        for i, w in enumerate([wq, wk]):
                            wp = w[:].rearrange("p c (n two) -> p c two n", two=2)
                            for j in range(2):
                                for c in range(DC):
                                    last = pe.matmul(bank[s][2 * i + j][:], wp[:, c, j, :], xnT[s][:, c, :],
                                                     start=c == 0, stop=c == DC - 1)
                            last.then_inc(qk_psum[s], 1)

                    def values(s):
                        pe.wait_ge(qk_mults[s], 4)
                        for t in range(NT):
                            for c in range(DC):
                                last = pe.matmul(bank[s][t // 2][:, (t % 2) * D:(t % 2 + 1) * D], xnT[s][:, c, t * P:(t + 1) * P],
                                                 wv[:, c, :], start=c == 0, stop=c == DC - 1)
                            if t % 2:
                                last.then_inc(v_psum[s], 1)

                    def scores(s, qt):
                        if qt == 0:
                            pe.wait_ge(qk_ready[s], 4)
                            pe.wait_ge(v_ready[s], 2)
                        if qt >= 2:
                            pe.wait_ge(probs_ready[s], qt - 1)
                        for c in range(DC):
                            last = pe.matmul(bank[s][qt % 2][:], qT[s][:, c, qt * P:(qt + 1) * P], kT[s][:, c, :],
                                             start=c == 0, stop=c == DC - 1)
                        last.then_inc(scores_ready[s], 1)

                    def flip(s, qt):
                        pe.wait_ge(probs_ready[s], qt + 1)
                        if qt:
                            pe.wait_ge(probsT_ready[s], qt)
                        for kt in range(NT):
                            last = pe.transpose(bank[s][2][:, (NT - 1 - kt) * P:(NT - kt) * P],
                                                probs[s][:, kt * P:(kt + 1) * P], g.ident[:])
                        last.then_inc(probsT_psum[s], 1)

                    def output(s, qt):
                        pe.wait_ge(probsT_ready[s], qt + 1)
                        if qt:
                            pe.wait_ge(x1_ready[s], qt)
                        for kt in range(NT):
                            last = pe.matmul(bank[s][3][:, 0:D], probsT[s][:, NT - 1 - kt, :], v[s][:, kt, :],
                                             start=kt == 0, stop=kt == NT - 1)
                        last.then_inc(o_psum[s], 1)

                    for s in range(NS):
                        transposes(s, 0)
                    pe.wait_ge(consts_in, 16 * len(CONSTS))
                    for s in range(NS):
                        project(s)
                    for s in range(NS):
                        values(s)
                    for qt in range(NT + 1):
                        for s in range(NS):
                            if qt < NT:
                                scores(s, qt)
                            if qt:
                                flip(s, qt - 1)
                        for s in range(NS):
                            if qt:
                                output(s, qt - 1)
                    for s in range(NS):
                        transposes(s, 1)
                    for s in range(NS):
                        pe.wait_ge(xnT_ready[s], 2 * DC)
                        for t in range(NT):
                            for c in range(DC):
                                last = pe.matmul(bank[s][2][:, t * EXPERTS:(t + 1) * EXPERTS], xnT[s][:, c, t * P:(t + 1) * P],
                                                 wr[:, c, :], start=c == 0, stop=c == DC - 1)
                        last.then_inc(logits_psum[s], 1)
            nc.all_engine_barrier(sems_to_clear=sem_range)

        with nc.Block() as block:
            @block.sync
            def _(sp):
                for s in range(NS):
                    sp.wait_ge(x_moved[s], 16 * (PAIRS + 1))


class Shared:

    def __init__(self, nc, ctx):
        self.nc, self.ctx = nc, ctx

    def take(self, v):
        self.X, self.W_Q, self.W_K, self.W_V, self.WrT, self.br = v["X"], v["W_Q"], v["W_K"], v["W_V"], v["WrT"], v["br"]
        self.W1T, self.W2T, self.b1T, self.b2d = v["W1T"], v["W2T"], v["b1T"], v["b2d"]
        self.Wqkv1T, self.Wo1T = v["Wqkv1T"], v["Wo1T"]
        self.wqkv, self.wo, self.w1d, self.w2d = v["wqkv"], v["wo"], v["w1d"], v["w2d"]
        self.b1l, self.b2l, self.qs, self.ks, self.lng, self.lnb = v["b1l"], v["b2l"], v["qs"], v["ks"], v["lng"], v["lnb"]
        self.xpos0, self.decay, self.ranks, self.iota = v["xpos0"], v["decay"], v["ranks"], v["iota"]
        self.rope1, self.rope2 = v["rope1"], v["rope2"]
        self.ident_d, self.shift_d, self.mask_d = v["ident_d"], v["shift_d"], v["mask_d"]

    def once(self, name):
        return self.ctx.enter_context(self.nc.semaphore(name))

    def keep(self, name, shape, dt=F32):
        return self.ctx.enter_context(self.nc.sbuf_tensor(name, shape, dt))


SLOT_LOOPS = 3
PER_LOOP = SLOTS // SLOT_LOOPS
assert PER_LOOP * SLOT_LOOPS == SLOTS


def phase_route(nc, g):
    TE = TILES * EXPERTS
    with ExitStack() as ctx:
        def sb(name, shape, dt=F32):
            return ctx.enter_context(nc.sbuf_tensor(f"m_{name}", shape, dt))

        ranks, iota = sb("ranks", [P, 2 * P]), sb("iota", [P, P])
        best, score = sb("best", [P, TILES]), sb("score", [P, TILES, EXPERTS])
        onehot = sb("onehot", [P, TILES, EXPERTS])
        order = sb("order", [P, EXPERTS])
        totals, upto = sb("totals", [P, EXPERTS, TILES]), sb("upto", [P, EXPERTS, TILES])
        ones, starts = sb("ones", [P, TILES]), sb("starts", [P, TILES])
        passed = sb("passed", [P, EXPERTS, TILES])
        slots_of, ends, base = sb("slots_of", [P, EXPERTS]), sb("ends", [P, EXPERTS]), sb("base", [P, EXPERTS])
        over, owner = sb("over", [P, MAXSLOT, EXPERTS]), sb("owner", [P, MAXSLOT])
        rows, row = sb("rows", [P, TILES, EXPERTS]), sb("row", [P, TILES])
        rank_psum = ctx.enter_context(nc.psum_tensor("rank_psum", [P, TE], F32))
        total_psum = ctx.enter_context(nc.psum_tensor("total_psum", [P, TE], F32))
        tables_in, dve_chain = g.once("tables_in"), g.once("rt_chain")
        onehot_ready, counted = g.once("onehot_ready"), g.once("counted")
        rows_ready, scattered = g.once("rows_ready"), g.once("scattered")

        with nc.Block() as block:
            @block.sync
            def _(sp):
                sp.dma_start(ranks[:], g.ranks).then_inc(tables_in, 16)
                sp.dma_start(iota[:], g.iota).then_inc(tables_in, 16)
                sp.dma_start(g.b1[:], g.b1T).then_inc(g.w1_in, 16)
                for e in range(EXPERTS):
                    sp.dma_start(g.w2[:, e], g.W2T[e].rearrange("(c p) n -> p c n", p=P)).then_inc(g.w2_in, 16)
                sp.dma_start(g.b2[:], g.b2d.partition_broadcast(P)).then_inc(g.w2_in, 16)

            @block.tensor
            def _(pe):
                pe.wait_ge(tables_in, 32)
                pe.wait_ge(onehot_ready, 1)
                oh = onehot[:].rearrange("p t e -> p (t e)")
                pe.matmul(rank_psum[:], ranks[:, 0:P], oh, start=True, stop=True)
                pe.matmul(total_psum[:], ranks[:, P:2 * P], oh, start=True, stop=True).then_inc(counted, 1)

            @block.vector
            def _(dve):
                chain = Chain(dve, dve_chain)
                step = chain.step

                def over_experts(a):
                    return a.unsqueeze(2).to_broadcast([P, a.shape[1], EXPERTS])

                dve.wait_ge(tables_in, 32)
                step(dve.memset(ones[:], 1.0))
                step(dve.tensor_reduce(best[:], g.logits[:], AX, ALU.max))
                step(dve.tensor_tensor(onehot[:], g.logits[:], over_experts(best[:]), ALU.is_equal))
                step(dve.tensor_scalar(order[:], iota[:, 0:EXPERTS], -1.0, float(EXPERTS), ALU.mult, ALU.add))
                step(dve.tensor_tensor(score[:], onehot[:], order[:].unsqueeze(1).to_broadcast([P, TILES, EXPERTS]), ALU.mult))
                step(dve.tensor_reduce(best[:], score[:], AX, ALU.max))
                dve.tensor_tensor(onehot[:], score[:], over_experts(best[:]), ALU.is_equal).then_inc(onehot_ready, 1)
                dve.wait_ge(counted, 1)
                step(dve.tensor_copy(totals[:], total_psum[:].rearrange("p (t e) -> p e t", e=EXPERTS)))
                for e in range(EXPERTS):
                    last = chain.mark(dve.tensor_tensor_scan(upto[:, e, :], ones[:], totals[:, e, :], 0.0, ALU.mult, ALU.add))
                chain.wait(last)
                step(dve.tensor_scalar(starts[:], iota[:, 0:TILES], float(P), None, ALU.mult))
                step(dve.tensor_tensor(passed[:], upto[:, :, TILES - 1:TILES].to_broadcast([P, EXPERTS, TILES]),
                                       starts[:].unsqueeze(1).to_broadcast([P, EXPERTS, TILES]), ALU.is_gt))
                step(dve.tensor_reduce(slots_of[:], passed[:], AX, ALU.add))
                step(dve.tensor_tensor_scan(ends[:], ones[:, 0:EXPERTS], slots_of[:], 0.0, ALU.mult, ALU.add))
                step(dve.tensor_tensor(base[:], ends[:], slots_of[:], ALU.subtract))
                step(dve.tensor_scalar(base[:], base[:], float(P), None, ALU.mult))
                step(dve.tensor_tensor(over[:], ends[:].unsqueeze(1).to_broadcast([P, MAXSLOT, EXPERTS]),
                                       iota[:, 0:MAXSLOT].unsqueeze(2).to_broadcast([P, MAXSLOT, EXPERTS]), ALU.is_le))
                step(dve.tensor_reduce(owner[:], over[:], AX, ALU.add))
                step(dve.tensor_scalar(g.owner[:], owner[:], float(EXPERTS - 1), None, ALU.min))
                step(dve.tensor_tensor(passed[:], upto[:], totals[:], ALU.subtract))
                step(dve.tensor_tensor(rows[:], rank_psum[:].rearrange("p (t e) -> p t e", e=EXPERTS),
                                       passed[:].rearrange("p e t -> p t e"), ALU.add))
                step(dve.tensor_tensor(rows[:], rows[:], base[:].unsqueeze(1).to_broadcast([P, TILES, EXPERTS]), ALU.add))
                step(dve.tensor_tensor(rows[:], rows[:], onehot[:], ALU.mult))
                step(dve.tensor_reduce(row[:], rows[:], AX, ALU.add))
                dve.memset(g.row_of[:, TILES:TILES + NS * NT], 0)
                dve.tensor_copy(g.row_of[:, 0:TILES], row[:]).then_inc(rows_ready, 1)

            @block.gpsimd
            def _(pool):
                pool.wait_ge(rows_ready, 1)
                pool.wait_ge(g.zeros_out, 16 * (MAXSLOT // ZEROED))
                for t in range(TILES):
                    pool.indirect_dma_start(g.xs_d, bass.IndirectOffsetOnAxis(ap=g.row_of[:, t:t + 1], axis=0),
                                            g.xn2[:, t, :], None).then_inc(scattered, 16)
                pool.wait_ge(scattered, 16 * TILES)


def phase_experts(nc, g):
    with ExitStack() as ctx:
        def sb(name, shape, dt=F32):
            return ctx.enter_context(nc.sbuf_tensor(f"m_{name}", shape, dt))

        sems = []

        def sem(name):
            sems.append(ctx.enter_context(nc.semaphore(f"m_{name}", num=LOOP_SEMS + len(sems))))
            return sems[-1]

        XB = 3
        xs = sb("xs", [P, XB, D])
        xsT = sb("xsT", [P, 2, DC, P])
        h_offset = -(-nc.sbuf_base // 32) * 32
        hT = sb("hT", [P, 2, FC, P])
        h_low = nc.alloc_sbuf_tensor_at("m_h_low", [P, 2, FC, P], F32R, offset=h_offset)
        h_high = sb("h_high", [P, FC, P], F32R)
        y = sb("y", [P, 2, D])
        b1s = sb("b1s", [P, 2, FC])
        W = DC * FF
        staged = g.xn2[:].rearrange("p t n -> p (t n)")
        w1s = [staged[:, k * W:(k + 1) * W].rearrange("p (c f) -> p c f", c=DC) for k in range(2)]
        w2_high_part = nc.alloc_sbuf_tensor_at("m_w2_high", [P, 2, FC, D], F32R, offset=g.xn2_offset + 2 * W * 4)
        w2_low_part = sb("w2_low", [P, 2, FC, D], F32R)
        xT_bank = [ctx.enter_context(nc.psum_tensor(f"xT_bank{i}", [P, 512], F32)) for i in range(2)]
        h_bank = [ctx.enter_context(nc.psum_tensor(f"h_bank{i}", [P, 4, P], F32)) for i in range(4)]
        y_bank = [ctx.enter_context(nc.psum_tensor(f"y_bank{i}", [P, 512], F32)) for i in range(2)]

        x_in = [sem(f"xs_in{i}") for i in range(XB)]
        xT_psum, xT_ready, w1_staged, w2_staged = sem("xT_psum"), sem("xT_ready"), sem("w1_staged"), sem("w2_staged")
        h_psum, h_done, y_psum, y_ready = sem("h_psum"), sem("h_done"), sem("y_psum"), sem("y_ready")
        h_split, h_ready, w2_split = sem("h_split"), sem("h_ready"), sem("w2_split")
        w2_rest = sem("w2_rest")
        y_out = [sem(f"y_out{i}") for i in range(2)]
        sem_range = range(sems[0].num, sems[-1].num + 1)
        N = PER_LOOP

        with nc.Fori(0, SLOT_LOOPS) as loop:
            with nc.Block() as block:
                @block.sync
                def _(sp):
                    def store(j):
                        sp.wait_ge(y_ready, j + 1)
                        sp.dma_start(g.ys_d[bass.ds((loop * N + j) * P, P), :], y[:, j % 2, :]).then_inc(y_out[j % 2], 16)

                    for j in range(N):
                        if j >= XB:
                            sp.wait_ge(xT_psum, j - XB + 1)
                        sp.dma_start(xs[:, j % XB, :], g.xs_d[bass.ds((loop * N + j) * P, P), :]).then_inc(x_in[j % XB], 16)
                        if j >= XB:
                            store(j - XB)
                    for j in range(N - XB, N):
                        store(j)
                    for k in range(2):
                        sp.wait_ge(y_out[k], 16 * ((N - k + 1) // 2))

                def low_w2(eng, j, owner, f):
                    return eng.tensor_tensor(w2_low_part[:, j % 2, f].unsqueeze(1), g.w2[:, bass.ds(owner, 1), f],
                                             w2_high_part[:, j % 2, f].unsqueeze(1).bitcast(F32), ALU.subtract)

                @block.vector
                def _(dve):
                    owner = [None] * 3

                    def stage_w1(j):
                        k = j % 2
                        owner[j % 3] = dve.value_load(g.owner[0:1, bass.ds(loop * N + j, 1)], min_val=0, max_val=EXPERTS - 1)
                        e = bass.ds(owner[j % 3], 1)
                        if j >= 2:
                            dve.wait_ge(h_done, 2 * (j - 1))
                        dve.tensor_copy(b1s[:, k, :].unsqueeze(1), g.b1[:, e, :]).then_inc(w1_staged, 1)
                        dve.tensor_copy(w1s[k].unsqueeze(1), g.w1[:, e]).then_inc(w1_staged, 1)

                    def stage_w2(j):
                        if j >= 2:
                            dve.wait_ge(y_psum, j - 1)
                        dve.tensor_copy(w2_high_part[:, j % 2].unsqueeze(1), g.w2[:, bass.ds(owner[j % 3], 1)]).then_inc(w2_split, 1)

                    def rest_w2(j):
                        dve.wait_ge(w2_split, j + 1)
                        low_w2(dve, j, owner[j % 3], slice(FC // 2, FC)).then_inc(w2_rest, 1)

                    def low_units(j):
                        for h in range(2):
                            f = slice(4 * h, 4 * h + 4)
                            dve.wait_ge(h_split, 2 * j + h + 1)
                            dve.tensor_tensor(h_low[:, j % 2, f, :], hT[:, j % 2, f, :], h_high[:, f, :].bitcast(F32), ALU.subtract)\
                               .then_inc(h_ready, 1)

                    def finish(j):
                        dve.wait_ge(y_psum, j + 1)
                        if j >= 2:
                            dve.wait_ge(y_out[j % 2], 16 * (j // 2))
                        dve.tensor_tensor(y[:, j % 2, :].unsqueeze(1), y_bank[j % 2][:, 0:D].unsqueeze(1),
                                          g.b2[:, bass.ds(owner[j % 3], 1), :], ALU.add).then_inc(y_ready, 1)

                    dve.wait_ge(g.w1_in, 16 * (EXPERTS + 1))
                    stage_w1(0)
                    dve.wait_ge(g.w2_in, 16 * (EXPERTS + 1))
                    stage_w2(0)
                    stage_w1(1)
                    rest_w2(0)
                    stage_w2(1)
                    for j in range(2, N):
                        low_units(j - 2)
                        stage_w1(j)
                        rest_w2(j - 1)
                        finish(j - 2)
                        stage_w2(j)
                    rest_w2(N - 1)
                    for j in range(N - 2, N):
                        low_units(j)
                        finish(j)

                @block.gpsimd
                def _(pool):
                    for j in range(N):
                        e = pool.value_load(g.owner[0:1, bass.ds(loop * N + j, 1)], min_val=0, max_val=EXPERTS - 1)
                        pool.wait_ge(w2_split, j + 1)
                        low_w2(pool, j, e, slice(0, FC // 2)).then_inc(w2_staged, 1)

                @block.scalar
                def _(act):
                    def xT_out(j):
                        act.wait_ge(xT_psum, j + 1)
                        if j >= 2:
                            act.wait_ge(h_psum, 2 * (j - 1))
                        act.activation(xsT[:, j % 2].rearrange("p c n -> p (c n)"), xT_bank[j % 2][:, 0:DC * P], ACT.Copy)\
                           .then_inc(xT_ready, 1)

                    def split(j):
                        if j:
                            act.wait_ge(y_psum, j)
                        for h in range(2):
                            f = slice(4 * h, 4 * h + 4)
                            act.wait_ge(h_done, 2 * j + h + 1)
                            act.activation(h_high[:, f, :], hT[:, j % 2, f, :], ACT.Copy).then_inc(h_split, 1)

                    xT_out(0)
                    for j in range(N):
                        if j:
                            split(j - 1)
                        if j + 1 < N:
                            xT_out(j + 1)
                        act.wait_ge(w1_staged, 2 * (j + 1))
                        if j >= 2:
                            act.wait_ge(y_psum, j - 1)
                        for h in range(2):
                            act.wait_ge(h_psum, 2 * j + h + 1)
                            for f in range(4):
                                last = act.activation(hT[:, j % 2, 4 * h + f, :], h_bank[2 * (j % 2) + h][:, f, :], ACT.Relu,
                                                      bias=b1s[:, j % 2, 4 * h + f:4 * h + f + 1])
                            last.then_inc(h_done, 1)
                    split(N - 1)

                @block.tensor
                def _(pe):
                    def flip(j):
                        pe.wait_ge(x_in[j % XB], 16 * (j // XB + 1))
                        if j >= 2:
                            pe.wait_ge(xT_ready, j - 1)
                        for c in range(DC):
                            last = pe.transpose(xT_bank[j % 2][:, c * P:(c + 1) * P], xs[:, j % XB, c * P:(c + 1) * P], g.ident[:])
                        last.then_inc(xT_psum, 1)

                    def up(j):
                        pe.wait_ge(xT_ready, j + 1)
                        pe.wait_ge(w1_staged, 2 * (j + 1))
                        if j >= 2:
                            pe.wait_ge(h_done, 2 * (j - 1))
                        for h in range(2):
                            for f in range(4):
                                for c in range(DC):
                                    last = pe.matmul(h_bank[2 * (j % 2) + h][:, f, :], w1s[j % 2][:, c, (4 * h + f) * P:(4 * h + f + 1) * P],
                                                     xsT[:, j % 2, c, :], start=c == 0, stop=c == DC - 1)
                            last.then_inc(h_psum, 1)

                    def down(j):
                        pe.wait_ge(h_ready, 2 * (j + 1))
                        pe.wait_ge(w2_staged, j + 1)
                        pe.wait_ge(w2_rest, j + 1)
                        if j >= 2:
                            pe.wait_ge(y_ready, j - 1)
                        for f in range(FC):
                            y_out_bank, h_hi, w_hi = y_bank[j % 2][:, 0:D], h_high[:, f, :], w2_high_part[:, j % 2, f, :]
                            pe.matmul(y_out_bank, h_hi, w_hi, start=f == 0, stop=False)
                            pe.matmul(y_out_bank, h_hi, w2_low_part[:, j % 2, f, :], start=False, stop=False)
                            last = pe.matmul(y_out_bank, h_low[:, j % 2, f, :], w_hi, start=False, stop=f == FC - 1)
                        last.then_inc(y_psum, 1)

                    flip(0)
                    for j in range(N + 1):
                        if j + 1 < N:
                            flip(j + 1)
                        if j < N:
                            up(j)
                        if j:
                            down(j - 1)
            nc.all_engine_barrier(sems_to_clear=sem_range)


H1, DH1 = 16, 16
HG = 4
GROUPS = H1 // HG
HP = H1 // 2


def phase_attn1(nc, g):
    with ExitStack() as ctx:
        def sb(name, shape, dt=F32):
            return ctx.enter_context(nc.sbuf_tensor(f"c_{name}", shape, dt))

        def stream(name, shape, dt=F32):
            return [sb(f"{name}{s}", shape, dt) for s in range(NS)]

        sems = []

        def sem(name):
            sems.append(ctx.enter_context(nc.semaphore(f"c_{name}", num=LOOP_SEMS + len(sems))))
            return sems[-1]

        def sem2(name):
            return [sem(f"{name}{s}") for s in range(NS)]

        QK = 2 * D
        PB = 3
        w = sb("wqkv1", [P, DC, 3 * D])
        wo = sb("wo1", [P, DC, D])
        rope = sb("rope1", [P, NT, 2, 2, DH1])
        x, xn = stream("cx", [P, NT, D]), stream("cxn", [P, NT, D])
        came, yrow = stream("came", [P, NT, D]), stream("yrow", [P, NT, D])
        rowb = stream("rowb", [P, NT], I32)
        xnT = stream("cxnT", [P, DC, L])
        cosed, sined = stream("cosed", [P, QK]), stream("sined", [P, QK])
        qhl = stream("qhl", [P, H1, 4, DH1], F32R)
        khl = stream("khl", [P, H1, 4, DH1], F32R)
        qT, kT = stream("cqT", [P, HP, L], F32R), stream("ckT", [P, HP, L], F32R)
        v = stream("cv", [P, NT, H1, 2 * DH1])
        probs, probsT = stream("cprobs", [P, PB, L]), stream("cprobsT", [P, 2, NT, P])
        raw = stream("raw", [P, NT, GROUPS, P])
        y0 = [a[:, 0:DC].rearrange("p a b n -> p (a b n)").rearrange("p (t n) -> p t n", n=D) for a in raw]
        o, oT = stream("o", [P, NT, D]), xnT
        stats, mv = stream("cstats", [P, NT, 6]), stream("cmv", [P, NT, 2])
        ve, rstd = stream("cve", [P, NT]), stream("crstd", [P, NT])
        nmax, rinv = (stream(n, [P, NT, H1]) for n in ("cnmax", "crinv"))
        identr = sb("identr", [P, P], F32R)
        bank = [[ctx.enter_context(nc.psum_tensor(f"cbank{s}{i}", [P, L], F32)) for i in range(4)]
                for s in range(NS)]

        c_in, c_set = g.once("c_in"), g.once("c_set")
        y_in = [g.once(f"rows_in{s}") for s in range(NS)]
        x_stored, y_stored = ([g.once(f"{n}_stored{s}") for s in range(NS)] for n in ("x3", "y0"))
        first_in, row_first = g.once("x1_first_in"), g.once("row_first")
        x_in, row_copied = sem2("cx_in"), sem2("row_copied")
        x2_ready, dve_chain, var_ready, rstd_ready = sem2("x2_ready"), sem("c_chain"), sem2("cvar"), sem2("crstd")
        xn_ready, xnT_psum, xnT_ready = sem2("cxn_ready"), sem2("cxnT_psum"), sem2("cxnT_ready")
        qk_psum, v_psum, v_ready = sem2("cqk_psum"), sem2("cv_psum"), sem2("cv_ready")
        turned, rotated, high_ready = sem2("turned"), sem2("rotated"), sem2("high_ready")
        q_split, k_split = sem2("q_split"), sem2("k_split")
        qkT_psum, qkT_ready = sem2("qkT_psum"), sem2("qkT_ready")
        scores_ready, nmax_ready, probs_ready = sem2("cscores"), sem2("cnmax_r"), sem2("cprobs_r")
        pT_psum, pT_ready, pv_done, o_ready = sem2("pT_psum"), sem2("pT_ready"), sem2("pv_done"), sem2("o_ready")
        oT_psum, oT_ready, raw_ready, raw_psum = sem2("oT_psum"), sem2("oT_ready"), sem2("raw_ready"), sem2("raw_psum")
        wo_psum, x3_ready = sem2("wo_psum"), sem2("x3_ready")
        sem_range = range(sems[0].num, sems[-1].num + 1)
        assert len(sem_range) == len(sems)

        def kw(qt):
            return max(2, qt + 1) * P

        turns = [(s, t) for t in range(NT) for s in range(NS)]
        LAG = 3
        order = list(reversed(range(NT)))
        units = [unit for qt in order for unit in ([(qt, 4 * i + a, 2) for i in range(H1 // 4) for a in range(2)] if qt < 2 else
                                                   [(qt, h, 1) for h in range(H1)])]
        UNITS = len(units)
        ends = [max(u for u in range(UNITS) if units[u][0] == qt) + 1 for qt in order]

        def taken_by_dve(s, u):
            return s == 0

        def gather(pool, s):
            for t in range(NT):
                pool.indirect_dma_start(yrow[s][:, t, :], None, g.ys_d,
                                        bass.IndirectOffsetOnAxis(ap=rowb[s][:, t:t + 1], axis=0)).then_inc(y_in[s], 16)

        with nc.Block() as block:
            @block.sync
            def _(sp):
                for s in range(NS):
                    sp.dma_start(came[s][:], g.x1_d[s].rearrange("(t p) n -> p t n", p=P)).then_inc(first_in, 16)
                sp.wait_ge(c_set, 1 + NS)
                for s in range(NS):
                    for i, done in enumerate((x_stored[s], y_stored[s])):
                        sp.dma_start(g.x1_d[B + s, i * 2 * P:(i + 1) * 2 * P].rearrange("(p a) n -> p (a n)", p=P),
                                     v[s][:, 0].rearrange("p h d -> p (h d)")).then_inc(done, 16)
                sp.dma_start(w[:], g.Wqkv1T.rearrange("(c p) n -> p c n", p=P)).then_inc(c_in, 16)
                sp.dma_start(rope[:], g.rope1).then_inc(c_in, 16)
                sp.dma_start(wo[:], g.Wo1T.rearrange("(c p) n -> p c n", p=P)).then_inc(c_in, 16)
                for s in range(NS):
                    sp.wait_ge(x_stored[s], 16)
                    sp.wait_ge(y_stored[s], 16)
                sp.wait_ge(first_in, 16 * NS)
                sp.wait_ge(c_in, 48)

            @block.gpsimd
            def _(pool):
                for s in range(NS):
                    pool.tensor_copy(rowb[s][:], g.row_of[:, s * NT:(s + 1) * NT]).then_inc(row_first, 1)
                pool.wait_ge(row_first, NS)
                for s in range(NS):
                    gather(pool, s)

            @block.vector
            def _(dve):
                dve.tensor_copy(identr[:], g.ident[:]).then_inc(c_set, 1)
                for s in range(NS):
                    dve.memset(v[s][:], 0.0).then_inc(c_set, 1)
                for s in range(NS):
                    dve.wait_ge(x_stored[s], 16)
                    dve.wait_ge(y_stored[s], 16)
                    dve.memset(v[s][:, :, :, DH1:DH1 + 1], 1.0).then_inc(c_set, 1)
                dve.wait_ge(c_set, 1 + 2 * NS)

        with nc.Fori(0, PAIRS) as pair:
            with nc.Block() as block:
                @block.sync
                def _(sp):
                    for s in range(NS):
                        sp.wait_ge(x2_ready[s], 1)
                        sp.dma_start(came[s][:], g.x1_d[pair * NS + (NS + s)].rearrange("(t p) n -> p t n", p=P)).then_inc(x_in[s], 16)
                    for s in range(NS):
                        sp.wait_ge(x3_ready[s], NT)
                        sp.dma_start(g.x3_d[pair * NS + s].rearrange("(t p) n -> p t n", p=P), x[s][:]).then_inc(x_stored[s], 16)
                    for s in range(NS):
                        sp.wait_ge(xn_ready[s], 2 * NT)
                        sp.dma_start(g.y_d[0][pair * NS + s].rearrange("(t p) n -> p t n", p=P), y0[s]).then_inc(y_stored[s], 16)
                    for s in range(NS):
                        sp.wait_ge(x_in[s], 16)

                @block.gpsimd
                def _(pool):
                    def power(s, k):
                        pool.wait_ge(var_ready[s], k)
                        pool.tensor_tensor(rstd[s][:], ve[s][:], g.minus_half[:, 0:NT], ALU.pow).then_inc(rstd_ready[s], 1)

                    for s in range(NS):
                        power(s, 1)
                    def low_q(s, t):
                        pool.wait_ge(high_ready[s], 2 * t + 1)
                        src, high = cosed[s][:, 0:D].rearrange("p (h d) -> p h d", d=DH1), qhl[s][:, :, 0::2, :]
                        pool.tensor_tensor(qhl[s][:, :, 1::2, :], src.unsqueeze(2).to_broadcast([P, H1, 2, DH1]), high.bitcast(F32), ALU.subtract)\
                            .then_inc(q_split[s], 1)

                    for t in range(NT):
                        for s in range(NS):
                            pool.wait_ge(turned[s], 3 * (t + 1))
                            pool.tensor_tensor(cosed[s][:], cosed[s][:], sined[s][:], ALU.add).then_inc(rotated[s], 1)
                            if t or s:
                                low_q(*((s - 1, t) if s else (NS - 1, t - 1)))
                    low_q(NS - 1, NT - 1)
                    for s in range(NS):
                        pool.wait_ge(x2_ready[s], 1)
                        pool.tensor_copy(rowb[s][:], g.row_of[:, bass.ds(pair * (NS * NT) + (NS + s) * NT, NT)]).then_inc(row_copied[s], 1)
                    for s in range(NS):
                        pool.wait_ge(row_copied[s], 1)
                        gather(pool, s)
                    for s in range(NS):
                        power(s, 2)

                @block.vector
                def _(dve):
                    chain = Chain(dve, dve_chain)

                    def measure(s, done=0):
                        row_stats(dve, chain, var_ready[s], lambda t: [x[s][:, t, :]], stats[s], mv[s], ve[s], done)

                    def norm(s, k):
                        out = xn[s] if k == 1 else y0[s]
                        for ins in normalised_rows(dve, rstd_ready[s], k, lambda t: [x[s][:, t, :]], mv[s], rstd[s],
                                                   lambda t: [out[:, t, :]]):
                            ins.then_inc(xn_ready[s], 1)

                    def turn(s, t):
                        if t == 1:
                            dve.wait_ge(y_stored[s], pair * 16 + 16)
                        dve.wait_ge(qk_psum[s], t + 1)
                        if t:
                            dve.wait_ge(k_split[s], t)
                            dve.wait_ge(q_split[s], t)
                        def heads(a):
                            return a.rearrange("p (i h d) -> p i h d", i=2, d=DH1)

                        src, out = heads(bank[s][0][:]), heads(sined[s][:])
                        dve.tensor_tensor(heads(cosed[s][:]), src, rope[:, t, :, 0, :].unsqueeze(2).to_broadcast([P, 2, H1, DH1]),
                                          ALU.mult).then_inc(turned[s], 1)
                        for a in range(2):
                            dve.tensor_tensor(out[:, :, :, a::2], src[:, :, :, 1 - a::2],
                                              rope[:, t, :, 1, a::2].unsqueeze(2).to_broadcast([P, 2, H1, DH1 // 2]),
                                              ALU.mult).then_inc(turned[s], 1)

                    def parts(s, t):
                        dve.wait_ge(rotated[s], t + 1)
                        if t:
                            dve.wait_ge(qkT_psum[s], 4 * t)
                        q = cosed[s][:, 0:D].rearrange("p (h d) -> p h d", d=DH1)
                        k = cosed[s][:, D:QK].rearrange("p (h d) -> p h d", d=DH1)
                        twice = [P, H1, 2, DH1]
                        hi = [(qhl[s][:, :, 0::2, :], q), (khl[s][:, :, 0:2, :], k)]
                        for dst, src in hi:
                            dve.tensor_copy(dst, src.unsqueeze(2).to_broadcast(twice)).then_inc(high_ready[s], 1)
                        dve.wait_ge(high_ready[s], 2 * (t + 1))
                        dve.tensor_tensor(khl[s][:, :, 2:4, :], k.unsqueeze(2).to_broadcast(twice), khl[s][:, :, 0:2, :].bitcast(F32), ALU.subtract)\
                           .then_inc(k_split[s], 1)

                    def row_max(s, u):
                        qt, h, n = units[u]
                        dve.wait_ge(scores_ready[s], u + 1)
                        S = bank[s][u % 2][:] if n == 1 else bank[s][u % 2][:].rearrange("p (h k) -> p h k", h=n)
                        S = S[:, 0:(qt + 1) * P].unsqueeze(1) if n == 1 else S[:, :, 0:(qt + 1) * P]
                        dve.tensor_reduce(nmax[s][:, qt, h:h + 2 * n - 1:2], S, AX, ALU.max, negate=True).then_inc(nmax_ready[s], 1)

                    def pT_out(s, u):
                        qt, h, n = units[u]
                        dve.wait_ge(pT_psum[s], u + 1)
                        if u >= 2:
                            dve.wait_ge(pv_done[s], u - 1)
                        w = n * (qt + 1)
                        dve.tensor_copy(probsT[s][:, u % 2, 0:w, :], bank[s][2][:, 0:w * P].rearrange("p (a b) -> p a b", b=P)).then_inc(pT_ready[s], 1)

                    def outputs(s, i):
                        qt = order[i]
                        dve.wait_ge(raw_psum[s], i + 1)
                        heads = bank[s][i % 2][:].rearrange("p (h d) -> p h d", d=2 * DH1)
                        chain.step(dve.reciprocal(rinv[s][:, qt, :].unsqueeze(2), heads[:, :, DH1:DH1 + 1]))
                        dve.tensor_tensor(o[s][:, qt, :].rearrange("p (h d) -> p h d", d=DH1),
                                          heads[:, :, 0:DH1],
                                          rinv[s][:, qt, :].unsqueeze(2).to_broadcast([P, H1, DH1]), ALU.mult).then_inc(o_ready[s], 1)

                    for s in range(NS):
                        dve.wait_ge(x_stored[s], pair * 16 + 16)
                        dve.wait_ge(y_in[s], pair * (16 * NT) + 16 * NT)
                        dve.tensor_tensor(x[s][:], came[s][:], yrow[s][:], ALU.add).then_inc(x2_ready[s], 1)
                        dve.wait_ge(x2_ready[s], 1)
                        measure(s)
                    for s in range(NS):
                        norm(s, 1)
                    for i in range(len(turns) + 1):
                        if i < len(turns):
                            turn(*turns[i])
                        if i:
                            parts(*turns[i - 1])
                    for u in range(UNITS + 2):
                        for s in range(NS):
                            if u < UNITS:
                                row_max(s, u)
                        for s in range(NS):
                            if 2 <= u < UNITS + 2 and taken_by_dve(s, u - 2):
                                pT_out(s, u - 2)
                    for s in range(NS):
                        for i in range(NT):
                            outputs(s, i)
                    def residual(s, t):
                        dve.wait_ge(wo_psum[s], t + 1)
                        dve.tensor_tensor(x[s][:, t, :], bank[s][t % 2][:, 0:D], x[s][:, t, :], ALU.add).then_inc(x3_ready[s], 1)

                    def ahead(s, t):
                        dve.wait_ge(x3_ready[s], t + 1)
                        tile_stats(dve, chain, lambda t: [x[s][:, t, :]], stats[s], t)

                    for t in range(NT):
                        residual(0, t)
                        if t:
                            ahead(0, t - 1)
                    residual(1, 0)
                    dve.wait_ge(x3_ready[0], NT)
                    measure(0, NT - 1)
                    residual(1, 1)
                    ahead(1, 0)
                    residual(1, 2)
                    ahead(1, 1)
                    norm(0, 2)
                    residual(1, 3)
                    ahead(1, 2)
                    dve.wait_ge(x3_ready[1], NT)
                    measure(1, NT - 1)
                    norm(1, 2)

                @block.scalar
                def _(act):
                    for s in range(NS):
                        for c in range(DC):
                            act.wait_ge(xnT_psum[s], c + 1)
                            act.activation(xnT[s][:, c, :], bank[s][c][:], ACT.Copy).then_inc(xnT_ready[s], 1)

                    def qkT_out(s, t, i):
                        act.wait_ge(qkT_psum[s], 4 * t + i + 1)
                        dst = (qT, kT)[i // 2][s]
                        act.activation(dst[:, 4 * (i % 2):4 * (i % 2) + 4, t * P:(t + 1) * P],
                                       bank[s][2 + i % 2][:].rearrange("p (a b) -> p a b", b=P), ACT.Copy).then_inc(qkT_ready[s], 1)

                    for i in range(len(turns) + LAG):
                        if i >= LAG:
                            for j in range(4):
                                qkT_out(*turns[i - LAG], j)
                        if i < len(turns):
                            s, t = turns[i]
                            act.wait_ge(v_psum[s], t + 1)
                            act.activation(v[s][:, t, :, 0:DH1], bank[s][1][:, 0:D].rearrange("p (h d) -> p h d", d=DH1), ACT.Copy)\
                               .then_inc(v_ready[s], 1)

                    def exps(s, u):
                        qt, h, n = units[u]
                        w = (qt + 1) * P
                        act.wait_ge(nmax_ready[s], u + 1)
                        if u >= PB:
                            act.wait_ge(pT_psum[s], u - PB + 1)
                        for j in range(n):
                            last = act.activation(probs[s][:, u % PB, j * w:(j + 1) * w], bank[s][u % 2][:, j * 2 * P:j * 2 * P + w], ACT.Exp,
                                                  bias=nmax[s][:, qt, h + 2 * j:h + 2 * j + 1])
                        last.then_inc(probs_ready[s], 1)

                    def pT_out(s, u):
                        qt, h, n = units[u]
                        act.wait_ge(pT_psum[s], u + 1)
                        if u >= 2:
                            act.wait_ge(pv_done[s], u - 1)
                        w = n * (qt + 1)
                        act.activation(probsT[s][:, u % 2, 0:w, :], bank[s][2][:, 0:w * P].rearrange("p (a b) -> p a b", b=P), ACT.Copy)\
                           .then_inc(pT_ready[s], 1)

                    for u in range(UNITS + 3):
                        for s in range(NS):
                            if u < UNITS:
                                exps(s, u)
                        for s in range(NS):
                            if 2 <= u < UNITS + 2 and not taken_by_dve(s, u - 2):
                                pT_out(s, u - 2)
                        for s in range(NS):
                            if u - 2 in ends:
                                act.wait_ge(pv_done[s], u - 2)
                                act.activation(raw[s][:, order[ends.index(u - 2)]].rearrange("p a b -> p (a b)"), bank[s][3][:], ACT.Copy).then_inc(raw_ready[s], 1)
                    for s in range(NS):
                        for c in range(DC):
                            act.wait_ge(oT_psum[s], c + 1)
                            act.activation(oT[s][:, c, :], bank[s][2 + c][:], ACT.Copy).then_inc(oT_ready[s], 1)

                @block.tensor
                def _(pe):
                    def transposes(s):
                        for c in range(DC):
                            for t in range(NT):
                                if c == 0:
                                    pe.wait_ge(xn_ready[s], t + 1)
                                last = pe.transpose(bank[s][c][:, t * P:(t + 1) * P], xn[s][:, t, c * P:(c + 1) * P], g.ident[:])
                            last.then_inc(xnT_psum[s], 1)

                    def project(s, t):
                        if t == 0:
                            pe.wait_ge(xnT_ready[s], DC)
                        else:
                            pe.wait_ge(turned[s], 3 * t)
                        for c in range(DC):
                            last = pe.matmul(bank[s][0][:], xnT[s][:, c, t * P:(t + 1) * P], w[:, c, 0:QK], start=c == 0, stop=c == DC - 1)
                        last.then_inc(qk_psum[s], 1)

                    def project_v(s, t):
                        if t:
                            pe.wait_ge(v_ready[s], t)
                        for c in range(DC):
                            last = pe.matmul(bank[s][1][:, 0:D], xnT[s][:, c, t * P:(t + 1) * P], w[:, c, QK:3 * D], start=c == 0, stop=c == DC - 1)
                        last.then_inc(v_psum[s], 1)

                    def flip_qk(s, t, which):
                        pe.wait_ge((q_split, k_split)[which][s], t + 1)
                        for i in (2 * which, 2 * which + 1):
                            if 4 * t + i >= 2:
                                pe.wait_ge(qkT_ready[s], 4 * t + i - 1)
                            out = bank[s][2 + i % 2]
                            for a in range(4):
                                p = 4 * (i % 2) + a
                                src = (qhl, khl)[i // 2][s][:, 2 * p:2 * p + 2].rearrange("p h a d -> p (h a d)")
                                last = pe.transpose(out[:, a * P:(a + 1) * P].bitcast(F32R), src, identr[:])
                            last.then_inc(qkT_psum[s], 1)

                    def scores(s, u):
                        qt, h, n = units[u]
                        if u == 0:
                            pe.wait_ge(qkT_ready[s], 4 * NT)
                            pe.wait_ge(v_ready[s], NT)
                        if u >= 2:
                            pe.wait_ge(probs_ready[s], u - 1)
                        for j in range(n):
                            r, p = slice(64 * (h % 2), 64 * (h % 2) + 64), h // 2 + j
                            S = bank[s][u % 2][:, j * 2 * P:]
                            pe.matmul(S[:, 0:kw(qt)], qT[s][r, p, qt * P:(qt + 1) * P], kT[s][r, p, 0:kw(qt)], start=True, stop=False)
                            last = pe.matmul(S[:, qt * P:(qt + 1) * P], g.mask[:, 0, :], g.mask[:, 2, :], start=False, stop=True)
                        last.then_inc(scores_ready[s], 1)

                    def flip(s, u):
                        qt, h, n = units[u]
                        pe.wait_ge(probs_ready[s], u + 1)
                        if u:
                            pe.wait_ge(pT_ready[s], u)
                        for k in range(n * (qt + 1)):
                            last = pe.transpose(bank[s][2][:, k * P:(k + 1) * P], probs[s][:, u % PB, k * P:(k + 1) * P], g.ident[:])
                        last.then_inc(pT_psum[s], 1)

                    def output(s, u):
                        qt, h, n = units[u]
                        pe.wait_ge(pT_ready[s], u + 1)
                        if u in ends:
                            pe.wait_ge(raw_ready[s], ends.index(u) + 1)
                        for j in range(n):
                            i, r = (h + 2 * j) // HG, 32 * ((h + 2 * j) % HG)
                            for kt in range(qt + 1):
                                last = pe.matmul(bank[s][3][r:r + 32, i * P:(i + 1) * P], v[s][:, kt, h + 2 * j, :], probsT[s][:, u % 2, j * (qt + 1) + kt, :],
                                                 start=kt == 0, stop=kt == qt, tile_position=(0, r))
                        last.then_inc(pv_done[s], 1)

                    for s in range(NS):
                        transposes(s)
                    for i in range(len(turns) + LAG):
                        for j, work in enumerate((project, project_v)):
                            if i >= LAG:
                                flip_qk(*turns[i - LAG], j)
                            if i < len(turns):
                                work(*turns[i])
                    for u in range(UNITS + 3):
                        for s in range(NS):
                            if u < UNITS:
                                scores(s, u)
                        for s in range(NS):
                            if u >= 3:
                                output(s, u - 3)
                        for s in range(NS):
                            if 2 <= u < UNITS + 2:
                                flip(s, u - 2)
                    for s in range(NS):
                        for k, qt in enumerate(order):
                            pe.wait_ge(raw_ready[s], k + 1)
                            if k >= 2:
                                pe.wait_ge(o_ready[s], k - 1)
                            for i in range(GROUPS):
                                last = pe.transpose(bank[s][k % 2][:, i * P:(i + 1) * P], raw[s][:, qt, i, :], g.ident[:])
                            last.then_inc(raw_psum[s], 1)
                    for s in range(NS):
                        pe.wait_ge(o_ready[s], NT)
                        for c in range(DC):
                            for t in range(NT):
                                last = pe.transpose(bank[s][2 + c][:, t * P:(t + 1) * P], o[s][:, t, c * P:(c + 1) * P], g.ident[:])
                            last.then_inc(oT_psum[s], 1)
                        pe.wait_ge(oT_ready[s], DC)
                        for t in range(NT):
                            if t >= 2:
                                pe.wait_ge(x3_ready[s], t - 1)
                            for c in range(DC):
                                last = pe.matmul(bank[s][t % 2][:, 0:D], oT[s][:, c, t * P:(t + 1) * P], wo[:, c, :], start=c == 0, stop=c == DC - 1)
                            last.then_inc(wo_psum[s], 1)
            nc.all_engine_barrier(sems_to_clear=sem_range)

        with nc.Block() as block:
            @block.sync
            def _(sp):
                for s in range(NS):
                    sp.wait_ge(x_stored[s], 16 * (PAIRS + 1))
                    sp.wait_ge(y_stored[s], 16 * (PAIRS + 1))

            @block.gpsimd
            def _(pool):
                for s in range(NS):
                    pool.wait_ge(y_in[s], 16 * NT * (PAIRS + 1))


H2, DH2 = 8, 64
INNER = H2 * DH2
HP2 = H2 // 2
HID = 682
UC = (HID + P - 1) // P


def phase_layer(nc, g, layer):
    final = layer == 1
    with ExitStack() as ctx:
        def sb(name, shape, dt=F32):
            return ctx.enter_context(nc.sbuf_tensor(f"l{layer}_{name}", shape, dt))

        def stream(name, shape, dt=F32):
            return [sb(f"{name}{s}", shape, dt) for s in range(NS)]

        def paired(name, shape, other, other_shape):
            offset = -(-nc.sbuf_base // 32) * 32
            first = sb(name, shape)
            assert int(np.prod(shape)) >= int(np.prod(other_shape))
            return first, nc.alloc_sbuf_tensor_at(f"l{layer}_{other}", other_shape, F32R, offset=offset)

        def paired_streams(name, shape, other, other_shape):
            return zip(*[paired(f"{name}{s}", shape, f"{other}{s}", other_shape) for s in range(NS)])

        sems = []

        def sem(name):
            sems.append(ctx.enter_context(nc.semaphore(f"l{layer}_{name}", num=LOOP_SEMS + len(sems))))
            return sems[-1]

        def sem2(name):
            return [sem(f"{name}{s}") for s in range(NS)]

        def weight(name, shape):
            raw, low = paired(f"{name}_raw", shape, f"{name}_low", shape)
            return raw, [low, sb(f"{name}_high", shape, F32R)]

        wqkv_raw, wqkv = weight("wqkv", [P, DC, 3 * INNER])
        w1_raw, w1 = weight("w1", [P, DC, 2 * HID])
        w2_raw, w2 = weight("w2", [P, UC, D])
        wo = sb("wo", [P, HP2, D])
        b1 = sb("b1", [P, 2, UC])
        b2 = sb("b2", [P, D])
        lng = sb("lng", [P, 2, DC])
        scales = sb("scales", [P, 2, DH2])
        scaled = sb("scaled", [P, NT, 4, DH2])
        came = stream("came", [P, NT, D])
        hT, yT = paired_streams("hT", [P, DC, L + 1], "yT", [P, DC, L + 1])
        work, u_low = paired_streams("work", [P, 3, 2 * INNER], "u_low", [P, UC, L])
        squares, rot2 = ([w[:, i, :] for w in work] for i in (0, 2))
        uT = [w[:].rearrange("p a (b n) -> p (a b) n", n=L) for w in work]
        assert uT[0].shape[1] == UC
        rope = work[0][:, 0, :].rearrange("p (t i d) -> p t i d", t=NT, i=4)
        ss, root, inv = stream("ss", [P, 2 * H2]), stream("root", [P, 2 * H2]), stream("inv", [P, 2 * H2])
        flipped, u_high_part = paired_streams("flipped", [P, UC, L], "u_high", [P, UC, L])
        qT = [f[:, 0:HP2, :] for f in flipped]
        probsT = [f[:, HP2:UC, :].rearrange("p a (b n) -> p a b n", n=P) for f in flipped]
        kT = stream("kT", [P, 2, HP2, L])
        v = stream("v", [P, NT, INNER])
        gate = [a[:, 0:2, :] for a in v]
        hn = [a[:, 2:NT, :].rearrange("p a (b n) -> p (a b) n", n=D) for a in v]
        probs = stream("probs", [P, 2, 2, 2 * P])
        y = [a[:].rearrange("p a b n -> p (a b) n") for a in probs]
        rot = [[work[s][:, 1, :], probs[s][:].rearrange("p a b c -> p (a b c)")] for s in range(NS)]
        oT, part = paired_streams("oT", [P, HP2, L], "part", [P, DC, L + 1])
        stats, mv = stream("stats", [P, NT, 12]), stream("mv", [P, NT, 2])
        ve, rstd = stream("ve", [P, NT]), stream("rstd", [P, NT])
        UNITS = HP2 * NT
        nmax, rsum, rinv = stream("nmax", [P, UNITS, 2]), stream("rsum", [P, UNITS, 2]), stream("rinv", [P, UNITS, 2])
        bank = [[ctx.enter_context(nc.psum_tensor(f"l{layer}_bank{s}{i}", [P, L], F32)) for i in range(4)]
                for s in range(NS)]

        w_in, w_set, w_high = g.once(f"w_in{layer}"), g.once(f"w_set{layer}"), g.once(f"w_high{layer}")
        late_in, late_high, late_split = (g.once(f"{n}{layer}") for n in ("late_in", "late_high", "late_split"))
        stored, first_in = [g.once(f"stored{layer}{s}") for s in range(NS)], g.once(f"first_in{layer}")
        y_in, yT_psum, yT_ready, yT_split = sem2("y_in"), sem2("yT_psum"), sem2("yT_ready"), sem2("yT_split")
        affine, hT_high, u_done, u_high = sem2("affine"), sem2("hT_high"), sem2("u_done"), sem2("u_high")
        qkv_psum, squared, v_ready, summed = sem2("qkv_psum"), sem2("squared"), sem2("v_ready"), sem2("summed")
        rooted, inv_ready, turned, added = sem2("rooted"), sem2("inv_ready"), sem2("turned"), sem2("added")
        q_rotated, k_rotated = sem2("q_rotated"), sem2("k_rotated")
        qkT_psum, qkT_ready = sem2("qkT_psum"), sem2("qkT_ready")
        scores_ready, nmax_ready, probs_ready, normed = sem2("scores"), sem2("nmax_r"), sem2("probs_r"), sem2("normed")
        pT_psum, pT_ready, pv_done, oT_ready = sem2("pT_psum"), sem2("pT_ready"), sem2("pv_done"), sem2("oT_ready")
        wo_psum, y1_ready, shifted = sem2("wo_psum"), sem2("y1_ready"), sem2("shifted")
        chain_sem, var_ready, rstd_ready, hn_ready = sem("chain"), sem2("var"), sem2("rstd_r"), sem2("hn_ready")
        biased, hT_psum, hT_ready = sem2("biased"), sem2("hT_psum"), sem2("hT_ready")
        ag_psum, gate_ready, u_ready = sem2("ag_psum"), sem2("gate_ready"), sem2("u_ready")
        w2_psum, y2_ready, x_in, xadded = sem2("w2_psum"), sem2("y2_ready"), sem2("x_in"), sem2("xadded")
        sem_range = range(sems[0].num, sems[-1].num + 1)
        assert len(sem_range) == len(sems)
        units = [(cp, w, r) for cp in range(HP2 // 2) for w in range(NT) for r in range(2)]

        turns = [(s, t) for t in range(NT) for s in range(NS)]
        LAG = 3

        LEAD = 3
        chunks = [(0, c) for c in range(LEAD)] + [turn for c in range(UC - LEAD) for turn in ((1, c), (0, c + LEAD))] +\
                 [(1, c) for c in range(UC - LEAD, UC)]

        def kT_bank(t):
            return 2 if t == NT - 1 else 3

        def rows(c):
            return min(P, HID - c * P)

        WHOLE = HID // P * P
        tail = rows(UC - 1)
        halves = [[w[:] for w in (w1_raw, *w1)], [w[:, 0:UC - 1, :] for w in (w2_raw, *w2)],
                  [w[0:tail, UC - 1, :] for w in (w2_raw, *w2)]]
        SPLIT_SRC = [g.w1d[layer].rearrange("(c p) n -> p c n", p=P),
                     g.w2d[layer][0:WHOLE].rearrange("(c p) n -> p c n", p=P), g.w2d[layer][WHOLE:HID]]
        LOADS = [(wqkv_raw[:], g.wqkv[layer].rearrange("(c p) n -> p c n", p=P)), (rope, g.rope2),
                 (scales[:, 0, :], g.qs[layer].partition_broadcast(P)), (scales[:, 1, :], g.ks[layer].partition_broadcast(P))]
        LATE = [(lng[:, 0, :], g.lng[layer]), (lng[:, 1, :], g.lnb[layer]), (b1[:], g.b1l[layer]),
                 (b2[:], g.b2l[layer].partition_broadcast(P)), (wo[:], g.wo[layer].rearrange("(c p) n -> p c n", p=P))]

        LATE_ALL = 16 * (len(halves) + len(LATE))

        with nc.Block() as block:
            @block.sync
            def _(sp):
                for dst, src in LOADS:
                    sp.dma_start(dst, src).then_inc(w_in, 16)
                for s in range(NS):
                    sp.dma_start(came[s][:], g.y_d[layer][s].rearrange("(t p) n -> p t n", p=P)).then_inc(first_in, 16)
                sp.wait_ge(w_set, NS)
                for s in range(NS):
                    sp.dma_start(g.y_d[layer][B + s].rearrange("(p a) n -> p (a n)", p=DH2), kT[s][DH2:P, 0].rearrange("p a b -> p (a b)"))\
                      .then_inc(stored[s], 16)
                for (raw, _, _), src in zip(halves, SPLIT_SRC):
                    sp.dma_start(raw, src).then_inc(late_in, 16)
                for dst, src in LATE:
                    sp.dma_start(dst, src).then_inc(late_in, 16)
                for s in range(NS):
                    sp.wait_ge(stored[s], 16)
                sp.wait_ge(first_in, 16 * NS)

            @block.vector
            def _(dve):
                for s in range(NS):
                    dve.memset(yT[s][:, 1, 0:1].bitcast(F32), 0.0)
                    dve.memset(kT[s][DH2:P, 0], 0.0)
                    dve.memset(kT[s][0:DH2, 1], 0.0).then_inc(w_set, 1)
                dve.wait_ge(w_in, 16 * len(LOADS))
                for i in range(2):
                    dve.tensor_tensor(scaled[:, :, 2 * i, :], rope[:, :, 2 * i, :],
                                      scales[:, i, :].unsqueeze(1).to_broadcast([P, NT, DH2]), ALU.mult).then_inc(w_set, 1)
                    for a in range(2):
                        h = DH2 // 2
                        dve.tensor_tensor(scaled[:, :, 2 * i + 1, a * h:(a + 1) * h], rope[:, :, 2 * i + 1, a * h:(a + 1) * h],
                                          scales[:, i, (1 - a) * h:(2 - a) * h].unsqueeze(1).to_broadcast([P, NT, h]),
                                          ALU.mult).then_inc(w_set, 1)
                dve.wait_ge(w_high, 1)
                dve.tensor_tensor(wqkv[0][:], wqkv_raw[:], wqkv[1][:].bitcast(F32), ALU.subtract).then_inc(w_set, 1)
                dve.wait_ge(w_set, NS + 7)

            @block.scalar
            def _(act):
                act.wait_ge(w_in, 16 * len(LOADS))
                act.activation(wqkv[1][:], wqkv_raw[:], ACT.Copy).then_inc(w_high, 1)

        def turn_of(pair, first):
            with nc.Block() as block:
                @block.sync
                def _(sp):
                    for s in range(NS):
                        sp.wait_ge(y1_ready[s], NT)
                        sp.dma_start(came[s][:], g.y_d[layer][pair * NS + (NS + s)].rearrange("(t p) n -> p t n", p=P)).then_inc(y_in[s], 16)
                    if final:
                        for s in range(NS):
                            sp.wait_ge(hT_psum[s], DC)
                            sp.dma_start(hn[s][:], g.x3_d[pair * NS + s].rearrange("(t p) n -> p t n", p=P)).then_inc(x_in[s], 16)
                    dst = g.out if final else g.y_d[layer + 1]
                    for s in range(NS):
                        sp.wait_ge(y2_ready[s], NT)
                        sp.dma_start(dst[pair * NS + s].rearrange("(t p) n -> p t n", p=P), y[s]).then_inc(stored[s], 16)
                    for s in range(NS):
                        sp.wait_ge(y_in[s], 16)

                def heads(a):
                    return a.rearrange("p (h d) -> p h d", d=DH2)

                def normalise(eng, s, t, i):
                    space = heads(rot[s][t % 2][:, i * INNER:(i + 1) * INNER])
                    return eng.tensor_tensor(space, space, inv[s][:, i * H2:(i + 1) * H2].unsqueeze(2).to_broadcast([P, H2, DH2]), ALU.mult)

                @block.gpsimd
                def _(pool):
                    def add(s, t, j):
                        cols = slice(j * INNER, (j + 1) * INNER)
                        pool.wait_ge(turned[s], 6 * t + 3 * (j + 1))
                        pool.tensor_tensor(rot[s][t % 2][:, cols], rot[s][t % 2][:, cols], rot2[s][:, cols], ALU.add).then_inc(added[s], 1)

                    for i in range(len(turns) + 1):
                        if i < len(turns):
                            add(*turns[i], 0)
                        if i:
                            s, t = turns[i - 1]
                            pool.wait_ge(added[s], 2 * (t + 1))
                            pool.wait_ge(inv_ready[s], t + 1)
                            normalise(pool, s, t, 1).then_inc(k_rotated[s], 1)
                        if i < len(turns):
                            add(*turns[i], 1)
                    pool.wait_ge(late_in, LATE_ALL)
                    if first:
                        for i, (raw, low, high) in enumerate(halves):
                            pool.tensor_copy(high, raw).then_inc(late_high, 1)
                        for i, (raw, low, high) in enumerate(halves):
                            pool.wait_ge(late_high, i + 1)
                            pool.tensor_tensor(low, raw, high.bitcast(F32), ALU.subtract).then_inc(late_split, 1)
                    for s in range(NS):
                        pool.wait_ge(var_ready[s], 1)
                        pool.tensor_tensor(rstd[s][:], ve[s][:], g.minus_half[:, 0:NT], ALU.pow).then_inc(rstd_ready[s], 1)
                    for s in range(NS):
                        pool.wait_ge(hn_ready[s], 2 * NT)
                        pool.wait_ge(shifted[s], 1)
                        pool.tensor_tensor(y[s], y[s], b2[:].unsqueeze(1).to_broadcast([P, NT, D]), ALU.add).then_inc(biased[s], 1)
                    if final:
                        for s in range(NS):
                            pool.wait_ge(x_in[s], 16)
                            pool.wait_ge(biased[s], 1)
                            pool.tensor_tensor(y[s], y[s], hn[s][:], ALU.add).then_inc(xadded[s], 1)

                @block.vector
                def _(dve):
                    chain = Chain(dve, chain_sem)

                    def norms(s, t):
                        if t:
                            dve.wait_ge(rooted[s], t)
                        chain.step(dve.tensor_reduce(ss[s][:], heads(squares[s]), AX, ALU.add))
                        dve.tensor_scalar(ss[s][:], ss[s][:], 1e-24, None, ALU.max).then_inc(summed[s], 1)

                    def turn(s, t):
                        if t:
                            dve.wait_ge(added[s], 2 * t)
                        if t >= 2:
                            dve.wait_ge(qkT_psum[s], 2 * (t - 1))
                        if t == 1:
                            dve.wait_ge(stored[s], pair * 16 + 16)
                        h, rot_t = DH2 // 2, rot[s][t % 2]
                        for i in range(2):
                            src = heads(bank[s][i][:])
                            dst, dst2 = (heads(a[:, i * INNER:(i + 1) * INNER]) for a in (rot_t, rot2[s]))
                            dve.wait_ge(squared[s], 2 * t + i + 1)
                            dve.tensor_tensor(dst, src, scaled[:, t, 2 * i:2 * i + 1, :].to_broadcast([P, H2, DH2]), ALU.mult).then_inc(turned[s], 1)
                            for a in range(2):
                                dve.tensor_tensor(dst2[:, :, a * h:(a + 1) * h], src[:, :, (1 - a) * h:(2 - a) * h],
                                                  scaled[:, t, 2 * i + 1:2 * i + 2, a * h:(a + 1) * h].to_broadcast([P, H2, h]),
                                                  ALU.mult).then_inc(turned[s], 1)

                    def invert(s, t):
                        dve.wait_ge(rooted[s], t + 1)
                        if t:
                            dve.wait_ge(k_rotated[s], t)
                        dve.reciprocal(inv[s][:], root[s][:]).then_inc(inv_ready[s], 1)

                    def row_max(s, u):
                        w = units[u][1]
                        dve.wait_ge(scores_ready[s], u + 1)
                        S = bank[s][u % 2][:].rearrange("p (h k) -> p h k", h=2)
                        dve.tensor_reduce(nmax[s][:, u, :], S[:, :, 0:(1 + min(w, 1)) * P], AX, ALU.max, negate=True).then_inc(nmax_ready[s], 1)

                    def norm_probs(s, u):
                        w = units[u][1]
                        n = (1 + min(w, 1)) * P
                        dve.wait_ge(probs_ready[s], 2 * (u + 1))
                        chain.step(dve.reciprocal(rinv[s][:, u, :], rsum[s][:, u, :]))
                        for h in range(2):
                            dve.tensor_scalar(probs[s][:, u % 2, h, 0:n], probs[s][:, u % 2, h, 0:n], rinv[s][:, u, h:h + 1], None, ALU.mult)\
                               .then_inc(normed[s], 1)

                    for s in range(NS):
                        dve.memset(part[s][:, 1, 0:1].bitcast(F32), 0.0).then_inc(yT_split[s], 1)
                        for c in range(DC):
                            dve.wait_ge(yT_ready[s], c + 1)
                            dve.tensor_tensor(part[s][:, c, c:L + c], bank[s][c][:, 0:L], yT[s][:, c, c:L + c].bitcast(F32), ALU.subtract)\
                               .then_inc(yT_split[s], 1)
                    for i in range(len(turns) + 1):
                        if i < len(turns):
                            turn(*turns[i])
                        if i:
                            s, t = turns[i - 1]
                            invert(s, t)
                            dve.wait_ge(added[s], 2 * t + 1)
                            dve.wait_ge(inv_ready[s], t + 1)
                            normalise(dve, s, t, 0).then_inc(q_rotated[s], 1)
                        if i < len(turns):
                            norms(*turns[i])
                    for u in range(UNITS + 1):
                        for s in range(NS):
                            if u:
                                norm_probs(s, u - 1)
                        for s in range(NS):
                            if u < UNITS:
                                row_max(s, u)
                    def residual(s, t):
                        dve.wait_ge(wo_psum[s], t + 1)
                        dve.tensor_tensor(y[s][:, t, :], bank[s][t % 2][:, 0:D], came[s][:, t, :], ALU.add).then_inc(y1_ready[s], 1)

                    def parts(s):
                        late = bank[s][2][:].rearrange("p (t n) -> p t n", t=NT)
                        return lambda t: [y[s][:, t, 0:P], late[:, t, :]]

                    def measure(s):
                        dve.wait_ge(y1_ready[s], NT)
                        dve.wait_ge(shifted[s], 1)
                        row_stats(dve, chain, var_ready[s], parts(s), stats[s], mv[s], ve[s])

                    def norm(s):
                        for ins in normalised_rows(dve, rstd_ready[s], 1, parts(s), mv[s], rstd[s],
                                                   lambda t: [hn[s][:, t, 0:P], hn[s][:, t, P:D]]):
                            ins.then_inc(hn_ready[s], 1)

                    def scale_rows(s):
                        for c in range(DC):
                            dve.wait_ge(hT_psum[s], c + 1)
                            dve.tensor_scalar(hT[s][:, c, 1:L + 1], bank[s][c][:], lng[:, 0, c:c + 1], lng[:, 1, c:c + 1], ALU.mult, ALU.add)\
                               .then_inc(affine[s], 1)

                    def low_rows(s):
                        for c in range(DC):
                            dve.wait_ge(hT_high[s], c + 1)
                            dve.tensor_tensor(yT[s][:, c, 1:L + 1], hT[s][:, c, 1:L + 1], part[s][:, c, 1:L + 1].bitcast(F32), ALU.subtract)\
                               .then_inc(hT_ready[s], 1)

                    def gated(s, c):
                        r = rows(c)
                        dve.wait_ge(gate_ready[s], c + 1)
                        dve.scalar_tensor_tensor(uT[s][0:r, c, :], bank[s][2 * (c % 2)][0:r, :], b1[0:r, 0, c:c + 1], gate[s][0:r, c % 2, :],
                                                 ALU.add, ALU.mult).then_inc(u_done[s], 1)

                    def low_units(s, c):
                        r = rows(c)
                        dve.wait_ge(u_high[s], c + 1)
                        dve.tensor_tensor(u_low[s][0:r, c, :], uT[s][0:r, c, :], u_high_part[s][0:r, c, :].bitcast(F32), ALU.subtract)\
                           .then_inc(u_ready[s], 1)

                    dve.wait_ge(late_in, LATE_ALL)
                    for t in range(NT):
                        residual(0, t)
                    residual(1, 0)
                    measure(0)
                    residual(1, 1)
                    residual(1, 2)
                    norm(0)
                    residual(1, 3)
                    scale_rows(0)
                    low_rows(0)
                    measure(1)
                    norm(1)
                    for i in range(len(chunks) + 1):
                        if i < len(chunks):
                            gated(*chunks[i])
                        if i == 0:
                            scale_rows(1)
                        if i:
                            low_units(*chunks[i - 1])
                        if i == 1:
                            low_rows(1)
                    for s in range(NS):
                        dve.wait_ge(xadded[s] if final else biased[s], 1)
                        for t in range(NT):
                            dve.wait_ge(w2_psum[s], t + 1)
                            dve.tensor_tensor(y[s][:, t, :], bank[s][t % 2][:, 0:D], y[s][:, t, :], ALU.add).then_inc(y2_ready[s], 1)

                @block.scalar
                def _(act):
                    for s in range(NS):
                        for c in range(DC):
                            act.wait_ge(yT_psum[s], c + 1)
                            act.activation(yT[s][:, c, c:L + c], bank[s][c][:, 0:L], ACT.Copy).then_inc(yT_ready[s], 1)

                    def qT_out(s, t):
                        act.wait_ge(qkT_psum[s], 2 * t + 1)
                        act.activation(qT[s][:, :, t * P:(t + 1) * P], bank[s][3][:].rearrange("p (a b) -> p a b", b=P), ACT.Copy)\
                           .then_inc(qkT_ready[s], 1)

                    def kT_out(s, t):
                        act.wait_ge(qkT_psum[s], 2 * t + 2)
                        src = bank[s][kT_bank(t)][:].rearrange("p (a b) -> p a b", b=P)
                        for half in range(2):
                            r = slice(DH2 * half, DH2 * (half + 1))
                            last = act.activation(kT[s][r, half, :, t * P:(t + 1) * P], src[r], ACT.Copy)
                        last.then_inc(qkT_ready[s], 1)

                    def square(s, t, j):
                        act.wait_ge(qkv_psum[s], 3 * t + j + 1)
                        act.activation(squares[s][:, j * INNER:(j + 1) * INNER], bank[s][j][:], ACT.Square).then_inc(squared[s], 1)

                    def square_root(s, t):
                        act.wait_ge(summed[s], t + 1)
                        if t:
                            act.wait_ge(inv_ready[s], t)
                        act.activation(root[s][:], ss[s][:], ACT.Sqrt).then_inc(rooted[s], 1)

                    for i in range(len(turns) + LAG):
                        now = turns[i] if i < len(turns) else None
                        before = turns[i - LAG] if i >= LAG else None
                        if now:
                            if now[1]:
                                act.wait_ge(summed[now[0]], now[1])
                            square(*now, 0)
                        if before:
                            qT_out(*before)
                        if now:
                            square(*now, 1)
                        if 1 <= i <= len(turns):
                            square_root(*turns[i - 1])
                        if before:
                            kT_out(*before)
                        if now:
                            s, t = now
                            act.wait_ge(qkv_psum[s], 3 * (t + 1))
                            act.activation(v[s][:, t, :], bank[s][2][:], ACT.Copy).then_inc(v_ready[s], 1)

                    def exps(s, u):
                        w = units[u][1]
                        n = (1 + min(w, 1)) * P
                        act.wait_ge(nmax_ready[s], u + 1)
                        if u >= 2:
                            act.wait_ge(pT_psum[s], u - 1)
                        for h in range(2):
                            act.activation(probs[s][:, u % 2, h, 0:n], bank[s][u % 2][:, 2 * P * h:2 * P * h + n], ACT.Exp,
                                           bias=nmax[s][:, u, h:h + 1], accum_out=rsum[s][:, u, h:h + 1]).then_inc(probs_ready[s], 1)

                    def pT_out(s, u):
                        act.wait_ge(pT_psum[s], u + 1)
                        if u >= 2:
                            act.wait_ge(pv_done[s], u - 1)
                        if units[u][1]:
                            act.activation(probsT[s][:, u % 2].rearrange("p a b -> p (a b)"), bank[s][2][:], ACT.Copy).then_inc(pT_ready[s], 1)
                        else:
                            act.activation(probsT[s][:, u % 2, 0:4:2, :], bank[s][2][:].rearrange("p (a b) -> p a b", b=P)[:, 0:4:2, :], ACT.Copy)\
                               .then_inc(pT_ready[s], 1)

                    def oT_out(s, i):
                        cp, w = i // NT, i % NT
                        act.wait_ge(pv_done[s], 2 * (i + 1))
                        act.activation(oT[s][:, 2 * cp:2 * cp + 2, w * P:(w + 1) * P], bank[s][3][:, 0:2 * P].rearrange("p (a b) -> p a b", b=P),
                                       ACT.Copy).then_inc(oT_ready[s], 1)

                    for u in range(UNITS + 2):
                        for s in range(NS):
                            if u < UNITS:
                                exps(s, u)
                        for s in range(NS):
                            if 1 <= u <= UNITS:
                                pT_out(s, u - 1)
                            if u >= 2 and u % 2:
                                oT_out(s, (u - 2) // 2)
                    def high_rows(s):
                        for c in range(DC):
                            act.wait_ge(affine[s], c + 1)
                            act.activation(part[s][:, c, 1:L + 1], hT[s][:, c, 1:L + 1], ACT.Copy).then_inc(hT_high[s], 1)

                    def high(s, c):
                        r = rows(c)
                        act.wait_ge(u_done[s], c + 1)
                        act.activation(u_high_part[s][0:r, c, :], uT[s][0:r, c, :], ACT.Copy).then_inc(u_high[s], 1)

                    act.wait_ge(late_in, LATE_ALL)
                    high_rows(0)
                    for i in range(len(chunks) + 1):
                        if i < len(chunks):
                            s, c = chunks[i]
                            r = rows(c)
                            act.wait_ge(ag_psum[s], c + 1)
                            if c >= 2:
                                act.wait_ge(u_done[s], c - 1)
                            act.activation(gate[s][0:r, c % 2, :], bank[s][2 * (c % 2) + 1][0:r, :], ACT.Gelu, bias=b1[0:r, 1, c:c + 1])\
                               .then_inc(gate_ready[s], 1)
                        if i:
                            high(*chunks[i - 1])
                        if i == 1:
                            high_rows(1)

                @block.tensor
                def _(pe):
                    for s in range(NS):
                        for c in range(DC):
                            for t in range(NT):
                                last = pe.transpose(bank[s][c][:, t * P:(t + 1) * P], came[s][:, t, c * P:(c + 1) * P], g.ident[:])
                            last.then_inc(yT_psum[s], 1)

                    def product(out, a, b, start, stop):
                        pe.matmul(out, a[0], b[0], start=start, stop=False)
                        pe.matmul(out, a[0], b[1], start=False, stop=False)
                        return pe.matmul(out, a[1], b[0], start=False, stop=stop)

                    def project(s, t, i):
                        if i == 0 and t == 0:
                            pe.wait_ge(yT_split[s], DC + 1)
                        elif i == 0:
                            pe.wait_ge(turned[s], 6 * t)
                        elif i == 2 and t:
                            pe.wait_ge(v_ready[s], t)
                        for c in range(DC):
                            last = product(bank[s][i][:], [a[:, c, t * P:(t + 1) * P] for a in (yT[s], part[s])],
                                           [wqkv[k][:, c, i * INNER:(i + 1) * INNER] for k in (1, 0)], c == 0, c == DC - 1)
                        last.then_inc(qkv_psum[s], 1)

                    def flip_qk(s, t, i):
                        pe.wait_ge((q_rotated, k_rotated)[i][s], t + 1)
                        if t == NT - 1 and i:
                            pe.wait_ge(v_ready[s], NT)
                        elif 2 * t + i >= 1:
                            pe.wait_ge(qkT_ready[s], 2 * t + i)
                        for a in range(HP2):
                            last = pe.transpose(bank[s][kT_bank(t) if i else 3][:, a * P:(a + 1) * P], rot[s][t % 2][:, i * INNER + a * P:i * INNER + (a + 1) * P], g.ident[:])
                        last.then_inc(qkT_psum[s], 1)

                    def scores(s, u):
                        cp, w, half = units[u]
                        if u == 0:
                            pe.wait_ge(qkT_ready[s], 2)
                            pe.wait_ge(turned[s], 6 * NT)
                        if u == 2:
                            pe.wait_ge(qkT_ready[s], 2 * NT)
                        if u >= 2:
                            pe.wait_ge(probs_ready[s], 2 * (u - 1))
                        k0, n = (w - 1, 2) if w else (0, 1)
                        for h in range(2):
                            p = 2 * cp + h
                            out = bank[s][u % 2][:, 2 * P * h:2 * P * h + n * P]
                            pe.matmul(out, qT[s][:, p, w * P:(w + 1) * P], kT[s][:, half, p, k0 * P:(k0 + n) * P], start=True, stop=False)
                            last = pe.matmul(out, g.mask[:, 0, :], g.mask[:, 3 - n:3, :].rearrange("p a b -> p (a b)"), start=False, stop=True)
                        last.then_inc(scores_ready[s], 1)

                    def flip(s, u):
                        w = units[u][1]
                        if u == 0:
                            pe.wait_ge(qkT_ready[s], 2 * NT)
                        pe.wait_ge(normed[s], 2 * (u + 1))
                        if u:
                            pe.wait_ge(pT_ready[s], u)
                        for h in range(2):
                            for k in range(1 + min(w, 1)):
                                last = pe.transpose(bank[s][2][:, (2 * h + k) * P:(2 * h + k + 1) * P], probs[s][:, u % 2, h, k * P:(k + 1) * P], g.ident[:])
                        last.then_inc(pT_psum[s], 1)

                    def output(s, u):
                        cp, w, half = units[u]
                        pe.wait_ge(pT_ready[s], u + 1)
                        if half == 0 and u:
                            pe.wait_ge(oT_ready[s], u // 2)
                        k0, n = (w - 1, 2) if w else (0, 1)
                        for h in range(2):
                            for k in range(n):
                                head = (2 * (2 * cp + h) + half) * DH2
                                last = pe.matmul(bank[s][3][DH2 * half:DH2 * (half + 1), h * P:(h + 1) * P], v[s][:, k0 + k, head:head + DH2],
                                                 probsT[s][:, u % 2, 2 * h + k, :], start=k == 0, stop=k == n - 1, tile_position=(0, DH2 * half))
                        last.then_inc(pv_done[s], 1)

                    def hidden(s, c):
                        if c >= 2:
                            pe.wait_ge(u_done[s], c - 1)
                        r = rows(c)
                        for i in range(2):
                            for k in range(DC):
                                last = product(bank[s][2 * (c % 2) + i][0:r, :], [w1[a][:, k, i * HID + c * P:i * HID + c * P + r] for a in (1, 0)],
                                               [a[:, k, 1:L + 1] for a in (part[s], yT[s])], k == 0, k == DC - 1)
                        last.then_inc(ag_psum[s], 1)

                    for i in range(len(turns) + LAG):
                        if i >= len(turns) + LAG - NS:
                            for u in range(2):
                                scores(i - (len(turns) + LAG - NS), u)
                        for j in range(3):
                            if i < len(turns):
                                project(*turns[i], j)
                            if i >= LAG and j < 2:
                                flip_qk(*turns[i - LAG], j)
                    for u in range(UNITS + 2):
                        for s in range(NS):
                            if 2 <= u < UNITS:
                                scores(s, u)
                        for s in range(NS):
                            if u >= 2:
                                output(s, u - 2)
                        for s in range(NS):
                            if 1 <= u <= UNITS:
                                flip(s, u - 1)
                    def attended(s, t):
                        if t == 0:
                            pe.wait_ge(oT_ready[s], UNITS // 2)
                        if t >= 2:
                            pe.wait_ge(y1_ready[s], t - 1)
                        for c in range(HP2):
                            last = pe.matmul(bank[s][t % 2][:, 0:D], oT[s][:, c, t * P:(t + 1) * P], wo[:, c, :], start=c == 0, stop=c == HP2 - 1)
                        last.then_inc(wo_psum[s], 1)

                    def shift(s):
                        pe.wait_ge(y1_ready[s], NT)
                        late = bank[s][2][:].rearrange("p (t n) -> p t n", t=NT)
                        pe.matmul(late, g.shift[:, 0, :], y[s][:, :, P:D], start=True, stop=False)
                        pe.matmul(late[:, 1:NT, :], g.shift[:, 1, :], y[s][:, 0:NT - 1, P:D], start=False, stop=True).then_inc(shifted[s], 1)

                    def flip_hn(s):
                        for c in range(DC):
                            for t in range(NT):
                                pe.wait_ge(hn_ready[s], 2 * (t + 1))
                                last = pe.transpose(bank[s][c][:, t * P:(t + 1) * P], hn[s][:, t, c * P:(c + 1) * P], g.ident[:])
                            last.then_inc(hT_psum[s], 1)

                    pe.wait_ge(late_in, LATE_ALL)
                    for t in range(NT):
                        attended(0, t)
                    attended(1, 0)
                    shift(0)
                    for t in range(1, NT):
                        attended(1, t)
                    flip_hn(0)
                    shift(1)
                    pe.wait_ge(late_split, len(halves))
                    for i, (s, c) in enumerate(chunks):
                        if c == 0:
                            pe.wait_ge(hT_ready[s], DC)
                        hidden(s, c)
                        if i == 1:
                            flip_hn(1)
                    for s in range(NS):
                        pe.wait_ge(u_ready[s], UC)
                        for t in range(NT):
                            if t >= 2:
                                pe.wait_ge(y2_ready[s], t - 1)
                            for c in range(UC):
                                r = rows(c)
                                last = product(bank[s][t % 2][:, 0:D], [a[0:r, c, t * P:(t + 1) * P] for a in (u_high_part[s], u_low[s])],
                                               [w2[a][0:r, c, :] for a in (1, 0)], c == 0, c == UC - 1)
                            last.then_inc(w2_psum[s], 1)
            nc.all_engine_barrier(sems_to_clear=sem_range)

        turn_of(0, True)
        with nc.Fori(1, PAIRS) as pair:
            turn_of(pair, False)

        with nc.Block() as block:
            @block.sync
            def _(sp):
                for s in range(NS):
                    sp.wait_ge(stored[s], 16 * (PAIRS + 1))


def shape_tables():
    f = np.float32
    t = {}
    scale_vec = ((np.arange(0, D, 2, dtype=f) + f(0.4 * D)) / f(1.4 * D)).astype(f)
    scale = (scale_vec[None, :] ** (np.arange(L, dtype=f) / f(512.0))[:, None]).astype(f)
    inv_freq = (f(1.0) / f(10000.0) ** (np.arange(D // 2, dtype=f) / f(D // 2))).astype(f)
    angle = (np.arange(L, dtype=f)[:, None] * inv_freq[None, :]).astype(f)
    sin, cos = np.sin(angle), np.cos(angle)
    inv = (f(1.0) / scale).astype(f)
    t["xpos0"] = np.stack([(cos * scale).T, (sin * scale).T, (cos * inv).T, (sin * inv).T], axis=1)
    t["decay"] = f(0.9) ** np.abs(np.arange(7 * P)[None, :] - (NT - 1) * P - np.arange(P)[:, None]).astype(f)
    t["ident"] = np.eye(P, dtype=f)
    t["ranks"] = np.concatenate([np.triu(np.ones((P, P), f), 1), np.ones((P, P), f)], axis=1)
    t["iota"] = np.tile(np.arange(P, dtype=f)[None, :], (P, 1))
    dh = 16
    freqs = np.exp(f(-np.log(10000.0)) * np.arange(0, dh, 2, dtype=f) / f(dh)).astype(f)
    ang = np.repeat(np.arange(L, dtype=f)[:, None] * freqs[None, :], 2, axis=1).astype(f)
    sign = np.where(np.arange(dh) % 2 == 0, f(-1), f(1)).astype(f)
    rope = np.stack([np.cos(ang), np.sin(ang) * sign], axis=1)
    rope = rope.astype(f)
    rope = np.stack([rope * f(0.25), rope], axis=1)
    t["rope1"] = rope.reshape(NT, P, 2, 2, dh).transpose(1, 0, 2, 3, 4)
    dh, window = 64, 128
    half = np.arange(0, dh, 2, dtype=f)
    invf = (f(1.0) / f(10000.0) ** (half / f(dh))).astype(f)
    fr = (np.arange(L, dtype=f)[:, None] * invf[None, :]).astype(f)
    fr = np.concatenate([fr, fr], axis=-1)
    base = ((half + f(0.4 * dh)) / f(1.4 * dh)).astype(f)
    power = ((np.arange(L, dtype=f) - f(L // 2)) / f(window // 2)).astype(f)
    sc = (base[None, :] ** power[:, None]).astype(f)
    sc = np.concatenate([sc, sc], axis=-1)
    sign = np.where(np.arange(dh) < dh // 2, f(-1), f(1)).astype(f)
    c, s_ = np.cos(fr), np.sin(fr) * sign
    w = np.stack([c * sc * f(8), s_ * sc * f(8), c / sc, s_ / sc], axis=1).astype(f)
    t["rope2"] = w.reshape(NT, P, 4, dh).transpose(1, 0, 2, 3)
    shift = np.zeros((P, 2, P), f)
    shift[np.arange(P - 1), 0, np.arange(1, P)] = 1
    shift[P - 1, 1, 0] = 1
    t["shift"] = shift
    a, cc = np.arange(P)[:, None], np.arange(P)[None, :]
    ban = np.stack([a > cc, cc > a], axis=1) * -1e30
    t["mask"] = np.concatenate([np.eye(P)[:, None, :], ban], axis=1).astype(f)
    return {k: np.ascontiguousarray(v) for k, v in t.items()}


def build(nc, g):
    with g.ctx:
        g.ident, g.shift = g.keep("ident", [P, P]), g.keep("shift", [P, 2, P])
        g.mask, g.minus_half = g.keep("mask", [P, 3, P], BF16), g.keep("minus_half", [P, 2 * H2])
        g.row_of, g.owner = g.keep("row_of", [P, TILES + NS * NT], I32), g.keep("owner", [P, MAXSLOT], I32)
        g.x1_d = nc.dram_tensor("x1_d", (B + NS, L, D), F32).ap()
        g.x3_d = nc.dram_tensor("x3_d", (B, L, D), F32).ap()
        g.y_d = [nc.dram_tensor(f"y{i}_d", (B + NS, L, D), F32).ap() for i in range(2)]
        g.xs_d = nc.dram_tensor("xs_d", (MAXSLOT * P, D), F32).ap()
        g.ys_d = nc.dram_tensor("ys_d", (SLOTS * P, D), F32).ap()
        tables_in = g.once("kept_in")
        g.w1_in, g.w2_in, g.pool_consts, g.zeros_out = (g.once(n) for n in ("w1_in", "w2_in", "pool_consts", "zeros_out"))
        with nc.sbuf_tensor("mask_f32", [P, 3, P], F32) as mask_f32, nc.Block() as block:
            @block.sync
            def _(sp):
                for dst, src in [(g.ident, g.ident_d), (g.shift, g.shift_d), (mask_f32, g.mask_d)]:
                    sp.dma_start(dst[:], src).then_inc(tables_in, 16)

            @block.vector
            def _(dve):
                dve.wait_ge(tables_in, 48)
                dve.tensor_copy(g.mask[:], mask_f32[:]).then_inc(tables_in, 1)
                dve.wait_ge(tables_in, 49)

        with ExitStack() as experts:
            def sb(name, shape, dt=F32):
                return experts.enter_context(nc.sbuf_tensor(name, shape, dt))

            g.w1 = sb("w1", [P, EXPERTS, DC, FF])
            g.xn2_offset = -(-nc.sbuf_base // 32) * 32
            g.xn2 = sb("xn2", [P, TILES, D])
            g.logits = sb("logits", [P, TILES, EXPERTS])
            with nc.sbuf_tensor("zrow", [P, ZEROED * D], F32) as zrow:
                g.zrow = zrow
                phase_attn0(nc, g)
            g.w2, g.b1, g.b2 = sb("w2", [P, EXPERTS, FC, D]), sb("b1", [P, EXPERTS, FC]), sb("b2", [P, EXPERTS, D])
            phase_route(nc, g)
            phase_experts(nc, g)
        phase_attn1(nc, g)
        for layer in range(2):
            phase_layer(nc, g, layer)


def kernel(**inputs):
    import concourse.bacc as bacc
    from concourse.bass_utils import run_bass_kernel_spmd

    a = {k: np.asarray(v) for k, v in inputs.items()}
    tables = shape_tables()
    HIDDEN = a["L1_ffn_b1"].shape[1] // 2
    padded = np.zeros((B + NS, L, D), a["L0_attn_X"].dtype)
    padded[0:B] = a["L0_attn_X"]
    b1 = np.zeros((2, UC * P, 2), np.float32)
    b1[:, 0:HIDDEN] = a["L1_ffn_b1"].reshape(2, 2, HIDDEN).transpose(0, 2, 1)
    laid_out = {
        "X": padded, "W_Q": a["L0_attn_W_Q"], "W_K": a["L0_attn_W_K"], "W_V": a["L0_attn_W_V"],
        "WrT": a["L0_ffn_Wr"].T, "br": a["L0_ffn_br"],
        "W1T": a["L0_ffn_W1"].transpose(0, 2, 1), "W2T": a["L0_ffn_W2"].transpose(0, 2, 1),
        "b1T": a["L0_ffn_b1"].reshape(EXPERTS, FC, P).transpose(2, 0, 1), "b2d": a["L0_ffn_b2"],
        "Wqkv1T": a["L1_attn_Wqkv"].T, "Wo1T": a["L1_attn_Wo"].T,
        "wqkv": a["L1_ffn_wqkv"], "wo": a["L1_ffn_wo"], "w1d": a["L1_ffn_w1"], "w2d": a["L1_ffn_w2"],
        "b1l": b1.reshape(2, UC, P, 2).transpose(0, 2, 3, 1), "b2l": a["L1_ffn_b2"],
        "qs": a["L1_ffn_q_scale"], "ks": a["L1_ffn_k_scale"],
        "lng": a["L1_ffn_ln_g"].reshape(2, DC, P).transpose(0, 2, 1), "lnb": a["L1_ffn_ln_b"].reshape(2, DC, P).transpose(0, 2, 1),
        "xpos0": tables["xpos0"], "decay": tables["decay"], "ranks": tables["ranks"], "iota": tables["iota"],
        "rope1": tables["rope1"], "rope2": tables["rope2"],
        "ident_d": tables["ident"], "shift_d": tables["shift"], "mask_d": tables["mask"],
    }
    nc = bacc.Bacc("TRN2", target_bir_lowering=False, num_devices=1)
    g = Shared(nc, ExitStack())
    arrays = {}
    views = {}
    for name, value in laid_out.items():
        value = np.ascontiguousarray(value)
        arrays[f"in_{name}"] = value
        views[name] = nc.dram_tensor(f"in_{name}", value.shape, mybir.dt.from_np(value.dtype), kind="ExternalInput").ap()
    g.take(views)
    g.out = nc.dram_tensor("out", (B, L, D), F32, kind="ExternalOutput").ap()
    build(nc, g)
    result = run_bass_kernel_spmd(nc, [arrays], core_ids=[0])
    return result.results[0]["out"]
```
